# Optimizing a Trainium2 kernel written in Bass

```python
import numpy as np
import jax
import jax.numpy as jnp

def _softmax(x, axis=-1):
    return jax.nn.softmax(x, axis=axis)

def _gelu(x):
    return jax.nn.gelu(x, approximate=True)

def _silu(x):
    return jax.nn.silu(x)

def _sigmoid(x):
    return jax.nn.sigmoid(x)

def _layernorm(x, axis=-1, eps=1e-05):
    m = jnp.mean(x, axis=axis, keepdims=True)
    v = jnp.var(x, axis=axis, keepdims=True)
    return (x - m) / jnp.sqrt(v + eps)

def _scatter_add(tgt, idx, src, axis=0):
    return tgt.at[idx].add(src)

def _segment_sum(src, seg, n):
    return jax.ops.segment_sum(src, seg, n)
kernel_name = 'mk_decoder_preln_d4_seqx_r8_a053f0'

def setup_inputs(seed: int=0):
    np.random.seed(seed)
    _w = jnp.asarray

    def _rec_inputs():
        import jax
        import jax.numpy as jnp
        _rk = jax.random.key(seed)
        x = -0.000125 + 0.9999 * jax.random.normal(jax.random.fold_in(_rk, 1), (8, 256, 128), jnp.float32)
        _lenS = 256 - jax.random.randint(jax.random.fold_in(_rk, 7), (8,), 0, max(1, 256 // 4) + 1, jnp.int32)
        _lenS2 = 256 - jax.random.randint(jax.random.fold_in(_rk, 8), (8,), 0, max(1, 256 // 4) + 1, jnp.int32)
        _ctx_768P = jax.random.normal(jax.random.fold_in(_rk, 11), (8, 16, 96), jnp.float32)
        _ctx_768c = jax.random.dirichlet(jax.random.fold_in(_rk, 511), 0.3 * jnp.ones((16,), jnp.float32), (8, 256))
        _ctx_768t = jnp.einsum('bsk,bkd->bsd', _ctx_768c, _ctx_768P)
        _ctx_768t = _ctx_768t * jax.lax.rsqrt(jnp.mean(jnp.square(_ctx_768t)) + 1e-12) * 0.953939
        ctx_768 = 0.00272024 + 0.999456 * (_ctx_768t + 0.3 * jax.random.normal(jax.random.fold_in(_rk, 611), (8, 256, 96), jnp.float32))
        return (x, ctx_768)
    x, ctx_768 = _rec_inputs()

    def _L0_attn_setup():
        import jax, jax.numpy as jnp
        import numpy as np
        B, S, E, H = (8, 128, 128, 16)
        EPS = 0.001
        key = jax.random.key(seed)
        ks = jax.random.split(key, 5)
        x = jax.random.normal(ks[0], (B, S, E), dtype=jnp.float32)
        Wq = jax.random.normal(ks[1], (E, E), dtype=jnp.float32) * 0.02
        Wk = jax.random.normal(ks[2], (E, E), dtype=jnp.float32) * 0.02
        Wv = jax.random.normal(ks[3], (E, E), dtype=jnp.float32) * 0.02
        rel_table = jax.random.normal(ks[4], (2 * S - 1, H), dtype=jnp.float32) * 0.02
        gamma = jnp.ones((E,), dtype=jnp.float32)
        beta = jnp.zeros((E,), dtype=jnp.float32)
        return {'x': x, 'Wq': Wq, 'Wk': Wk, 'Wv': Wv, 'rel_table': rel_table, 'gamma': gamma, 'beta': beta}
    _L0_attn_all = _L0_attn_setup()
    _L0_attn_in = {k: v for k, v in _L0_attn_all.items() if k in ('Wq', 'Wk', 'Wv', 'rel_table', 'gamma', 'beta')}
    del _L0_attn_all

    def _L0_xattn_setup():
        import jax, jax.numpy as jnp
        import numpy as np
        HEADS = 16
        DIM_HEAD = 64
        SCALE = DIM_HEAD ** (-0.5)
        QUERY_DIM = 128
        CONTEXT_DIM = 96
        INNER_DIM = HEADS * DIM_HEAD
        key = jax.random.key(seed)
        ks = jax.random.split(key, 7)
        B, Nq, Nk = (8, 512, 77)
        x = jax.random.normal(ks[0], (B, Nq, QUERY_DIM), dtype=jnp.float32)
        context = jax.random.normal(ks[1], (B, Nk, CONTEXT_DIM), dtype=jnp.float32)
        Wq = jax.random.normal(ks[2], (QUERY_DIM, INNER_DIM), dtype=jnp.float32) * QUERY_DIM ** (-0.5)
        Wk = jax.random.normal(ks[3], (CONTEXT_DIM, INNER_DIM), dtype=jnp.float32) * CONTEXT_DIM ** (-0.5)
        Wv = jax.random.normal(ks[4], (CONTEXT_DIM, INNER_DIM), dtype=jnp.float32) * CONTEXT_DIM ** (-0.5)
        Wo = jax.random.normal(ks[5], (INNER_DIM, QUERY_DIM), dtype=jnp.float32) * INNER_DIM ** (-0.5)
        bo = jnp.zeros((QUERY_DIM,), dtype=jnp.float32)
        return {'x': x, 'context': context, 'Wq': Wq, 'Wk': Wk, 'Wv': Wv, 'Wo': Wo, 'bo': bo}
    _L0_xattn_all = _L0_xattn_setup()
    _L0_xattn_in = {k: v for k, v in _L0_xattn_all.items() if k in ('Wq', 'Wk', 'Wv', 'Wo', 'bo')}
    del _L0_xattn_all

    def _L0_ffn_setup():
        import jax, jax.numpy as jnp
        import numpy as np
        NUM_EXPERTS = 8
        TOP_K = 2
        D = 128
        H = 4 * D
        B, S = (4, 256)
        key = jax.random.key(seed)
        ks = jax.random.split(key, 8)
        s = 0.02
        return {'x': jax.random.normal(ks[0], (B, S, D), dtype=jnp.float32), 'gate_w': jax.random.normal(ks[1], (NUM_EXPERTS, D), dtype=jnp.float32) * s, 'gate_b': jnp.zeros((NUM_EXPERTS,), dtype=jnp.float32), 'w1': jax.random.normal(ks[2], (NUM_EXPERTS, D, H), dtype=jnp.float32) * s, 'b1': jnp.zeros((NUM_EXPERTS, H), dtype=jnp.float32), 'w2': jax.random.normal(ks[3], (NUM_EXPERTS, H, D), dtype=jnp.float32) * s, 'b2': jnp.zeros((NUM_EXPERTS, D), dtype=jnp.float32)}
    _L0_ffn_all = _L0_ffn_setup()
    _L0_ffn_in = {k: v for k, v in _L0_ffn_all.items() if k in ('gate_w', 'gate_b', 'w1', 'b1', 'w2', 'b2')}
    del _L0_ffn_all

    def _L1_attn_setup():
        import jax, jax.numpy as jnp
        import numpy as np
        import math
        INPUT_SIZE = 128
        HIDDEN = 128
        SEQ_LEN = 32
        BATCH = 128

        def _lstm(input_seq, w, u, bias):
            H = u.shape[0]
            B = input_seq.shape[1]
            x_proj = jnp.einsum('sbi,ih->sbh', input_seq, w) + bias

            def step(carry, xp_t):
                h_prev, c_prev = carry
                g = xp_t + h_prev @ u
                gates = jax.nn.sigmoid(g[:, :3 * H])
                c_cand = jnp.tanh(g[:, 3 * H:])
                ig, fg, og = (gates[:, :H], gates[:, H:2 * H], gates[:, 2 * H:])
                c = fg * c_prev + ig * c_cand
                h = og * jnp.tanh(c)
                return ((h, c), h)
            init = (jnp.zeros((B, H), dtype=input_seq.dtype), jnp.zeros((B, H), dtype=input_seq.dtype))
            _, hs = jax.lax.scan(step, init, x_proj)
            return hs
        key = jax.random.key(seed)
        k1, k2, k3, k4 = jax.random.split(key, 4)
        stddev = 1.0 / math.sqrt(HIDDEN)
        input_seq = jax.random.normal(k1, (SEQ_LEN, BATCH, INPUT_SIZE), dtype=jnp.float32)
        w = jax.random.uniform(k2, (INPUT_SIZE, 4 * HIDDEN), minval=-stddev, maxval=stddev, dtype=jnp.float32)
        u = jax.random.uniform(k3, (HIDDEN, 4 * HIDDEN), minval=-stddev, maxval=stddev, dtype=jnp.float32)
        bias = jax.random.uniform(k4, (4 * HIDDEN,), minval=-stddev, maxval=stddev, dtype=jnp.float32)
        return {'input_seq': input_seq, 'w': w, 'u': u, 'bias': bias}
    _L1_attn_all = _L1_attn_setup()
    _L1_attn_in = {k: v for k, v in _L1_attn_all.items() if k in ('w', 'u', 'bias')}
    del _L1_attn_all

    def _L1_xattn_setup():
        import jax, jax.numpy as jnp
        import numpy as np
        HEADS = 8
        DIM_HEAD = 64
        SCALE = DIM_HEAD ** (-0.5)
        key = jax.random.key(seed)
        ks = jax.random.split(key, 7)
        b, n, m = (4, 256, 128)
        qd, cd, inner = (128, 96, HEADS * DIM_HEAD)
        s = lambda fan_in: 1.0 / np.sqrt(fan_in)
        return {'x': jax.random.normal(ks[0], (b, n, qd), jnp.float32), 'context': jax.random.normal(ks[1], (b, m, cd), jnp.float32), 'Wq': jax.random.normal(ks[2], (qd, inner), jnp.float32) * s(qd), 'Wk': jax.random.normal(ks[3], (cd, inner), jnp.float32) * s(cd), 'Wv': jax.random.normal(ks[4], (cd, inner), jnp.float32) * s(cd), 'Wout': jax.random.normal(ks[5], (inner, qd), jnp.float32) * s(inner), 'bout': jax.random.normal(ks[6], (qd,), jnp.float32) * 0.01}
    _L1_xattn_all = _L1_xattn_setup()
    _L1_xattn_in = {k: v for k, v in _L1_xattn_all.items() if k in ('Wq', 'Wk', 'Wv', 'Wout', 'bout')}
    del _L1_xattn_all

    def _L1_ffn_setup():
        import jax, jax.numpy as jnp
        import numpy as np
        D = 128
        H = 128
        E = 8
        K = 2
        I = 2 * 128
        ROUTE_SCALE = 1.0
        key = jax.random.key(seed)
        ks = jax.random.split(key, 12)
        s = lambda *sh: 1.0 / np.sqrt(sh[-1])
        return {'x': jax.random.normal(ks[0], (1, 256, D), jnp.float32), 'gate_w': jax.random.normal(ks[1], (E, D), jnp.float32) * s(E, D), 'w1': jax.random.normal(ks[2], (E, H, D), jnp.float32) * s(H, D), 'b1': jax.random.normal(ks[3], (E, H), jnp.float32) * 0.01, 'w2': jax.random.normal(ks[4], (E, D, H), jnp.float32) * s(D, H), 'b2': jax.random.normal(ks[5], (E, D), jnp.float32) * 0.01, 'w3': jax.random.normal(ks[6], (E, H, D), jnp.float32) * s(H, D), 'b3': jax.random.normal(ks[7], (E, H), jnp.float32) * 0.01, 'sw1': jax.random.normal(ks[8], (I, D), jnp.float32) * s(I, D), 'sw2': jax.random.normal(ks[9], (I, D), jnp.float32) * s(I, D), 'sw3': jax.random.normal(ks[10], (D, I), jnp.float32) * s(D, I)}
    _L1_ffn_all = _L1_ffn_setup()
    _L1_ffn_in = {k: v for k, v in _L1_ffn_all.items() if k in ('gate_w', 'w1', 'b1', 'w2', 'b2', 'w3', 'b3', 'sw1', 'sw2', 'sw3')}
    del _L1_ffn_all

    def _L2_attn_setup():
        import jax, jax.numpy as jnp
        import numpy as np
        NUM_HEADS = 16
        WINDOW = 64
        key = jax.random.key(seed)
        ks = jax.random.split(key, 6)
        b, l, d = (2, 256, 128)
        s = 1.0 / np.sqrt(d)
        return {'x': jax.random.normal(ks[0], (b, l, d), dtype=jnp.float32), 'Wq': jax.random.normal(ks[1], (d, d), dtype=jnp.float32) * s, 'Wk': jax.random.normal(ks[2], (d, d), dtype=jnp.float32) * s, 'Wv': jax.random.normal(ks[3], (d, d), dtype=jnp.float32) * s, 'Wo': jax.random.normal(ks[4], (d, d), dtype=jnp.float32) * s, 'bo': jax.random.normal(ks[5], (d,), dtype=jnp.float32) * 0.01}
    _L2_attn_all = _L2_attn_setup()
    _L2_attn_in = {k: v for k, v in _L2_attn_all.items() if k in ('Wq', 'Wk', 'Wv', 'Wo', 'bo')}
    del _L2_attn_all

    def _L2_xattn_setup():
        import jax, jax.numpy as jnp
        import numpy as np
        NUM_HEADS = 16
        CLAMP = 10000.0
        key = jax.random.key(seed)
        ks = jax.random.split(key, 8)
        B, Nq, Nkv, Cq, Ckv = (4, 256, 256, 128, 96)
        s_q = 1.0 / np.sqrt(Cq)
        s_kv = 1.0 / np.sqrt(Ckv)
        return {'query': jax.random.normal(ks[0], (B, Nq, Cq), jnp.float32), 'key_value': jax.random.normal(ks[1], (B, Nkv, Ckv), jnp.float32), 'Wq': jax.random.normal(ks[2], (Cq, Cq), jnp.float32) * s_q, 'bq': jnp.zeros((Cq,), jnp.float32), 'Wk': jax.random.normal(ks[3], (Ckv, Cq), jnp.float32) * s_kv, 'bk': jnp.zeros((Cq,), jnp.float32), 'Wv': jax.random.normal(ks[4], (Ckv, Cq), jnp.float32) * s_kv, 'bv': jnp.zeros((Cq,), jnp.float32), 'Wo': jax.random.normal(ks[5], (Cq, Cq), jnp.float32) * s_q, 'bo': jnp.zeros((Cq,), jnp.float32)}
    _L2_xattn_all = _L2_xattn_setup()
    _L2_xattn_in = {k: v for k, v in _L2_xattn_all.items() if k in ('Wq', 'bq', 'Wk', 'bk', 'Wv', 'bv', 'Wo', 'bo')}
    del _L2_xattn_all

    def _L2_ffn_setup():
        import jax, jax.numpy as jnp
        import numpy as np
        B, S, D = (1, 256, 128)
        E, F = (16, 128)
        NG, TKG, K = (4, 2, 4)
        NSH = 2
        SCALE = 2.5
        STD = 0.02
        EPG = E // NG

        def _route(x_flat, router_w, bias):
            logits = x_flat.astype(jnp.float32) @ router_w.T
            scores = jax.nn.sigmoid(logits)
            s = scores + bias[None, :]
            sg = s.reshape(-1, NG, EPG)
            group_score = jax.lax.top_k(sg, 2)[0].sum(-1)
            gidx = jax.lax.top_k(group_score, TKG)[1]
            gmask = jnp.sum(jax.nn.one_hot(gidx, NG, dtype=jnp.float32), axis=1) > 0
            emask = jnp.repeat(gmask, EPG, axis=1)
            masked = jnp.where(emask, s, -1.0)
            topk_idx = jax.lax.top_k(masked, K)[1]
            tw = jnp.take_along_axis(scores, topk_idx, axis=1)
            tw = tw / (tw.sum(-1, keepdims=True) + 1e-20)
            tw = tw * SCALE
            return (topk_idx, tw)
        key = jax.random.key(seed)
        ks = jax.random.split(key, 8)
        return {'hidden_states': jax.random.normal(ks[0], (B, S, D), jnp.float32), 'router_w': jax.random.normal(ks[1], (E, D), jnp.float32) * STD, 'bias': jnp.zeros((E,), jnp.float32), 'gate_w': jax.random.normal(ks[2], (E, D, F), jnp.float32) * STD, 'up_w': jax.random.normal(ks[3], (E, D, F), jnp.float32) * STD, 'down_w': jax.random.normal(ks[4], (E, F, D), jnp.float32) * STD, 'sh_gate_w': jax.random.normal(ks[5], (D, NSH * F), jnp.float32) * STD, 'sh_up_w': jax.random.normal(ks[6], (D, NSH * F), jnp.float32) * STD, 'sh_down_w': jax.random.normal(ks[7], (NSH * F, D), jnp.float32) * STD}
    _L2_ffn_all = _L2_ffn_setup()
    _L2_ffn_in = {k: v for k, v in _L2_ffn_all.items() if k in ('router_w', 'bias', 'gate_w', 'up_w', 'down_w', 'sh_gate_w', 'sh_up_w', 'sh_down_w')}
    del _L2_ffn_all

    def _L3_attn_setup():
        import jax, jax.numpy as jnp
        import numpy as np
        N_HEAD = 16
        key = jax.random.key(seed)
        ks = jax.random.split(key, 10)
        C = 128
        B, T = (4, 1024)
        s = 1.0 / np.sqrt(C)
        return {'x': jax.random.normal(ks[0], (B, T, C), dtype=jnp.float32), 'Wq': jax.random.normal(ks[1], (C, C), dtype=jnp.float32) * s, 'bq': jax.random.normal(ks[2], (C,), dtype=jnp.float32) * s, 'Wk': jax.random.normal(ks[3], (C, C), dtype=jnp.float32) * s, 'bk': jax.random.normal(ks[4], (C,), dtype=jnp.float32) * s, 'Wv': jax.random.normal(ks[5], (C, C), dtype=jnp.float32) * s, 'bv': jax.random.normal(ks[6], (C,), dtype=jnp.float32) * s, 'Wp': jax.random.normal(ks[7], (C, C), dtype=jnp.float32) * s, 'bp': jax.random.normal(ks[8], (C,), dtype=jnp.float32) * s}
    _L3_attn_all = _L3_attn_setup()
    _L3_attn_in = {k: v for k, v in _L3_attn_all.items() if k in ('Wq', 'bq', 'Wk', 'bk', 'Wv', 'bv', 'Wp', 'bp')}
    del _L3_attn_all

    def _L3_xattn_setup():
        import jax, jax.numpy as jnp
        import numpy as np
        HEADS = 16
        DIM_HEAD = 64
        QUERY_DIM = 128
        CONTEXT_DIM = 96
        INNER = HEADS * DIM_HEAD
        SCALE = DIM_HEAD ** (-0.5)
        key = jax.random.key(seed)
        ks = jax.random.split(key, 7)
        B, Sq, Skv = (4, 256, 256)
        x = jax.random.normal(ks[0], (B, Sq, QUERY_DIM), dtype=jnp.float32)
        context = jax.random.normal(ks[1], (B, Skv, CONTEXT_DIM), dtype=jnp.float32)
        w_q = jax.random.normal(ks[2], (QUERY_DIM, INNER), dtype=jnp.float32) / np.sqrt(QUERY_DIM)
        w_k = jax.random.normal(ks[3], (CONTEXT_DIM, INNER), dtype=jnp.float32) / np.sqrt(CONTEXT_DIM)
        w_v = jax.random.normal(ks[4], (CONTEXT_DIM, INNER), dtype=jnp.float32) / np.sqrt(CONTEXT_DIM)
        w_o = jax.random.normal(ks[5], (INNER, QUERY_DIM), dtype=jnp.float32) / np.sqrt(INNER)
        b_o = jax.random.normal(ks[6], (QUERY_DIM,), dtype=jnp.float32) * 0.02
        return {'x': x, 'context': context, 'w_q': w_q, 'w_k': w_k, 'w_v': w_v, 'w_o': w_o, 'b_o': b_o}
    _L3_xattn_all = _L3_xattn_setup()
    _L3_xattn_in = {k: v for k, v in _L3_xattn_all.items() if k in ('w_q', 'w_k', 'w_v', 'w_o', 'b_o')}
    del _L3_xattn_all

    def _L3_ffn_setup():
        import jax, jax.numpy as jnp
        import numpy as np
        EPS = 0.05
        N_ITERS = 20
        TOP_K = 2

        def _sinkhorn(cost, n_iters=N_ITERS, epsilon=EPS):
            la = cost / epsilon
            for _ in range(n_iters):
                la = la - jax.scipy.special.logsumexp(la, axis=-1, keepdims=True)
                la = la - jax.scipy.special.logsumexp(la, axis=-2, keepdims=True)
            return jnp.exp(la)
        key = jax.random.key(seed)
        k0, k1, k2, k3, k4 = jax.random.split(key, 5)
        B, T, D, F, E = (2, 256, 128, 512, 8)
        x = jax.random.normal(k0, (B, T, D), dtype=jnp.float32)
        gate_W = jax.random.normal(k1, (E, D), dtype=jnp.float32) * 0.02
        W_gate = jax.random.normal(k2, (E, F, D), dtype=jnp.float32) * 0.02
        W_up = jax.random.normal(k3, (E, F, D), dtype=jnp.float32) * 0.02
        W_down = jax.random.normal(k4, (E, D, F), dtype=jnp.float32) * 0.02
        return {'x': x, 'gate_W': gate_W, 'W_gate': W_gate, 'W_up': W_up, 'W_down': W_down}
    _L3_ffn_all = _L3_ffn_setup()
    _L3_ffn_in = {k: v for k, v in _L3_ffn_all.items() if k in ('gate_W', 'W_gate', 'W_up', 'W_down')}
    del _L3_ffn_all
    return {'x': x, 'ctx_768': ctx_768, 'L0_attn_Wq': _L0_attn_in['Wq'], 'L0_attn_Wk': _L0_attn_in['Wk'], 'L0_attn_Wv': _L0_attn_in['Wv'], 'L0_attn_rel_table': _L0_attn_in['rel_table'], 'L0_attn_gamma': _L0_attn_in['gamma'], 'L0_attn_beta': _L0_attn_in['beta'], 'L0_xattn_Wq': _L0_xattn_in['Wq'], 'L0_xattn_Wk': _L0_xattn_in['Wk'], 'L0_xattn_Wv': _L0_xattn_in['Wv'], 'L0_xattn_Wo': _L0_xattn_in['Wo'], 'L0_xattn_bo': _L0_xattn_in['bo'], 'L0_ffn_gate_w': _L0_ffn_in['gate_w'], 'L0_ffn_gate_b': _L0_ffn_in['gate_b'], 'L0_ffn_w1': _L0_ffn_in['w1'], 'L0_ffn_b1': _L0_ffn_in['b1'], 'L0_ffn_w2': _L0_ffn_in['w2'], 'L0_ffn_b2': _L0_ffn_in['b2'], 'L1_attn_w': _L1_attn_in['w'], 'L1_attn_u': _L1_attn_in['u'], 'L1_attn_bias': _L1_attn_in['bias'], 'L1_xattn_Wq': _L1_xattn_in['Wq'], 'L1_xattn_Wk': _L1_xattn_in['Wk'], 'L1_xattn_Wv': _L1_xattn_in['Wv'], 'L1_xattn_Wout': _L1_xattn_in['Wout'], 'L1_xattn_bout': _L1_xattn_in['bout'], 'L1_ffn_gate_w': _L1_ffn_in['gate_w'], 'L1_ffn_w1': _L1_ffn_in['w1'], 'L1_ffn_b1': _L1_ffn_in['b1'], 'L1_ffn_w2': _L1_ffn_in['w2'], 'L1_ffn_b2': _L1_ffn_in['b2'], 'L1_ffn_w3': _L1_ffn_in['w3'], 'L1_ffn_b3': _L1_ffn_in['b3'], 'L1_ffn_sw1': _L1_ffn_in['sw1'], 'L1_ffn_sw2': _L1_ffn_in['sw2'], 'L1_ffn_sw3': _L1_ffn_in['sw3'], 'L2_attn_Wq': _L2_attn_in['Wq'], 'L2_attn_Wk': _L2_attn_in['Wk'], 'L2_attn_Wv': _L2_attn_in['Wv'], 'L2_attn_Wo': _L2_attn_in['Wo'], 'L2_attn_bo': _L2_attn_in['bo'], 'L2_xattn_Wq': _L2_xattn_in['Wq'], 'L2_xattn_bq': _L2_xattn_in['bq'], 'L2_xattn_Wk': _L2_xattn_in['Wk'], 'L2_xattn_bk': _L2_xattn_in['bk'], 'L2_xattn_Wv': _L2_xattn_in['Wv'], 'L2_xattn_bv': _L2_xattn_in['bv'], 'L2_xattn_Wo': _L2_xattn_in['Wo'], 'L2_xattn_bo': _L2_xattn_in['bo'], 'L2_ffn_router_w': _L2_ffn_in['router_w'], 'L2_ffn_bias': _L2_ffn_in['bias'], 'L2_ffn_gate_w': _L2_ffn_in['gate_w'], 'L2_ffn_up_w': _L2_ffn_in['up_w'], 'L2_ffn_down_w': _L2_ffn_in['down_w'], 'L2_ffn_sh_gate_w': _L2_ffn_in['sh_gate_w'], 'L2_ffn_sh_up_w': _L2_ffn_in['sh_up_w'], 'L2_ffn_sh_down_w': _L2_ffn_in['sh_down_w'], 'L3_attn_Wq': _L3_attn_in['Wq'], 'L3_attn_bq': _L3_attn_in['bq'], 'L3_attn_Wk': _L3_attn_in['Wk'], 'L3_attn_bk': _L3_attn_in['bk'], 'L3_attn_Wv': _L3_attn_in['Wv'], 'L3_attn_bv': _L3_attn_in['bv'], 'L3_attn_Wp': _L3_attn_in['Wp'], 'L3_attn_bp': _L3_attn_in['bp'], 'L3_xattn_w_q': _L3_xattn_in['w_q'], 'L3_xattn_w_k': _L3_xattn_in['w_k'], 'L3_xattn_w_v': _L3_xattn_in['w_v'], 'L3_xattn_w_o': _L3_xattn_in['w_o'], 'L3_xattn_b_o': _L3_xattn_in['b_o'], 'L3_ffn_gate_W': _L3_ffn_in['gate_W'], 'L3_ffn_W_gate': _L3_ffn_in['W_gate'], 'L3_ffn_W_up': _L3_ffn_in['W_up'], 'L3_ffn_W_down': _L3_ffn_in['W_down']}

def reference(x, ctx_768, L0_attn_Wq, L0_attn_Wk, L0_attn_Wv, L0_attn_rel_table, L0_attn_gamma, L0_attn_beta, L0_xattn_Wq, L0_xattn_Wk, L0_xattn_Wv, L0_xattn_Wo, L0_xattn_bo, L0_ffn_gate_w, L0_ffn_gate_b, L0_ffn_w1, L0_ffn_b1, L0_ffn_w2, L0_ffn_b2, L1_attn_w, L1_attn_u, L1_attn_bias, L1_xattn_Wq, L1_xattn_Wk, L1_xattn_Wv, L1_xattn_Wout, L1_xattn_bout, L1_ffn_gate_w, L1_ffn_w1, L1_ffn_b1, L1_ffn_w2, L1_ffn_b2, L1_ffn_w3, L1_ffn_b3, L1_ffn_sw1, L1_ffn_sw2, L1_ffn_sw3, L2_attn_Wq, L2_attn_Wk, L2_attn_Wv, L2_attn_Wo, L2_attn_bo, L2_xattn_Wq, L2_xattn_bq, L2_xattn_Wk, L2_xattn_bk, L2_xattn_Wv, L2_xattn_bv, L2_xattn_Wo, L2_xattn_bo, L2_ffn_router_w, L2_ffn_bias, L2_ffn_gate_w, L2_ffn_up_w, L2_ffn_down_w, L2_ffn_sh_gate_w, L2_ffn_sh_up_w, L2_ffn_sh_down_w, L3_attn_Wq, L3_attn_bq, L3_attn_Wk, L3_attn_bk, L3_attn_Wv, L3_attn_bv, L3_attn_Wp, L3_attn_bp, L3_xattn_w_q, L3_xattn_w_k, L3_xattn_w_v, L3_xattn_w_o, L3_xattn_b_o, L3_ffn_gate_W, L3_ffn_W_gate, L3_ffn_W_up, L3_ffn_W_down):
    import jax
    import jax.numpy as jnp

    def _L0_attn_ref(x, Wq, Wk, Wv, rel_table, gamma, beta):
        import jax, jax.numpy as jnp
        import numpy as np
        B, S, E, H = (8, 128, 128, 16)
        EPS = 0.001
        b, s, e = x.shape
        h = rel_table.shape[1]
        scale = e ** (-0.5)

        def split_heads(t):
            return t.reshape(b, s, h, -1).transpose(0, 2, 1, 3)
        q = split_heads(x @ Wq)
        k = split_heads(x @ Wk)
        v = split_heads(x @ Wv)
        attn = jnp.einsum('bhqd,bhkd->bhqk', q, k) * scale
        attn = jax.nn.softmax(attn, axis=-1)
        r = jnp.arange(s)
        rel_index = jnp.clip(r[None, :] - r[:, None] + (s - 1), 0, 2 * s - 2)
        bias = rel_table[rel_index]
        bias = bias.reshape(-1).reshape(h, s, s)
        attn = attn + bias[None]
        out = jnp.einsum('bhqk,bhkd->bhqd', attn, v)
        out = out.transpose(0, 2, 1, 3).reshape(b, s, e)
        mu = jnp.mean(out, axis=-1, keepdims=True)
        var = jnp.var(out, axis=-1, keepdims=True)
        out = (out - mu) / jnp.sqrt(var + EPS) * gamma + beta
        return out

    def _L0_xattn_ref(x, context, Wq, Wk, Wv, Wo, bo):
        import jax, jax.numpy as jnp
        import numpy as np
        HEADS = 16
        DIM_HEAD = 64
        SCALE = DIM_HEAD ** (-0.5)
        QUERY_DIM = 128
        CONTEXT_DIM = 96
        INNER_DIM = HEADS * DIM_HEAD
        B, Nq, _ = x.shape
        Nk = context.shape[1]
        q = x @ Wq
        k = context @ Wk
        v = context @ Wv
        q = q.reshape(B, Nq, HEADS, DIM_HEAD).transpose(0, 2, 1, 3)
        k = k.reshape(B, Nk, HEADS, DIM_HEAD).transpose(0, 2, 1, 3)
        v = v.reshape(B, Nk, HEADS, DIM_HEAD).transpose(0, 2, 1, 3)
        sim = jnp.einsum('bhid,bhjd->bhij', q, k) * SCALE
        attn = jax.nn.softmax(sim, axis=-1)
        out = jnp.einsum('bhij,bhjd->bhid', attn, v)
        out = out.transpose(0, 2, 1, 3).reshape(B, Nq, INNER_DIM)
        return out @ Wo + bo

    def _L0_ffn_ref(x, gate_w, gate_b, w1, b1, w2, b2):
        import jax, jax.numpy as jnp
        import numpy as np
        NUM_EXPERTS = 8
        TOP_K = 2
        D = 128
        H = 4 * D
        B, S = (4, 256)
        orig_shape = x.shape
        xf = x.reshape(-1, orig_shape[-1])
        gates = xf @ gate_w.T + gate_b
        weights, indices = jax.lax.top_k(gates, TOP_K)
        weights = jax.nn.softmax(weights, axis=-1)
        out = jnp.zeros_like(xf)
        for e in range(NUM_EXPERTS):
            w_e = jnp.sum(weights * (indices == e), axis=-1, keepdims=True)
            h = jax.nn.gelu(xf @ w1[e] + b1[e], approximate=False)
            out = out + w_e * (h @ w2[e] + b2[e])
        return out.reshape(orig_shape)

    def _L1_attn_ref(input_seq, w, u, bias):
        import jax, jax.numpy as jnp
        import numpy as np
        import math
        INPUT_SIZE = 128
        HIDDEN = 128
        SEQ_LEN = 32
        BATCH = 128

        def _lstm(input_seq, w, u, bias):
            H = u.shape[0]
            B = input_seq.shape[1]
            x_proj = jnp.einsum('sbi,ih->sbh', input_seq, w) + bias

            def step(carry, xp_t):
                h_prev, c_prev = carry
                g = xp_t + h_prev @ u
                gates = jax.nn.sigmoid(g[:, :3 * H])
                c_cand = jnp.tanh(g[:, 3 * H:])
                ig, fg, og = (gates[:, :H], gates[:, H:2 * H], gates[:, 2 * H:])
                c = fg * c_prev + ig * c_cand
                h = og * jnp.tanh(c)
                return ((h, c), h)
            init = (jnp.zeros((B, H), dtype=input_seq.dtype), jnp.zeros((B, H), dtype=input_seq.dtype))
            _, hs = jax.lax.scan(step, init, x_proj)
            return hs
        return _lstm(input_seq, w, u, bias)

    def _L1_xattn_ref(x, context, Wq, Wk, Wv, Wout, bout):
        import jax, jax.numpy as jnp
        import numpy as np
        HEADS = 8
        DIM_HEAD = 64
        SCALE = DIM_HEAD ** (-0.5)
        b, n, _ = x.shape
        m = context.shape[1]
        q = (x @ Wq).reshape(b, n, HEADS, DIM_HEAD)
        k = (context @ Wk).reshape(b, m, HEADS, DIM_HEAD)
        v = (context @ Wv).reshape(b, m, HEADS, DIM_HEAD)
        sim = jnp.einsum('bihd,bjhd->bhij', q, k) * SCALE
        attn = jax.nn.softmax(sim, axis=-1)
        out = jnp.einsum('bhij,bjhd->bihd', attn, v).reshape(b, n, HEADS * DIM_HEAD)
        return out @ Wout + bout

    def _L1_ffn_ref(x, gate_w, w1, b1, w2, b2, w3, b3, sw1, sw2, sw3):
        import jax, jax.numpy as jnp
        import numpy as np
        D = 128
        H = 128
        E = 8
        K = 2
        I = 2 * 128
        ROUTE_SCALE = 1.0
        B, S, _ = x.shape
        xt = x.reshape(-1, D)
        logits = xt @ gate_w.T
        scores = jax.nn.softmax(logits.astype(jnp.float32), axis=-1)
        top_vals, idx = jax.lax.top_k(scores, K)
        weights = jnp.take_along_axis(scores, idx, axis=1).astype(x.dtype) * ROUTE_SCALE
        xs = xt[:, None, :] * weights[:, :, None]
        y = jnp.zeros_like(xt)
        for e in range(E):
            mask = (idx == e).astype(x.dtype)
            h = jax.nn.silu(jnp.einsum('tkd,hd->tkh', xs, w1[e]) + b1[e])
            x2 = jnp.einsum('tkh,dh->tkd', h, w2[e]) + b2[e]
            x3 = jnp.einsum('tkd,hd->tkh', xs, w3[e]) + b3[e]
            y = y + jnp.sum(x2 * x3 * mask[:, :, None], axis=1)
        z = jax.nn.silu(xt @ sw1.T) * (xt @ sw2.T) @ sw3.T
        return (y + z).reshape(B, S, D)

    def _L2_attn_ref(x, Wq, Wk, Wv, Wo, bo):
        import jax, jax.numpy as jnp
        import numpy as np
        NUM_HEADS = 16
        WINDOW = 64
        b, l, d = x.shape
        h, w = (NUM_HEADS, WINDOW)
        dh = d // h
        p = w // 2
        q = (x @ Wq.T).reshape(b, l, h, dh)
        xp = jnp.pad(x, ((0, 0), (p, p), (0, 0)))
        k = (xp @ Wk.T).reshape(b, l + 2 * p, h, dh)
        v = (xp @ Wv.T).reshape(b, l + 2 * p, h, dh)
        win_idx = jnp.arange(l)[:, None] + jnp.arange(w)[None, :]
        kw = k[:, win_idx]
        vw = v[:, win_idx]
        scale = 1.0 / np.float32(np.sqrt(dh))
        scores = jnp.einsum('blhd,blwhd->blhw', q, kw) * scale
        attn = jax.nn.softmax(scores, axis=-1)
        out = jnp.einsum('blhw,blwhd->blhd', attn, vw).reshape(b, l, d)
        return out @ Wo.T + bo

    def _L2_xattn_ref(query, key_value, Wq, bq, Wk, bk, Wv, bv, Wo, bo):
        import jax, jax.numpy as jnp
        import numpy as np
        NUM_HEADS = 16
        CLAMP = 10000.0
        B, Nq, Cq = query.shape
        Nkv = key_value.shape[1]
        H = NUM_HEADS
        D = Cq // H
        scale = D ** (-0.5)
        q = (query @ Wq + bq).reshape(B, Nq, H, D).transpose(0, 2, 1, 3)
        k = (key_value @ Wk + bk).reshape(B, Nkv, H, D).transpose(0, 2, 1, 3)
        v = (key_value @ Wv + bv).reshape(B, Nkv, H, D).transpose(0, 2, 1, 3)
        attn = jnp.einsum('bhqd,bhkd->bhqk', q, k) * scale
        attn = jnp.clip(attn, -CLAMP, CLAMP)
        attn = jax.nn.softmax(attn, axis=-1)
        attn = jnp.where(jnp.any(jnp.isnan(attn)), jnp.asarray(1.0 / Nkv, attn.dtype), attn)
        x = jnp.einsum('bhqk,bhkd->bqhd', attn, v).reshape(B, Nq, Cq)
        return x @ Wo + bo

    def _L2_ffn_ref(hidden_states, router_w, bias, gate_w, up_w, down_w, sh_gate_w, sh_up_w, sh_down_w):
        import jax, jax.numpy as jnp
        import numpy as np
        B, S, D = (1, 256, 128)
        E, F = (16, 128)
        NG, TKG, K = (4, 2, 4)
        NSH = 2
        SCALE = 2.5
        STD = 0.02
        EPG = E // NG

        def _route(x_flat, router_w, bias):
            logits = x_flat.astype(jnp.float32) @ router_w.T
            scores = jax.nn.sigmoid(logits)
            s = scores + bias[None, :]
            sg = s.reshape(-1, NG, EPG)
            group_score = jax.lax.top_k(sg, 2)[0].sum(-1)
            gidx = jax.lax.top_k(group_score, TKG)[1]
            gmask = jnp.sum(jax.nn.one_hot(gidx, NG, dtype=jnp.float32), axis=1) > 0
            emask = jnp.repeat(gmask, EPG, axis=1)
            masked = jnp.where(emask, s, -1.0)
            topk_idx = jax.lax.top_k(masked, K)[1]
            tw = jnp.take_along_axis(scores, topk_idx, axis=1)
            tw = tw / (tw.sum(-1, keepdims=True) + 1e-20)
            tw = tw * SCALE
            return (topk_idx, tw)
        x = hidden_states.reshape(-1, D)
        topk_idx, tw = _route(x, router_w, bias)
        combine = (jax.nn.one_hot(topk_idx, E, dtype=tw.dtype) * tw[..., None]).sum(1)
        h = jnp.einsum('td,edf->etf', x, gate_w)
        u = jnp.einsum('td,edf->etf', x, up_w)
        y = jnp.einsum('etf,efd->etd', jax.nn.silu(h) * u, down_w)
        routed = jnp.einsum('etd,te->td', y, combine)
        sh = jax.nn.silu(x @ sh_gate_w) * (x @ sh_up_w) @ sh_down_w
        return (routed + sh).reshape(hidden_states.shape)

    def _L3_attn_ref(x, Wq, bq, Wk, bk, Wv, bv, Wp, bp):
        import jax, jax.numpy as jnp
        import numpy as np
        N_HEAD = 16
        B, T, C = x.shape
        H = N_HEAD
        d = C // H

        def proj_heads(W, b):
            h = x @ W.T + b
            return h.reshape(B, T, H, d).transpose(0, 2, 1, 3)
        q = proj_heads(Wq, bq)
        k = proj_heads(Wk, bk)
        v = proj_heads(Wv, bv)
        q = jax.nn.softmax(q, axis=-1)
        k = jax.nn.softmax(k, axis=-1)
        k_sum = k.sum(axis=-2, keepdims=True)
        D_inv = 1.0 / (q * k_sum).sum(axis=-1, keepdims=True)
        context = jnp.einsum('bhnd,bhnv->bhdv', k, v)
        out = jnp.einsum('bhqd,bhdv->bhqv', q, context)
        out = out * D_inv + q
        out = out.transpose(0, 2, 1, 3).reshape(B, T, C)
        return out @ Wp.T + bp

    def _L3_xattn_ref(x, context, w_q, w_k, w_v, w_o, b_o):
        import jax, jax.numpy as jnp
        import numpy as np
        HEADS = 16
        DIM_HEAD = 64
        QUERY_DIM = 128
        CONTEXT_DIM = 96
        INNER = HEADS * DIM_HEAD
        SCALE = DIM_HEAD ** (-0.5)
        B, Sq, _ = x.shape
        Skv = context.shape[1]
        q = (x @ w_q).reshape(B, Sq, HEADS, DIM_HEAD).transpose(0, 2, 1, 3)
        k = (context @ w_k).reshape(B, Skv, HEADS, DIM_HEAD).transpose(0, 2, 1, 3)
        v = (context @ w_v).reshape(B, Skv, HEADS, DIM_HEAD).transpose(0, 2, 1, 3)
        sim = jnp.einsum('bhid,bhjd->bhij', q, k) * SCALE
        attn = jax.nn.softmax(sim, axis=-1)
        out = jnp.einsum('bhij,bhjd->bhid', attn, v)
        out = out.transpose(0, 2, 1, 3).reshape(B, Sq, INNER)
        return out @ w_o + b_o

    def _L3_ffn_ref(x, gate_W, W_gate, W_up, W_down):
        import jax, jax.numpy as jnp
        import numpy as np
        EPS = 0.05
        N_ITERS = 20
        TOP_K = 2

        def _sinkhorn(cost, n_iters=N_ITERS, epsilon=EPS):
            la = cost / epsilon
            for _ in range(n_iters):
                la = la - jax.scipy.special.logsumexp(la, axis=-1, keepdims=True)
                la = la - jax.scipy.special.logsumexp(la, axis=-2, keepdims=True)
            return jnp.exp(la)
        B, T, D = x.shape
        xf = x.reshape(B * T, D)
        logits = xf @ gate_W.T
        pi = _sinkhorn(-logits)
        _, top_idx = jax.lax.top_k(pi, TOP_K)
        g = jnp.einsum('nd,efd->enf', xf, W_gate)
        u = jnp.einsum('nd,efd->enf', xf, W_up)
        y = jnp.einsum('enf,edf->end', jax.nn.silu(g) * u, W_down)
        n_ar = jnp.arange(xf.shape[0])
        out = jnp.zeros_like(xf)
        for k in range(TOP_K):
            out = out + y[top_idx[:, k], n_ar] * pi[:, k:k + 1]
        return out.reshape(B, T, D)
    x = x + _L0_attn_ref(_layernorm(x, axis=-1), L0_attn_Wq, L0_attn_Wk, L0_attn_Wv, L0_attn_rel_table, L0_attn_gamma, L0_attn_beta)
    x = x + _L0_xattn_ref(_layernorm(x, axis=-1), ctx_768, L0_xattn_Wq, L0_xattn_Wk, L0_xattn_Wv, L0_xattn_Wo, L0_xattn_bo)
    x = x + _L0_ffn_ref(_layernorm(x, axis=-1), L0_ffn_gate_w, L0_ffn_gate_b, L0_ffn_w1, L0_ffn_b1, L0_ffn_w2, L0_ffn_b2)
    x = x + _L1_attn_ref(_layernorm(x, axis=-1), L1_attn_w, L1_attn_u, L1_attn_bias)
    x = x + _L1_xattn_ref(_layernorm(x, axis=-1), ctx_768, L1_xattn_Wq, L1_xattn_Wk, L1_xattn_Wv, L1_xattn_Wout, L1_xattn_bout)
    x = x + _L1_ffn_ref(_layernorm(x, axis=-1), L1_ffn_gate_w, L1_ffn_w1, L1_ffn_b1, L1_ffn_w2, L1_ffn_b2, L1_ffn_w3, L1_ffn_b3, L1_ffn_sw1, L1_ffn_sw2, L1_ffn_sw3)
    x = x + _L2_attn_ref(_layernorm(x, axis=-1), L2_attn_Wq, L2_attn_Wk, L2_attn_Wv, L2_attn_Wo, L2_attn_bo)
    x = x + _L2_xattn_ref(_layernorm(x, axis=-1), ctx_768, L2_xattn_Wq, L2_xattn_bq, L2_xattn_Wk, L2_xattn_bk, L2_xattn_Wv, L2_xattn_bv, L2_xattn_Wo, L2_xattn_bo)
    x = x + _L2_ffn_ref(_layernorm(x, axis=-1), L2_ffn_router_w, L2_ffn_bias, L2_ffn_gate_w, L2_ffn_up_w, L2_ffn_down_w, L2_ffn_sh_gate_w, L2_ffn_sh_up_w, L2_ffn_sh_down_w)
    x = x + _L3_attn_ref(_layernorm(x, axis=-1), L3_attn_Wq, L3_attn_bq, L3_attn_Wk, L3_attn_bk, L3_attn_Wv, L3_attn_bv, L3_attn_Wp, L3_attn_bp)
    x = x + _L3_xattn_ref(_layernorm(x, axis=-1), ctx_768, L3_xattn_w_q, L3_xattn_w_k, L3_xattn_w_v, L3_xattn_w_o, L3_xattn_b_o)
    x = x + _L3_ffn_ref(_layernorm(x, axis=-1), L3_ffn_gate_W, L3_ffn_W_gate, L3_ffn_W_up, L3_ffn_W_down)
    return x

_drawn_inputs = setup_inputs


def setup_inputs(seed=0):
    import zlib

    import numpy as np

    out = dict(_drawn_inputs(seed))
    spreads = {'L0_attn_gamma': (1.0, 0.2),
     'L0_attn_beta': (0.0, 0.1),
     'L0_xattn_bo': (0.0, 0.1),
     'L0_ffn_gate_b': (0.0, 0.1),
     'L0_ffn_b1': (0.0, 0.8),
     'L0_ffn_b2': (0.0, 0.1),
     'L2_xattn_bq': (0.0, 0.729),
     'L2_xattn_bk': (0.0, 2.0),
     'L2_xattn_bv': (0.0, 0.1),
     'L2_xattn_bo': (0.0, 0.1),
     'L2_ffn_bias': (0.0, 0.8)}
    factors = {'L0_attn_Wq': 8.0,
     'L0_attn_Wk': 8.0,
     'L0_ffn_w1': 2.703,
     'L1_attn_u': 4.727,
     'L1_attn_bias': 4.534,
     'L1_xattn_bout': 8.0,
     'L1_ffn_b1': 8.0,
     'L1_ffn_b2': 8.0,
     'L1_ffn_b3': 8.0,
     'L2_attn_bo': 8.0,
     'L2_ffn_router_w': 8.0,
     'L2_ffn_gate_w': 8.0,
     'L2_ffn_up_w': 8.0,
     'L2_ffn_down_w': 8.0,
     'L2_ffn_sh_gate_w': 8.0,
     'L2_ffn_sh_up_w': 8.0,
     'L2_ffn_sh_down_w': 8.0,
     'L3_attn_bq': 34.655,
     'L3_attn_Wk': 26.651,
     'L3_attn_bk': 64.0,
     'L3_xattn_b_o': 20.808,
     'L3_ffn_gate_W': 64.0,
     'L3_ffn_W_gate': 64.0,
     'L3_ffn_W_up': 64.0,
     'L3_ffn_W_down': 64.0,
     'L3_attn_Wq': 3.328,
     'L3_attn_bv': 4.621,
     'L3_attn_bp': 4.783}
    for name, (base, spread) in spreads.items():
        noise = np.random.default_rng([zlib.crc32(name.encode()), seed]).standard_normal(out[name].shape)
        drawn = base * np.exp(spread * noise) if base else spread * noise
        out[name] = jnp.asarray(drawn.astype(out[name].dtype))
    for name, factor in factors.items():
        out[name] = (out[name] * factor).astype(out[name].dtype)
    return out
```

```python
from contextlib import ExitStack

import numpy as np
import concourse.bass as bass
from concourse import mybir

F32 = mybir.dt.float32
BF16 = mybir.dt.bfloat16
ALU = mybir.AluOpType
ACT = mybir.ActivationFunctionType
AX = mybir.AxisListType

P = 128
B, S, D, CD = 8, 256, 128, 96
T = S // P
NT = B * T
TOK = B * S
LN_EPS = 1e-5
REL_ROWS = 255
MASKED = -1e30
SINK_ITERS, SINK_EPS = 20, 0.05
CLAMP = 10000.0
FLT_MIN = float(np.finfo(np.float32).tiny)
LAST = 12

ATT = {
    "L0a": dict(H=16, dh=8, keys=256, group=16, scale=float(D) ** -0.5),
    "L0x": dict(H=16, dh=64, keys=256, group=4, scale=0.125),
    "L1x": dict(H=8, dh=64, keys=256, group=4, scale=0.125),
    "L2a": dict(H=16, dh=8, keys=192, group=16, scale=float(1.0 / np.float32(np.sqrt(8)))),
    "L2x": dict(H=16, dh=8, keys=256, group=16, scale=8.0 ** -0.5),
    "L3x": dict(H=16, dh=64, keys=256, group=4, scale=0.125),
}
FFN = {
    "L0f": dict(E=8, chunks=[4] * 8, glu=False),
    "L2f": dict(E=16, chunks=[1] * 16 + [2], glu=True),
    "L3f": dict(E=8, chunks=[4] * 8, glu=True),
}
LAYERS = ["L0a", "L0x", "L0f", "L1a", "L1x", "L1f", "L2a", "L2x", "L2f", "L3a", "L3x", "L3f"][:LAST]
HALO = 32
PADS = S + 2 * HALO

ROWS = {}
_at = 0
for _n, _w in [("L0x_bo", 128), ("L1x_bo", 128), ("L2a_bo", 128), ("L2x_bv", 128), ("L2x_bo", 128),
               ("L3a_bqkv", 384), ("L3a_bp", 128), ("L3x_bo", 128), ("L0f_b2", 1024), ("L1f_b2", 1024)]:
    ROWS[_n] = _at
    _at += _w
ROWS_W = _at
WIDE = {}
_at = 0
for _n, _w in [("gamma", 128), ("beta", 128), ("L0f_gb", 8), ("L2f_bias", 16), ("L1f_b3", 1024)]:
    WIDE[_n] = (_at, _w)
    _at += _w
WIDE_W = _at
COLS = {}
_at = 0
for _n, _w in [("L0f_b1", 32), ("L1a_b", 4), ("L1f_b1", 8), ("L2x_bq", 1), ("L2x_bk", 1)]:
    COLS[_n] = _at
    _at += _w
COLS_W = _at

WEIGHTS = {}


def _place(layer, region, parts):
    at = 0
    for name, cols, rows in parts:
        WEIGHTS[f"{layer}_{name}"] = (region, at, cols, rows)
        at += cols


_place("L0a", "wL0a", [("wq", 128, 128), ("wk", 128, 128), ("wv", 128, 128)])
_place("L1a", "wL1a", [("w", 512, 128), ("u", 512, 128)])
_place("L2a", "wL2a", [("wq", 128, 128), ("wk", 128, 128), ("wv", 128, 128), ("wo", 128, 128)])
_place("L2x", "wL2x", [("wq", 128, 128), ("wk", 128, CD), ("wv", 128, CD), ("wo", 128, 128)])
_place("L3a", "wL3a", [("wqkv", 384, 128), ("wp", 128, 128)])
_place("L1x", "wL1x", [("wq", 512, 128), ("wk", 512, CD), ("wv", 512, CD), ("wo", 512, 128)])
for _l in ("L0x", "L3x"):
    _place(_l, "wB", [("wq", 1024, 128), ("wk", 1024, CD), ("wv", 1024, CD), ("wo", 1024, 128)])
_place("L1f", "wB", [("w1", 1024, 128), ("w2", 1024, 128), ("w3", 1024, 128),
                     ("sg", 256, 128), ("su", 256, 128), ("sd", 256, 128)])
_place("L0f", "wA", [("up", 4096, 128), ("down", 4096, 128)])
_place("L2f", "wA", [("gate", 2304, 128), ("up", 2304, 128), ("down", 2304, 128)])
_place("L3f", "wA", [("gate", 4096, 128), ("up", 4096, 128), ("down", 4096, 128)])
GATES = {"L0f": (0, 8), "L1f": (8, 8), "L2f": (16, 16), "L3f": (32, 8)}
REGION_W = {"wL0a": 384, "wL1a": 1024, "wL2a": 512, "wL2x": 512, "wL3a": 512, "wL1x": 2048,
            "wB": 4096, "wA": 12288}
FREED_BY = {"L1f": "L0x", "L3x": "L1f", "L2f": "L0f", "L3f": "L2f"}


def side_schedule():
    sched = {}

    def put(layer, step, item):
        if item[0] == "tail" and layer == LAYERS[-1]:
            return
        sched.setdefault((layer, step), []).append(item)

    for b in range(B):
        put("init", b, ("tail", b))
    for layer in LAYERS:
        if layer in ATT:
            a = ATT[layer]
            U = a["H"]
            if layer == "L2x":
                put(layer, -3, ("nan",))
            for b in range(B):
                if a["dh"] == 64:
                    for p in range(a["H"] // 2):
                        at = -2 if b == 0 else (b - 1) * U + 2 * p + 3
                        put(layer, at, ("qk", b, p))
                        put(layer, at, ("v", b, p))
                    for i in range(U // a["group"]):
                        put(layer, b * U + 4 * i + 7, ("ot", b, i))
                    put(layer, (b + 1) * U + 5, ("wo", b))
                else:
                    at = -2 if b == 0 else (b - 1) * U + 4
                    if layer == "L2a":
                        put(layer, at, ("q", b))
                        put(layer, at, ("k", b))
                    else:
                        put(layer, at, ("qk", b))
                    if layer == "L0a":
                        put(layer, -4, ("v", b))
                    else:
                        put(layer, at, ("v", b))
                        if layer == "L2x":
                            put(layer, at, ("vmean", b))
                        put(layer, (b + 1) * U + 3, ("ot", b, 0))
                        put(layer, (b + 1) * U + 5, ("wo", b))
                put(layer, (b + 1) * U + 11, ("tail", b))
            if layer == "L0a":
                for kt in range(2):
                    put(layer, -5, ("rel", kt))
                for t in range(T):
                    for half in range(2):
                        put(layer, -3, ("relout", t, half))
        elif layer in FFN:
            put(layer, -2, ("gate",))
            E = len(FFN[layer]["chunks"])
            for b in range(B):
                put(layer, (b + 1) * E + 3, ("tail", b))
        elif layer == "L1f":
            put(layer, -2, ("gate",))
            for b in range(B):
                put(layer, (b + 1) * 9 + 2, ("tail", b))
        elif layer == "L1a":
            for b in range(B):
                put(layer, b, ("hout", b))
                put(layer, b + 1, ("tail", b))
        elif layer == "L3a":
            for b in range(B):
                put(layer, b, ("qT", b))
                put(layer, b, ("ot", b, 0))
                put(layer, b, ("wo", b))
                put(layer, b + 1, ("tail", b))
    order = {}
    n = 0
    for layer in ["init"] + LAYERS:
        for step in sorted(s for (l, s) in sched if l == layer):
            for item in sched[(layer, step)]:
                order[(layer, item)] = n
                n += 1
    return sched, order


def build(nc, d, out):
    sched, order = side_schedule()
    last_block = LAYERS[-1]

    def before(layer):
        i = LAYERS.index(layer)
        return "init" if i == 0 else LAYERS[i - 1]

    unit0, group0, n_unit, n_group = {}, {}, 0, 0
    hop0, exp0, n_hop, n_exp = {}, {}, 0, 0
    for l in LAYERS:
        if l in ATT:
            unit0[l], group0[l] = n_unit, n_group
            n_unit += B * ATT[l]["H"]
            n_group += B * ATT[l]["H"] // ATT[l]["group"]
        if l in FFN:
            per = sum(c if FFN[l]["glu"] else c // 2 for c in FFN[l]["chunks"])
            hop0[l], exp0[l] = n_hop, n_exp
            n_hop += B * per
            n_exp += B * len(FFN[l]["chunks"])

    glu_first, n_glu = {}, 0
    for l in LAYERS:
        if l in FFN and FFN[l]["glu"]:
            glu_first[l] = hop0[l] - n_glu
            n_glu += B * sum(FFN[l]["chunks"])
    N_VAR = B * (1 + len([l for l in LAYERS if l != "L3f"]) + ("L0a" in LAYERS))
    PER_VAR = 2 if last_block == "L0a" else 1
    tail_order = [order[k] for k in sorted((k for k in order if k[1][0] == "tail"), key=order.get)]
    zero_no, qz_no, scaled_no, rout_no, res_no, loads = {}, {}, {}, {}, {}, 0
    for l in LAYERS:
        if l in ATT:
            zero_no[l] = 1 + sum(1 for m in zero_no if ATT[m]["dh"] == 64)
            qz_no[l] = sum(1 for m in qz_no if ATT[m]["dh"] == 8)
            scaled_no[l] = len(scaled_no) + 1 + ("L2x" in scaled_no or l == "L2x")
        if l in GATES:
            rout_no[l] = len(rout_no) + 1
        if l in ATT or l in ("L1a", "L3a"):
            for b in range(B):
                res_no[(l, b)] = len(res_no)

    with ExitStack() as ctx:
        def sb(name, shape, dt=F32):
            return ctx.enter_context(nc.sbuf_tensor(name, shape, dt))

        def sem(name):
            return ctx.enter_context(nc.semaphore(name))

        psS = [ctx.enter_context(nc.psum_tensor(f"psS{i}", [P, 512], F32)) for i in range(2)]
        psT = [ctx.enter_context(nc.psum_tensor(f"psT{i}", [P, 512], F32)) for i in range(2)]
        psO = [ctx.enter_context(nc.psum_tensor(f"psO{i}", [P, 512], F32)) for i in range(2)]
        psM = [ctx.enter_context(nc.psum_tensor(f"psM{i}", [P, 512], F32)) for i in range(2)]
        psH = [psS[0], psS[1], psT[0], psT[1]]

        x = sb("x", [P, NT, D])
        xTs = sb("xTs", [P, 2, TOK])
        ctxT = sb("ctxT", [CD, TOK])
        qz = sb("qz", [P, 4096])
        kv = sb("kv", [P, 4096])
        prob = sb("prob", [P, 2, 512])
        probT = sb("probT", [P, 2, 512])
        o_sb = sb("o_sb", [P, 2, 512])
        oT = sb("oT", [P, 2048])
        o_res = sb("o_res", [P, T, D])
        hT = sb("hT", [P, 2, 4, 256])
        sg = sb("sg", [P, 2, 256])
        W = {r: sb(r, [P, w]) for r, w in REGION_W.items()}
        gw = sb("gw", [P, 40])
        rows = sb("rows", [P, ROWS_W])
        wide = sb("wide", [P, WIDE_W])
        cols = sb("cols", [P, COLS_W])
        ident = sb("ident", [P, P])
        ones = sb("ones", [P, P])
        identb = sb("identb", [P, P], BF16)
        band = sb("band", [P, 2, 192], BF16)
        relT = o_sb
        hmask = sb("hmask", [P, 16])
        inv_keys = sb("inv_keys", [P, P])
        nanmask = sb("nanmask", [P, 1], mybir.dt.int32)
        tri = sb("tri", [P, 16, 16])
        mhalf = sb("mhalf", [P, 2])
        negmax = sb("negmax", [P, 2, 2])
        rsum = sb("rsum", [P, 2, 32])
        rrec = sb("rrec", [P, 32])
        stats = sb("stats", [P, T, 6])
        mv = sb("mv", [P, T, 2])
        ve = sb("ve", [P, T])
        rstd = sb("rstd", [P, T])
        xn = sb("xn", [P, T, D])
        lg = sb("lg", [P, NT, 16])
        wexp = sb("wexp", [P, NT, 16])
        nanf = sb("nanf", [P, 8])
        rel_rows = hT[:, 0, :, :]
        v_all = hT[:, :, :, :].rearrange("p a c n -> p (a c n)").rearrange("p (b k n) -> p b k n", b=B, k=2)
        rel_out = oT[:, :].rearrange("p (t h b d) -> p t h b d", t=T, h=16, b=B)
        k_sb, v_sb = kv[:, 0:2048], kv[:, 2048:4096]
        xpad = hT[:, :, :, :].rearrange("p a c n -> p (a c n)")[:, 0:2 * PADS].rearrange("p (a n) -> p a n", a=2)
        clamped = hT[:, :, 0:2, :].rearrange("p a c n -> p a (c n)")
        gates = qz[:, 0:1024].rearrange("p (i n) -> p i n", i=4)
        c_state, tanh_c, c_in = qz[:, 1024:1280], qz[:, 1280:1536], qz[:, 2048:2304]
        qk3 = qz[:, 0:512].rearrange("p (t n) -> p t n", t=T)
        va3 = qz[:, 512:772].rearrange("p (t n) -> p t n", t=T)
        cm3 = qz[:, 1024:1168]
        ol3 = qz[:, 2048:2304].rearrange("p (t n) -> p t n", t=T)
        la, sk_d, sk_e = (prob[:, 0, 128 * i:128 * i + 128].rearrange("p (n e) -> p n e", e=8) for i in range(3))
        sk_s, sk_l, sk_m = (prob[:, 1, 32 * i:32 * i + 32] for i in range(3))
        sk_col, sk_diag = prob[:, 1, 128:256], prob[:, 1, 256:264]
        rank, r_a, r_b = (probT[:, :, :].rearrange("p a n -> p (a n)")[:, 256 * i:256 * i + 256] for i in range(3))
        r_s = probT[:, 1, 256:512]

        def q_small(b):
            return k_sb[:, 640 + 256 * (b % 2):896 + 256 * (b % 2)]

        def k_of(layer, b):
            return k_sb[:, PADS * (b % 2):PADS * (b % 2) + (PADS if layer == "L2a" else S)]

        def rel_bias(r, kt):
            return qz[:, 2048 * (r % 2) + 1024 * kt:2048 * (r % 2) + 1024 * kt + 1024]

        def h_state(b):
            return qz[:, 1536 + 256 * (b % 2):1792 + 256 * (b % 2)]

        s_load = {n: sem(f"s_load_{n}") for n in ["x", "ctx", "vec", "rel", "gw"] + LAYERS}
        s_relbias = sem("s_relbias")
        s_rel_ext = sem("s_rel_ext")
        s_const = sem("s_const")
        s_const2 = sem("s_const2")
        s_scaled = sem("s_scaled")
        s_qzero = sem("s_qzero")
        s_side_full = sem("s_side_full")
        s_side_done = sem("s_side_done")
        s_qk = sem("s_qk")
        s_max = sem("s_max")
        s_exp = sem("s_exp")
        s_tr = sem("s_tr")
        s_ptc = sem("s_ptc")
        s_pv = sem("s_pv")
        s_norm = sem("s_norm")
        s_qz = sem("s_qz")
        s_xpad = sem("s_xpad")
        s_var = sem("s_var")
        s_rstd = sem("s_rstd")
        s_xn = sem("s_xn")
        s_hfull = sem("s_hfull")
        s_sg = sem("s_sg")
        s_hop = sem("s_hop")
        s_down = sem("s_down")
        s_acc = sem("s_acc")
        s_dve = sem("s_dve")
        s_act = sem("s_act")
        s_bc = sem("s_bc")
        s_xs = sem("s_xs")
        s_a1 = sem("s_a1")
        s_h1 = sem("s_h1")
        s_x23 = sem("s_x23")
        s_t23 = sem("s_t23")
        s_shg = sem("s_shg")
        s_shs = sem("s_shs")
        s_shh = sem("s_shh")
        s_shd = sem("s_shd")
        s_sho = sem("s_sho")
        s_xadd = sem("s_xadd")
        s_pacc = sem("s_pacc")
        s_g = sem("s_g")
        s_ga = sem("s_ga")
        s_c = sem("s_c")
        s_tc = sem("s_tc")
        s_h = sem("s_h")
        s_routing_exp = sem("s_routing_exp")
        s_routing_in = sem("s_routing_in")
        s_qkv = sem("s_qkv")
        s_sub = sem("s_sub")
        s_ex3 = sem("s_ex3")
        s_v3 = sem("s_v3")
        s_sm3 = sem("s_sm3")
        s_ctx3 = sem("s_ctx3")
        s_cm3 = sem("s_cm3")
        s_num3 = sem("s_num3")
        s_ol3 = sem("s_ol3")
        s_sk_in = sem("s_sk_in")
        s_sk_act = sem("s_sk_act")
        s_sk_v = sem("s_sk_v")
        s_sk_pe = sem("s_sk_pe")
        s_nansum = sem("s_nansum")
        s_xfin = sem("s_xfin")
        s_out = sem("s_out")

        def w(layer, name, rws=None):
            region, at, n, r = WEIGHTS[f"{layer}_{name}"]
            return W[region][0:r, at:at + n]

        def xT(layer):
            return xTs[:, LAYERS.index(layer) % 2, :]

        def wide_of(name):
            at, n = WIDE[name]
            return wide[:, at:at + n]

        def heads_of(layer, p):
            return 2 * p, 2 * p + 1

        def all_done(eng, layer):
            eng.wait_ge(s_side_done, order[(before(layer), ("tail", B - 1))] + 1)

        def n_loads(layer):
            return 16 * sum(1 for k in WEIGHTS if k.startswith(layer + "_"))

        block = ctx.enter_context(nc.Block())

        @block.sync
        def _(sp):
            x_view = d["x"].rearrange("(n p) d -> p n d", p=P)
            sp.dma_start(x[:, :, :], x_view).then_inc(s_load["x"], 16)
            if "L0a" in LAYERS:
                sp.dma_start(d["rel_ext"][0:REL_ROWS, :], d["rel"]).then_inc(s_rel_ext, 16)
                sp.dma_start(d["rel_ext"][REL_ROWS:528, :],
                             d["rel"][REL_ROWS - 1:REL_ROWS, :].broadcast_to([528 - REL_ROWS, 16])).then_inc(s_rel_ext, 16)
            for l in LAYERS:
                if l in FREED_BY:
                    continue
                for k in WEIGHTS:
                    if k.startswith(l + "_"):
                        region, at, n, r = WEIGHTS[k]
                        sp.dma_start(W[region][0:r, at:at + n], d[k]).then_inc(s_load[l], 16)
                if l == "L0a":
                    sp.wait_ge(s_const2, 1)
                    sp.dma_start(rows[0:1, :], d["rows"]).then_inc(s_load["vec"], 16)
                    sp.dma_start(wide[:, :], d["wide"].broadcast_to([P, WIDE_W])).then_inc(s_load["vec"], 16)
                    sp.dma_start(cols[:, :], d["cols"]).then_inc(s_load["vec"], 16)
                    sp.dma_start(gw[:, :], d["gw"]).then_inc(s_load["gw"], 16)
                    sp.wait_ge(s_rel_ext, 32)
                    src = d["rel_ext"]
                    windows = bass.AP(tensor=src.tensor, offset=0, ap=[[16, P], [16 * P, 4], [1, 256]])
                    sp.dma_start(rel_rows, windows).then_inc(s_load["rel"], 16)
                    sp.dma_start(ctxT[:, :], d["ctxT"]).then_inc(s_load["ctx"], 16)
            for l in LAYERS:
                if l not in FREED_BY:
                    continue
                prev = FREED_BY[l]
                sp.wait_ge(s_side_done, order[(prev, ("tail", B - 1))] + 1)
                for k in WEIGHTS:
                    if k.startswith(l + "_"):
                        region, at, n, r = WEIGHTS[k]
                        sp.dma_start(W[region][0:r, at:at + n], d[k]).then_inc(s_load[l], 16)
            o_view = out.rearrange("(n p) d -> p n d", p=P)
            for b in range(B):
                if last_block == "L3f":
                    sp.wait_ge(s_acc, exp0["L3f"] + 8 * (b + 1))
                else:
                    sp.wait_ge(s_var, N_VAR - (B - 1 - b) * PER_VAR)
                sp.dma_start(o_view[:, T * b:T * b + T, :], x[:, T * b:T * b + T, :]).then_inc(s_out, 16)
            sp.wait_ge(s_out, 16 * B)

        @block.gpsimd
        def _(pool):
            g = nc.gpsimd
            step = [0]

            def link(ins):
                step[0] += 1
                ins.then_inc(s_const, 1)
                pool.wait_ge(s_const, step[0])

            g.memset(rows[:, :], 0.0).then_inc(s_const2, 1)
            g.memset(mhalf[:, :], -0.5)
            g.memset(ones[:, :], 1.0)
            g.memset(inv_keys[:, :], 1.0 / S)
            link(g.memset(ident[:, :], 0.0))
            link(g.affine_select(out=ident[:, :], in_=ident[:, :], compare_op=ALU.not_equal, fill=1.0, base=0,
                                 pattern=[[-1, P]], channel_multiplier=1))
            link(g.tensor_copy(identb[:, :], ident[:, :]))
            link(g.memset(band[:, :, :], 0.0))
            link(g.affine_select(out=band[:, :, :], in_=band[:, :, :], compare_op=ALU.is_ge, fill=MASKED, base=0,
                                 pattern=[[0, 2], [1, 192]], channel_multiplier=-1))
            link(g.affine_select(out=band[:, :, :], in_=band[:, :, :], compare_op=ALU.is_ge, fill=MASKED,
                                 base=2 * HALO - 1, pattern=[[0, 2], [-1, 192]], channel_multiplier=1))
            link(g.memset(hmask[:, :], 1.0))
            link(g.affine_select(out=hmask[:, :], in_=hmask[:, :], compare_op=ALU.is_ge, fill=0.0, base=0,
                                 pattern=[[-8, 16]], channel_multiplier=1))
            link(g.affine_select(out=hmask[:, :], in_=hmask[:, :], compare_op=ALU.is_ge, fill=0.0, base=7,
                                 pattern=[[8, 16]], channel_multiplier=-1))
            link(g.memset(tri[:, :, :], 1.0))
            link(g.affine_select(out=tri[:, :, :], in_=tri[:, :, :], compare_op=ALU.is_gt, fill=0.0, base=0,
                                 pattern=[[1, 16], [-1, 16]], channel_multiplier=0))
            powers = [0]

            def inverse_root():
                n = powers[0]
                powers[0] += 1
                pool.wait_ge(s_var, n + 1)
                g.tensor_tensor(rstd[:, :], ve[:, :], mhalf[:, :], ALU.pow).then_inc(s_rstd, 1)

            def pad_x(layer, b):
                if b >= 2:
                    pool.wait_ge(s_side_done, order[(layer, ("v", b - 2))] + 1)
                g.tensor_copy(xpad[:, b % 2, HALO:HALO + S], xT(layer)[:, S * b:S * b + S]).then_inc(s_xpad, 1)

            def mask_queries(layer, b):
                pool.wait_ge(s_side_done, order[(layer, ("q" if layer == "L2a" else "qk", b))] + 1)
                for h in range(16):
                    if b:
                        pool.wait_ge(s_qk, unit0[layer] + (b - 1) * 16 + 2 * (h // 2) + 2)
                    g.tensor_scalar(qz[:, 256 * h:256 * h + 256], q_small(b), hmask[:, h:h + 1], None,
                                    ALU.mult).then_inc(s_qz, 1)

            for b in range(B):
                inverse_root()
            for layer in LAYERS:
                if layer in ATT:
                    a = ATT[layer]
                    pool.wait_ge(s_load[layer], n_loads(layer))
                    g.tensor_scalar(w(layer, "wq"), w(layer, "wq"), a["scale"], None, ALU.mult).then_inc(s_scaled, 1)
                    if layer == "L2x":
                        pool.wait_ge(s_load["vec"], 48)
                        at = COLS["L2x_bq"]
                        g.tensor_scalar(cols[:, at:at + 1], cols[:, at:at + 1], a["scale"], None,
                                        ALU.mult).then_inc(s_scaled, 1)
                    all_done(pool, layer)
                    if a["dh"] == 64:
                        g.memset(qz[:, :], 0.0).then_inc(s_qzero, 1)
                    if layer == "L2a":
                        g.memset(xpad[:, :, 0:HALO], 0.0)
                        g.memset(xpad[:, :, HALO + S:PADS], 0.0)
                        for i in range(2):
                            g.memset(v_sb[0:64, 512 * i + 256:512 * i + 512], 0.0)
                        pad_x(layer, 0)
                    if layer == "L0a":
                        pool.wait_ge(s_side_full, order[(layer, ("relout", T - 1, 1))] + 1)
                    for b in range(B):
                        if layer == "L2a" and b + 1 < B:
                            pad_x(layer, b + 1)
                        if a["dh"] == 8:
                            mask_queries(layer, b)
                        if b:
                            if layer == "L0a":
                                inverse_root()
                            inverse_root()
                    if layer == "L0a":
                        inverse_root()
                    inverse_root()
                elif layer == "L1f":
                    for b in range(B):
                        for e in range(8):
                            n = 8 * b + e
                            pool.wait_ge(s_t23, n + 1)
                            if n:
                                pool.wait_ge(s_pacc, n)
                            g.tensor_tensor(x[:, T * b:T * b + T, :], x[:, T * b:T * b + T, :],
                                            o_sb[:, n % 2, 0:256].rearrange("p (t d) -> p t d", t=T),
                                            ALU.add).then_inc(s_pacc, 1)
                        inverse_root()
                elif layer != "L3f":
                    for b in range(B):
                        inverse_root()

        @block.scalar
        def _(act):
            a_ = nc.scalar
            copy = lambda dst, src: a_.activation(dst, src, ACT.Copy)
            side = [0]

            def move(layer, item):
                k = side[0]
                side[0] += 1
                m = psM[k % 2]
                kind, b = item[0], (item[1] if len(item) > 1 else 0)
                act.wait_ge(s_side_full, k + 1)
                if kind == "tail":
                    nxt = LAYERS[0] if layer == "init" else LAYERS[LAYERS.index(layer) + 1]
                    ins = copy(xT(nxt)[:, S * b:S * b + S], m[:, 0:256])
                elif kind == "qk" and ATT[layer]["dh"] == 64:
                    p = item[2]
                    if b == 0 and p == 0:
                        act.wait_ge(s_qzero, zero_no[layer])
                    copy(qz[0:64, 512 * p:512 * p + 256], m[0:64, 0:256])
                    copy(qz[64:128, 512 * p + 256:512 * p + 512], m[64:128, 0:256])
                    ins = copy(k_sb[:, 256 * p:256 * p + 256], m[:, 256:512])
                elif kind == "qk":
                    if b >= 2:
                        act.wait_ge(s_qz, 16 * (8 * qz_no[layer] + b - 1))
                    if layer == "L2x":
                        cq, ck = COLS["L2x_bq"], COLS["L2x_bk"]
                        act.wait_ge(s_scaled, scaled_no[layer])
                        act.wait_ge(s_load["vec"], 48)
                        a_.activation(q_small(b), m[:, 0:256], ACT.Identity, bias=cols[:, cq:cq + 1])
                        ins = a_.activation(k_of(layer, b), m[:, 256:512], ACT.Identity, bias=cols[:, ck:ck + 1])
                    else:
                        copy(q_small(b), m[:, 0:256])
                        ins = copy(k_of(layer, b), m[:, 256:512])
                elif kind == "q":
                    if b >= 2:
                        act.wait_ge(s_qz, 16 * (8 * qz_no[layer] + b - 1))
                    ins = copy(q_small(b), m[:, 0:256])
                elif kind == "k":
                    ins = copy(k_of(layer, b), m[:, 0:PADS])
                elif kind == "v" and ATT[layer]["dh"] == 64:
                    p = item[2]
                    ins = copy(v_sb[:, :].rearrange("p (k n) -> p k n", k=2)[:, :, 128 * p:128 * p + 128],
                               m[:, 0:256].rearrange("p (k n) -> p k n", k=2))
                elif kind == "v":
                    if layer == "L0a":
                        ins = copy(v_all[:, b, :, :], m[:, 0:256].rearrange("p (k n) -> p k n", k=2))
                    elif layer == "L2a":
                        at = 512 * (b % 2)
                        copy(v_sb[:, at:at + 256], m[:, 0:256])
                        ins = copy(v_sb[64:128, at + 256:at + 512], m[64:128, 256:512])
                    else:
                        at = 512 * (b % 2)
                        ins = copy(v_sb[:, at:at + 256], m[:, 0:256])
                elif kind == "vmean":
                    ins = copy(v_sb[:, 1024 + 128 * (b % 2):1152 + 128 * (b % 2)], m[:, 0:128])
                elif kind == "nan":
                    ins = copy(nanf[:, 5:6], m[:, 0:1])
                elif kind == "rel":
                    ins = copy(relT[:, b, :], m[:, :])
                elif kind == "relout":
                    t, half = item[1], item[2]
                    ins = copy(rel_out[:, t, 8 * half:8 * half + 8, :, :].rearrange("p h b d -> p (h b d)"), m[:, :])
                elif kind == "ot" and layer in ATT and ATT[layer]["dh"] == 64:
                    a = ATT[layer]
                    j0 = (2 * item[2]) % (a["H"] // 2)
                    dst = oT[:, 0:64 * a["H"] * T].rearrange("p (t j n) -> p j t n", t=T, j=a["H"] // 2)[:, j0:j0 + 2, :, :]
                    ins = copy(dst, m[:, :].rearrange("p (j t n) -> p j t n", j=2, t=T))
                elif kind in ("ot", "qT"):
                    ins = copy(oT[:, 0:256], m[:, 0:256]) if kind == "ot" else copy(oT[:, 256:512], m[:, 0:256])
                elif kind in ("wo", "hout"):
                    r = res_no[(layer, b)]
                    if r:
                        act.wait_ge(s_xadd, r)
                    ins = copy(o_res[:, :, :], m[:, 0:256].rearrange("p (t d) -> p t d", t=T))
                elif kind == "gate":
                    E = GATES[layer][1]
                    ins = copy(lg[:, :, 0:E], m[:, 0:NT * E].rearrange("p (n e) -> p n e", n=NT))
                ins.then_inc(s_side_done, 1)

            def moves(layer, step):
                for item in sched.get((layer, step), ()):
                    move(layer, item)

            def attention(layer):
                a = ATT[layer]
                U, K, g0 = a["H"], a["keys"], unit0[layer]
                NU = B * U
                for s in range(-5, NU + 13):
                    u = s + 1
                    if 0 <= u < NU:
                        g = g0 + u
                        act.wait_ge(s_max, g + 1)
                        if g >= 2:
                            act.wait_ge(s_tr, g - 1)
                        for i in range(2):
                            sc = clamped[:, g % 2, :] if layer == "L2x" else psS[g % 2][:, :]
                            ins = a_.activation(prob[:, g % 2, K * i:K * i + K], sc[:, K * i:K * i + K], ACT.Exp,
                                                bias=negmax[:, g % 2, i:i + 1],
                                                accum_out=rsum[:, (u // U) % 2, 2 * (u % U) + i:2 * (u % U) + i + 1])
                        ins.then_inc(s_exp, 1)
                    moves(layer, s)

            def experts(layer):
                f = FFN[layer]
                E = len(f["chunks"])
                NE = B * E
                hop = hop0[layer]
                for n in range(-1, NE + 4):
                    if n + 1 < NE:
                        e = (n + 1) % E
                        g = exp0[layer] + n + 1
                        C = f["chunks"][e]
                        if f["glu"]:
                            for c in range(C):
                                act.wait_ge(s_hfull, hop + 1)
                                if hop >= 2:
                                    act.wait_ge(s_hop, hop - 1)
                                a_.activation(sg[:, hop % 2, :], psH[hop % 4][:, 0:256], ACT.Silu).then_inc(s_sg, 1)
                                hop += 1
                        else:
                            if n + 1 == 0:
                                act.wait_ge(s_load["vec"], 48)
                            if g >= 2:
                                act.wait_ge(s_down, g - 1)
                            for c in range(0, C, 2):
                                act.wait_ge(s_hfull, hop + 1)
                                for i in range(2):
                                    at = COLS[layer + "_b1"] + 4 * e + c + i
                                    ins = a_.activation(hT[:, g % 2, c + i, :], psH[hop % 4][:, 256 * i:256 * i + 256],
                                                        ACT.Gelu, bias=cols[:, at:at + 1])
                                ins.then_inc(s_hop, 1)
                                hop += 1
                    moves(layer, n)

            for b in range(B):
                moves("init", b)
            for layer in LAYERS:
                if layer in ATT:
                    attention(layer)
                elif layer in FFN:
                    moves(layer, -2)
                    if layer != "L3f":
                        if layer == "L2f":
                            act.wait_ge(s_side_done, order[(layer, ("gate",))] + 1)
                        else:
                            act.wait_ge(s_routing_in, rout_no[layer])
                        a_.activation(wexp[:, :, 0:GATES[layer][1]], lg[:, :, 0:GATES[layer][1]],
                                      ACT.Exp if layer == "L0f" else ACT.Sigmoid).then_inc(s_routing_exp, 1)
                    if layer == "L3f":
                        for k in range(4 * SINK_ITERS + 1):
                            act.wait_ge(s_sk_in, k + 1)
                            if k % 4 in (0, 2):
                                a_.activation(sk_e[:, :, :], sk_d[:, :, :] if k < 4 * SINK_ITERS else la[:, :, :],
                                              ACT.Exp).then_inc(s_sk_act, 1)
                            elif k % 4 == 1:
                                a_.activation(sk_l[:, 0:16], sk_s[:, 0:16], ACT.Ln).then_inc(s_sk_act, 1)
                            else:
                                a_.activation(sk_l[:, 0:8], psO[1][:, 0:8], ACT.Ln).then_inc(s_sk_act, 1)
                    experts(layer)
                elif layer == "L1f":
                    moves(layer, -2)
                    act.wait_ge(s_routing_in, rout_no[layer])
                    a_.activation(wexp[:, :, 0:8], lg[:, :, 0:8], ACT.Exp).then_inc(s_routing_exp, 1)
                    act.wait_ge(s_load["vec"], 48)
                    for b in range(B):
                        for e in range(9):
                            step = 9 * b + e
                            if e < 8:
                                n = 8 * b + e
                                act.wait_ge(s_a1, n + 1)
                                if n >= 2:
                                    act.wait_ge(s_x23, n - 1)
                                at = COLS["L1f_b1"] + e
                                a_.activation(hT[:, n % 2, 0, :], psT[n % 2][:, 0:256], ACT.Silu,
                                              bias=cols[:, at:at + 1]).then_inc(s_h1, 1)
                            else:
                                for c in range(2):
                                    act.wait_ge(s_shg, 2 * b + c + 1)
                                    if b:
                                        act.wait_ge(s_shh, 2 * (b - 1) + c + 1)
                                    a_.activation(sg[:, c, :], psS[c][:, 0:256], ACT.Silu).then_inc(s_shs, 1)
                            moves(layer, step)
                    moves(layer, 72)
                    moves(layer, 73)
                    moves(layer, 74)
                elif layer == "L1a":
                    act.wait_ge(s_load["vec"], 48)
                    for b in range(B + 1):
                        if b < B:
                            act.wait_ge(s_g, b + 1)
                            if b:
                                act.wait_ge(s_h, b)
                            for i in range(4):
                                at = COLS["L1a_b"] + i
                                ins = a_.activation(gates[:, i, :], psH[i][:, 0:256], ACT.Sigmoid if i < 3 else ACT.Tanh,
                                                    bias=cols[:, at:at + 1])
                            ins.then_inc(s_ga, 1)
                            act.wait_ge(s_c, b + 1)
                            a_.activation(tanh_c, c_state, ACT.Tanh).then_inc(s_tc, 1)
                        moves(layer, b)
                elif layer == "L3a":
                    for b in range(B + 1):
                        if b < B:
                            for t in range(T):
                                n = T * b + t
                                act.wait_ge(s_sub, n + 1)
                                a_.activation(qk3[:, t, :], qk3[:, t, :], ACT.Exp).then_inc(s_ex3, 1)
                                if n >= 2:
                                    act.wait_ge(s_ctx3, b)
                                copy(va3[:, t, 0:128], psS[t][:, 256:384]).then_inc(s_v3, 1)
                        moves(layer, b)

        @block.tensor
        def _(pe):
            mm = nc.tensor.matmul
            side = [0]
            tails = [0]

            def across(out_, in_):
                return nc.tensor.transpose(out_, in_, ident[:, :])

            def row_bias(out_, name, at=0, n=128, stop=True):
                return mm(out_, ones[:, :], rows[:, ROWS[name] + at:ROWS[name] + at + n], start=False, stop=stop)

            def fill(layer, item):
                k = side[0]
                side[0] += 1
                m = psM[k % 2]
                kind, b = item[0], (item[1] if len(item) > 1 else 0)
                if k >= 2:
                    pe.wait_ge(s_side_done, k - 1)
                tok = lambda t: slice(S * b + P * t, S * b + P * t + P)
                if kind == "tail":
                    n = tails[0]
                    tails[0] += 1
                    pe.wait_ge(s_xn, n + 1)
                    for t in range(T):
                        ins = across(m[:, P * t:P * t + P], xn[:, t, :])
                elif kind == "qk":
                    dh64 = ATT[layer]["dh"] == 64
                    at = 128 * item[2] if dh64 else 0
                    src = xT(layer) if layer == "L0a" else ctxT[:, :]
                    mm(m[:, 0:256], w(layer, "wq")[:, at:at + 128], xT(layer)[:, S * b:S * b + S], start=True, stop=True)
                    ins = mm(m[:, 256:512], w(layer, "wk")[:, at:at + 128], src[:, S * b:S * b + S], start=True, stop=True)
                elif kind == "q":
                    ins = mm(m[:, 0:256], w(layer, "wq"), xT(layer)[:, S * b:S * b + S], start=True, stop=True)
                elif kind == "k":
                    pe.wait_ge(s_xpad, b + 1)
                    ins = mm(m[:, 0:PADS], w(layer, "wk"), xpad[:, b % 2, :], start=True, stop=True)
                elif kind == "v":
                    if layer == "L2a":
                        for i, at in enumerate((0, P, P // 2, P + P // 2)):
                            ins = mm(m[:, P * i:P * i + P], xpad[:, b % 2, at:at + P], w(layer, "wv"), start=True, stop=True)
                    else:
                        at = 128 * item[2] if ATT[layer]["dh"] == 64 else 0
                        src = xT(layer) if layer == "L0a" else ctxT[:, :]
                        for kt in range(2):
                            ins = mm(m[:, P * kt:P * kt + P], src[:, tok(kt)], w(layer, "wv")[:, at:at + 128],
                                     start=True, stop=layer != "L2x")
                            if layer == "L2x":
                                ins = row_bias(m[:, P * kt:P * kt + P], "L2x_bv")
                elif kind == "vmean":
                    pe.wait_ge(s_side_done, order[(layer, ("v", b))] + 1)
                    for kt in range(2):
                        ins = mm(m[:, 0:128], inv_keys[:, :], v_sb[:, 512 * (b % 2) + P * kt:512 * (b % 2) + P * kt + P],
                                 start=kt == 0, stop=kt == 1)
                elif kind == "nan":
                    pe.wait_ge(s_nansum, 1)
                    ins = mm(m[:, 0:1], ones[:, :], nanf[:, 4:5], start=True, stop=True)
                elif kind == "rel":
                    if b == 0:
                        pe.wait_ge(s_load["rel"], 16)
                    for j in range(4):
                        ins = across(m[:, P * j:P * j + P], rel_rows[:, j, P * b:P * b + P])
                elif kind == "relout":
                    t, half = item[1], item[2]
                    r = 2 * t + half
                    pe.wait_ge(s_side_done, order[(layer, ("v", B - 1))] + 1)
                    pe.wait_ge(s_relbias, r + 1)
                    for h in range(8 * half, 8 * half + 8):
                        for kt in range(2):
                            at = 64 * (h % 8)
                            ins = mm(m[:, at:at + 64].rearrange("p (b d) -> p b d", b=B),
                                     rel_bias(r, kt)[:, P * (h % 8):P * (h % 8) + P],
                                     v_all[:, :, kt, 8 * h:8 * h + 8], start=kt == 0, stop=kt == 1)
                elif kind == "ot" and layer == "L3a":
                    pe.wait_ge(s_cm3, b + 1)
                    pe.wait_ge(s_side_done, order[(layer, ("qT", b))] + 1)
                    for t in range(T):
                        ins = mm(psT[1][:, 144 * t:144 * t + 144], oT[:, 256 + P * t:256 + P * t + P], cm3,
                                 start=True, stop=True)
                    ins.then_inc(s_num3, 1)
                    pe.wait_ge(s_ol3, b + 1)
                    for t in range(T):
                        ins = across(m[:, P * t:P * t + P], ol3[:, t, :])
                elif kind == "ot":
                    a = ATT[layer]
                    per = a["H"] // a["group"]
                    gi = per * b + item[2]
                    pe.wait_ge(s_norm, group0[layer] + gi + 1)
                    for i in range(4 if a["dh"] == 64 else 2):
                        ins = across(m[:, P * i:P * i + P], o_sb[:, gi % 2, P * i:P * i + P])
                elif kind == "wo":
                    n_ot = 0 if layer == "L3a" else ATT[layer]["H"] // ATT[layer]["group"] - 1
                    pe.wait_ge(s_side_done, order[(layer, ("ot", b, n_ot))] + 1)
                    J = ATT[layer]["H"] // 2 if layer in ATT and ATT[layer]["dh"] == 64 else 1
                    wo = w(layer, "wp" if layer == "L3a" else "wo")
                    for t in range(T):
                        for j in range(J):
                            mm(m[:, P * t:P * t + P], oT[:, P * (J * t + j):P * (J * t + j) + P],
                               wo[:, P * j:P * j + P], start=j == 0, stop=False)
                        ins = row_bias(m[:, P * t:P * t + P], layer + ("_bp" if layer == "L3a" else "_bo"))
                elif kind == "hout":
                    pe.wait_ge(s_h, b + 1)
                    for t in range(T):
                        ins = across(m[:, P * t:P * t + P], h_state(b)[:, P * t:P * t + P])
                elif kind == "qT":
                    pe.wait_ge(s_sm3, 2 * b + 2)
                    for t in range(T):
                        ins = across(m[:, P * t:P * t + P], qk3[:, t, 0:128])
                elif kind == "gate":
                    at, E = GATES[layer]
                    for n in range(NT):
                        ins = mm(m[:, E * n:E * n + E], xT(layer)[:, P * n:P * n + P], gw[:, at:at + E], start=True, stop=True)
                ins.then_inc(s_side_full, 1)

            def fills(layer, step):
                for item in sched.get((layer, step), ()):
                    fill(layer, item)

            def attention(layer):
                a = ATT[layer]
                dh, U, K, g0, size = a["dh"], a["H"], a["keys"], unit0[layer], a["group"]
                NU = B * U
                pe.wait_ge(s_scaled, scaled_no[layer])

                def scores(u):
                    b, r, g = u // U, u % U, g0 + u
                    p, t = r // 2, r % 2
                    bank = psS[g % 2]
                    if g >= 2:
                        pe.wait_ge(s_exp, g - 1)
                    if t == 0:
                        if dh == 64:
                            pe.wait_ge(s_side_done, order[(layer, ("qk", b, p))] + 1)
                        else:
                            pe.wait_ge(s_qz, 128 * qz_no[layer] + 16 * b + 2 * p + 2)
                            if p == 0:
                                pe.wait_ge(s_side_done, order[(layer, ("k" if layer == "L2a" else "qk", b))] + 1)
                    if layer == "L2a":
                        mm(bank[:, 0:2 * K], identb[:, :], band[:, :, :].rearrange("p h k -> p (h k)"), start=True, stop=False)
                    for i in range(2):
                        h = 2 * p + i
                        if dh == 64:
                            keys = k_sb[:, 256 * p:256 * p + 256]
                        elif layer == "L2a":
                            keys = k_of(layer, b)[:, P * t:P * t + K]
                        else:
                            keys = k_of(layer, b)
                        ins = mm(bank[:, K * i:K * i + K], qz[:, 256 * h + P * t:256 * h + P * t + P], keys,
                                 start=layer != "L2a", stop=layer != "L2a" or i == 1)
                    ins.then_inc(s_qk, 1)

                def turn(u):
                    g = g0 + u
                    pe.wait_ge(s_exp, g + 1)
                    if g >= 2:
                        pe.wait_ge(s_ptc, g - 1)
                    for i in range(2):
                        for kt in range(2):
                            at = K * i + (K - P) * kt
                            ins = across(psT[g % 2][:, P * (2 * i + kt):P * (2 * i + kt) + P], prob[:, g % 2, at:at + P])
                    ins.then_inc(s_tr, 1)

                def weigh(u):
                    b, r, g = u // U, u % U, g0 + u
                    p, t = r // 2, r % 2
                    gi = group0[layer] + u // size
                    pe.wait_ge(s_ptc, g + 1)
                    if t == 0 and (dh == 64 or p == 0):
                        pe.wait_ge(s_side_done, order[(layer, ("v", b, p) if dh == 64 else ("v", b))] + 1)
                    if u % size == 0 and gi >= 2:
                        pe.wait_ge(s_norm, gi - 1)
                    for i in range(2):
                        h = 2 * p + i
                        at = (u % size) * 2 * dh + dh * i
                        for kt in range(2):
                            if dh == 64:
                                v = v_sb[:, 1024 * kt + 64 * h:1024 * kt + 64 * h + 64]
                            elif layer == "L0a":
                                v = v_all[:, b, kt, 8 * h:8 * h + 8]
                            else:
                                c = 512 * (b % 2) + (P * kt if layer == "L2x" else P * (2 * kt + t)) + 8 * h
                                v = v_sb[:, c:c + 8]
                            ins = mm(psO[gi % 2][:, at:at + dh], probT[:, g % 2, P * (2 * i + kt):P * (2 * i + kt) + P], v,
                                     start=kt == 0, stop=kt == 1)
                    ins.then_inc(s_pv, 1)

                for s in range(-5, NU + 13):
                    if 0 <= s + 1 < NU:
                        scores(s + 1)
                    fills(layer, s)
                    if 0 <= s < NU:
                        turn(s)
                    if 0 <= s - 1 < NU:
                        weigh(s - 1)

            def experts(layer):
                f = FFN[layer]
                E, glu = len(f["chunks"]), f["glu"]
                NE = B * E
                hop = [hop0[layer]]
                hops_of = {}

                def up(n):
                    b, e = n // E, n % E
                    toks = xT(layer)[:, S * b:S * b + S]
                    at = 128 * sum(f["chunks"][:e])
                    for c in range(0, f["chunks"][e], 1 if glu else 2):
                        if hop[0] >= 4:
                            pe.wait_ge(s_hop, hop[0] - 3)
                        bank = psH[hop[0] % 4]
                        for i in range(2):
                            if glu:
                                lhsT = w(layer, ("gate", "up")[i])[:, at + 128 * c:at + 128 * c + 128]
                            else:
                                lhsT = w(layer, "up")[:, at + 128 * (c + i):at + 128 * (c + i) + 128]
                            ins = mm(bank[:, 256 * i:256 * i + 256], lhsT, toks, start=True, stop=True)
                        ins.then_inc(s_hfull, 1)
                        hop[0] += 1
                    hops_of[n] = hop[0]

                def down(n):
                    e, g = n % E, exp0[layer] + n
                    C = f["chunks"][e]
                    at = 128 * sum(f["chunks"][:e])
                    pe.wait_ge(s_hop, hops_of[n])
                    if g >= 2:
                        pe.wait_ge(s_acc, g - 1)
                    for t in range(T):
                        o = psO[g % 2][:, P * t:P * t + P]
                        for c in range(C):
                            ins = mm(o, hT[:, g % 2, c, P * t:P * t + P], w(layer, "down")[:, at + 128 * c:at + 128 * c + 128],
                                     start=c == 0, stop=c == C - 1 and layer != "L0f")
                        if layer == "L0f":
                            ins = row_bias(o, "L0f_b2", 128 * e)
                    ins.then_inc(s_down, 1)

                for n in range(-1, NE + 4):
                    if n + 1 < NE:
                        up(n + 1)
                    fills(layer, n)
                    if 0 <= n < NE:
                        down(n)

            pe.wait_ge(s_const, 11)
            for b in range(B):
                fills("init", b)
            for layer in LAYERS:
                pe.wait_ge(s_load[layer], n_loads(layer))
                all_done(pe, layer)
                if layer == "L0a":
                    pe.wait_ge(s_load["vec"], 48)
                    pe.wait_ge(s_load["gw"], 16)
                    pe.wait_ge(s_load["ctx"], 16)
                if layer in ATT:
                    attention(layer)
                elif layer in FFN:
                    fills(layer, -2)
                    if layer == "L3f":
                        for it in range(SINK_ITERS):
                            pe.wait_ge(s_sk_v, 3 * it + 1)
                            across(psO[0][:, 0:128], sk_col).then_inc(s_sk_pe, 1)
                            pe.wait_ge(s_sk_v, 3 * it + 2)
                            mm(psO[0][:, 0:8], ones[:, :], sk_diag, start=True, stop=True).then_inc(s_sk_pe, 1)
                            pe.wait_ge(s_sk_v, 3 * it + 3)
                            mm(psO[1][:, 0:8], ones[:, :], sk_s[:, 16:24], start=True, stop=True).then_inc(s_sk_in, 1)
                    experts(layer)
                elif layer == "L1a":
                    def from_x(b):
                        if b:
                            pe.wait_ge(s_ga, b)
                        for i in range(4):
                            ins = mm(psH[i][:, 0:256], w(layer, "w")[:, P * i:P * i + P], xT(layer)[:, S * b:S * b + S],
                                     start=True, stop=b == 0)
                        if b == 0:
                            ins.then_inc(s_g, 1)

                    from_x(0)
                    for b in range(B + 1):
                        if 1 <= b < B:
                            pe.wait_ge(s_h, b)
                            for i in range(4):
                                ins = mm(psH[i][:, 0:256], w(layer, "u")[:, P * i:P * i + P], h_state(b - 1),
                                         start=False, stop=True)
                            ins.then_inc(s_g, 1)
                        if b + 1 < B:
                            from_x(b + 1)
                        fills(layer, b)
                elif layer == "L1f":
                    fills(layer, -2)

                    def spread(n):
                        b, e = n // 8, n % 8
                        if n == 0:
                            pe.wait_ge(s_routing_in, rout_no[layer] + 1)
                        if n >= 2:
                            pe.wait_ge(s_xs, n - 1)
                        if b and e < 2:
                            pe.wait_ge(s_shh, 2 * b)
                        for t in range(T):
                            ins = mm(psS[n % 2][:, P * t:P * t + P],
                                     wexp[:, T * b + t, e:e + 1].broadcast_to([P, P]), ident[:, :], start=True, stop=True)
                        ins.then_inc(s_bc, 1)

                    def first(n):
                        e = n % 8
                        pe.wait_ge(s_xs, n + 1)
                        if n >= 2:
                            pe.wait_ge(s_h1, n - 1)
                        mm(psT[n % 2][:, 0:256], w(layer, "w1")[:, P * e:P * e + P], prob[:, n % 2, 0:256],
                           start=True, stop=True).then_inc(s_a1, 1)

                    def second(n):
                        b, e = n // 8, n % 8
                        if n >= 2:
                            pe.wait_ge(s_t23, n - 1)
                        if b and e < 2:
                            pe.wait_ge(s_sho, b)
                        o = psO[n % 2]
                        for t in range(T):
                            mm(o[:, P * t:P * t + P], xT(layer)[:, S * b + P * t:S * b + P * t + P],
                               w(layer, "w3")[:, P * e:P * e + P], start=True, stop=True)
                        pe.wait_ge(s_h1, n + 1)
                        for t in range(T):
                            at = 256 + P * t
                            mm(o[:, at:at + P], hT[:, n % 2, 0, P * t:P * t + P], w(layer, "w2")[:, P * e:P * e + P],
                               start=True, stop=False)
                            ins = row_bias(o[:, at:at + P], "L1f_b2", 128 * e)
                        ins.then_inc(s_x23, 1)

                    spread(0)
                    spread(1)
                    first(0)
                    for b in range(B):
                        for e in range(8):
                            n = 8 * b + e
                            if n + 2 < 8 * B and e < 6:
                                spread(n + 2)
                            if n + 1 < 8 * B and e < 7:
                                first(n + 1)
                            second(n)
                            fills(layer, 9 * b + e)
                        pe.wait_ge(s_xs, 8 * b + 8)
                        toks = xT(layer)[:, S * b:S * b + S]
                        for c in range(2):
                            for i, name in enumerate(("sg", "su")):
                                ins = mm(psS[c][:, 256 * i:256 * i + 256], w(layer, name)[:, P * c:P * c + P], toks,
                                         start=True, stop=True)
                            ins.then_inc(s_shg, 1)
                        pe.wait_ge(s_t23, 8 * b + 8)
                        pe.wait_ge(s_shh, 2 * b + 2)
                        for t in range(T):
                            for c in range(2):
                                ins = mm(psO[0][:, P * t:P * t + P], hT[:, c, 3, P * t:P * t + P],
                                         w(layer, "sd")[:, P * c:P * c + P], start=c == 0, stop=c == 1)
                        ins.then_inc(s_shd, 1)
                        if b + 1 < B:
                            spread(8 * b + 8)
                            spread(8 * b + 9)
                            first(8 * b + 8)
                        fills(layer, 9 * b + 8)
                    for s in range(72, 76):
                        fills(layer, s)
                elif layer == "L3a":
                    def project(b):
                        for t in range(T):
                            if b:
                                pe.wait_ge(s_v3, T * (b - 1) + t + 1)
                            mm(psS[t][:, 0:384], xT(layer)[:, S * b + P * t:S * b + P * t + P], w(layer, "wqkv"),
                               start=True, stop=False)
                            row_bias(psS[t][:, 0:384], "L3a_bqkv", 0, 384).then_inc(s_qkv, 1)

                    project(0)
                    for b in range(B + 1):
                        if b < B:
                            pe.wait_ge(s_sm3, T * (b + 1))
                            pe.wait_ge(s_v3, T * (b + 1))
                            for t in range(T):
                                ins = mm(psT[0][:, 0:129], qk3[:, t, 128:256], va3[:, t, 0:129], start=t == 0, stop=t == 1)
                            ins.then_inc(s_ctx3, 1)
                            if b + 1 < B:
                                project(b + 1)
                        fills(layer, b)

        @block.vector
        def _(dve):
            v = nc.vector
            tt, ts, stt = v.tensor_tensor, v.tensor_scalar, v.scalar_tensor_tensor
            steps = [0]

            def link(ins):
                steps[0] += 1
                ins.then_inc(s_dve, 1)
                dve.wait_ge(s_dve, steps[0])

            powers, normed = [0], [0]

            def moments(src, eps):
                for t in range(T):
                    ins = v.bn_stats(stats[:, t, :], src[:, t, :])
                link(ins)
                for t in range(T):
                    ins = v.bn_aggr(mv[:, t, :], stats[:, t, :])
                link(ins)
                if powers[0]:
                    dve.wait_ge(s_rstd, powers[0])
                ts(ve[:, :], mv[:, :, 1], eps, None, ALU.add).then_inc(s_var, 1)
                powers[0] += 1

            def center(dst, src):
                dve.wait_ge(s_rstd, powers[0])
                for t in range(T):
                    ins = ts(dst[:, t, :], src[:, t, :], mv[:, t, 0:1], rstd[:, t:t + 1], ALU.subtract, ALU.mult)
                return ins

            def tiles(b):
                return x[:, T * b:T * b + T, :]

            def tail_sum(layer, b):
                if res_no[(layer, b)] or True:
                    if layer != "L0a":
                        dve.wait_ge(s_side_done, order[(layer, ("hout" if layer == "L1a" else "wo", b))] + 1)
                ins = tt(tiles(b), tiles(b), o_res[:, :, :], ALU.add)
                ins.then_inc(s_xadd, 1)
                dve.wait_ge(s_xadd, res_no[(layer, b)] + 1)

            def tail_moments(layer, b):
                moments(tiles(b), LN_EPS)

            def tail_center(layer, b):
                if normed[0]:
                    dve.wait_ge(s_side_full, tail_order[normed[0] - 1] + 1)
                normed[0] += 1
                center(xn, tiles(b)).then_inc(s_xn, 1)

            def largest_first(src, n, E, dst):
                gt = qz[:, 0:n * E * E].rearrange("p (n e j) -> p n e j", n=n, e=E)
                eq = kv[:, 0:n * E * E].rearrange("p (n e j) -> p n e j", n=n, e=E)
                vj = src.unsqueeze(2).broadcast_to([P, n, E, E])
                ve_ = src.unsqueeze(3).broadcast_to([P, n, E, E])
                tt(gt, vj, ve_, ALU.is_gt)
                link(tt(eq, vj, ve_, ALU.is_equal))
                link(tt(eq, eq, tri[:, 0:E, 0:E].unsqueeze(1).broadcast_to([P, n, E, E]), ALU.mult))
                link(tt(gt, gt, eq, ALU.add))
                link(v.tensor_reduce(dst, gt, AX.X, ALU.add))

            def over_e(col, E):
                return col.unsqueeze(2).broadcast_to([P, NT, E])

            def routing(layer):
                at, E = GATES[layer]
                g = lg[:, :, 0:E]
                wx = wexp[:, :, 0:E]
                rk = rank[:, 0:NT * E].rearrange("p (n e) -> p n e", n=NT)
                ra = r_a[:, 0:NT * E].rearrange("p (n e) -> p n e", n=NT)
                rb = r_b[:, 0:NT * E].rearrange("p (n e) -> p n e", n=NT)
                c0, c1, c2 = r_s[:, 0:16], r_s[:, 16:32], r_s[:, 32:48]
                dve.wait_ge(s_side_done, order[(layer, ("gate",))] + 1)
                if layer == "L0f":
                    dve.wait_ge(s_load["vec"], 48)
                    link(tt(g, g, wide_of("L0f_gb").unsqueeze(1).broadcast_to([P, NT, E]), ALU.add))
                    link(v.tensor_reduce(c0, g, AX.X, ALU.max))
                    largest_first(g, NT, E, rk)
                    link(tt(g, g, over_e(c0, E), ALU.subtract))
                    ts(rk, rk, 1.5, None, ALU.is_lt).then_inc(s_routing_in, 1)
                    dve.wait_ge(s_routing_exp, rout_no[layer])
                    dve.wait_ge(s_routing_in, 1)
                    link(tt(wx, wx, rk, ALU.mult))
                    link(v.tensor_reduce(c1, wx, AX.X, ALU.add))
                    link(v.reciprocal(c2, c1))
                    link(tt(wx, wx, over_e(c2, E), ALU.mult))
                elif layer == "L1f":
                    link(v.tensor_reduce(c0, g, AX.X, ALU.max))
                    tt(g, g, over_e(c0, E), ALU.subtract).then_inc(s_routing_in, 1)
                    dve.wait_ge(s_routing_exp, rout_no[layer])
                    link(v.tensor_reduce(c1, wx, AX.X, ALU.add))
                    link(v.reciprocal(c2, c1))
                    link(tt(wx, wx, over_e(c2, E), ALU.mult))
                    link(stt(wx, wx, FLT_MIN, wx, ALU.is_ge, ALU.mult))
                    largest_first(wx, NT, E, rk)
                    link(ts(g, rk, 1.5, None, ALU.is_lt))
                    tt(wx, wx, g, ALU.mult).then_inc(s_routing_in, 1)
                    dve.wait_ge(s_routing_in, rout_no[layer] + 1)
                elif layer == "L2f":
                    dve.wait_ge(s_routing_exp, rout_no[layer])
                    s_ = rb
                    link(tt(s_, wx, wide_of("L2f_bias").unsqueeze(1).broadcast_to([P, NT, E]), ALU.add))
                    quad = r_b[:, 0:256].rearrange("p (g e) -> p g e", e=4)
                    big, small = r_s[:, 0:128], r_s[:, 128:256]
                    pair = r_b[:, 0:256].rearrange("p (q i) -> p q i", i=2)
                    tt(big, pair[:, :, 0], pair[:, :, 1], ALU.max)
                    link(tt(small, pair[:, :, 0], pair[:, :, 1], ALU.add))
                    b2, s2 = (z.rearrange("p (g i) -> p g i", i=2) for z in (big, small))
                    gs = r_a[:, 0:64]
                    tt(r_a[:, 64:128], b2[:, :, 0], b2[:, :, 1], ALU.add)
                    link(tt(gs, s2[:, :, 0], s2[:, :, 1], ALU.max))
                    link(tt(gs, gs, r_a[:, 64:128], ALU.max))
                    gr = r_a[:, 128:192].rearrange("p (n e) -> p n e", n=NT)
                    largest_first(gs.rearrange("p (n e) -> p n e", n=NT), NT, 4, gr)
                    gm = r_a[:, 192:256]
                    link(ts(gm, r_a[:, 128:192], 1.5, None, ALU.is_lt))
                    msk = r_s[:, 0:256].bitcast(mybir.dt.int32)
                    link(v.tensor_copy(msk.rearrange("p (g e) -> p g e", e=4), gm.unsqueeze(2).broadcast_to([P, 64, 4])))
                    link(v.memset(rank, -1.0))
                    link(v.copy_predicated(rank, msk, r_b))
                    link(v.tensor_copy(r_b, rank))
                    largest_first(rb, NT, E, rk)
                    link(ts(rk, rk, 3.5, None, ALU.is_lt))
                    link(tt(wx, wx, rk, ALU.mult))
                    link(v.tensor_reduce(c0, wx, AX.X, ALU.add))
                    link(ts(c0, c0, 1e-20, None, ALU.add))
                    link(v.reciprocal(c1, c0))
                    link(ts(c1, c1, 2.5, None, ALU.mult))
                    link(tt(wx, wx, over_e(c1, E), ALU.mult))
                elif layer == "L3f":
                    link(v.memset(sk_col, 0.0))
                    link(ts(la, g, -1.0 / float(np.float32(SINK_EPS)), None, ALU.mult))
                    by_col = lambda z: z.rearrange("p n e -> p e n")
                    for it in range(SINK_ITERS):
                        link(v.tensor_reduce(sk_m[:, 0:16], la, AX.X, ALU.max))
                        tt(sk_d, la, over_e(sk_m[:, 0:16], E), ALU.subtract).then_inc(s_sk_in, 1)
                        dve.wait_ge(s_sk_act, 4 * it + 1)
                        v.tensor_reduce(sk_s[:, 0:16], sk_e, AX.X, ALU.add).then_inc(s_sk_in, 1)
                        dve.wait_ge(s_sk_act, 4 * it + 2)
                        link(tt(la, sk_d, over_e(sk_l[:, 0:16], E), ALU.subtract))
                        v.tensor_reduce(sk_col[:, 0:8], by_col(la), AX.X, ALU.max).then_inc(s_sk_v, 1)
                        dve.wait_ge(s_sk_pe, 2 * it + 1)
                        link(v.tensor_reduce(sk_m[:, 16:17], psO[0][:, 0:128], AX.X, ALU.max))
                        ts(sk_diag, ident[:, 0:8], sk_m[:, 16:17], None, ALU.mult).then_inc(s_sk_v, 1)
                        dve.wait_ge(s_sk_pe, 2 * it + 2)
                        tt(sk_d, la, psO[0][:, 0:8].unsqueeze(1).broadcast_to([P, NT, E]), ALU.subtract).then_inc(s_sk_in, 1)
                        dve.wait_ge(s_sk_act, 4 * it + 3)
                        v.tensor_reduce(sk_s[:, 16:24], by_col(sk_e), AX.X, ALU.add).then_inc(s_sk_v, 1)
                        dve.wait_ge(s_sk_act, 4 * it + 4)
                        ins = tt(la, sk_d, sk_l[:, 0:8].unsqueeze(1).broadcast_to([P, NT, E]), ALU.subtract)
                        if it < SINK_ITERS - 1:
                            link(ins)
                        else:
                            ins.then_inc(s_sk_in, 1)
                    dve.wait_ge(s_sk_act, 4 * SINK_ITERS + 1)
                    link(stt(sk_e, sk_e, FLT_MIN, sk_e, ALU.is_ge, ALU.mult))
                    largest_first(sk_e, NT, E, rk)
                    ts(ra, rk, 0.0, None, ALU.is_equal)
                    link(ts(rb, rk, 1.0, None, ALU.is_equal))
                    tt(ra, ra, sk_e[:, :, 0:1].broadcast_to([P, NT, E]), ALU.mult)
                    link(tt(rb, rb, sk_e[:, :, 1:2].broadcast_to([P, NT, E]), ALU.mult))
                    link(tt(wx, ra, rb, ALU.add))

            def find_nan():
                all_done(dve, "L2x")
                dve.wait_ge(s_scaled, scaled_no["L2x"])
                dve.wait_ge(s_load["ctx"], 16)
                link(v.memset(nanf[:, :], 0.0))
                v.tensor_reduce(nanf[:, 0:1], xT("L2x"), AX.X, ALU.add)
                v.tensor_reduce(nanf[0:CD, 1:2], ctxT[:, :], AX.X, ALU.add)
                v.tensor_reduce(nanf[:, 2:3], w("L2x", "wq"), AX.X, ALU.add)
                v.tensor_reduce(nanf[0:CD, 3:4], w("L2x", "wk"), AX.X, ALU.add)
                at = COLS["L2x_bq"]
                link(v.tensor_reduce(nanf[:, 6:7], cols[:, at:at + 2], AX.X, ALU.add))
                link(tt(nanf[:, 3:4], nanf[:, 3:4], nanf[:, 6:7], ALU.add))
                v.tensor_reduce(nanf[:, 4:5], nanf[:, 0:4], AX.X, ALU.add).then_inc(s_nansum, 1)
                dve.wait_ge(s_side_done, order[("L2x", ("nan",))] + 1)
                link(tt(nanmask[:, :], nanf[:, 5:6], nanf[:, 5:6], ALU.not_equal))

            def spread_relative():
                dve.wait_ge(s_side_done, order[("L0a", ("rel", 1))] + 1)
                for t in range(T):
                    for half in range(2):
                        r = 2 * t + half
                        if r >= 2:
                            dve.wait_ge(s_side_full, order[("L0a", ("relout", t - 1, half))] + 1)
                        for kt in range(2):
                            first = relT[:, kt, 0:1]
                            src = bass.AP(tensor=first.tensor, offset=first.offset + 255 - 8 * t - 128 * half,
                                          ap=[list(first.ap[0]), [-16, 8], [-1, 8], [16, 16]])
                            ins = v.tensor_copy(rel_bias(r, kt).rearrange("p (h m n) -> p h m n", h=8, m=8), src)
                        ins.then_inc(s_relbias, 1)

            def attention(layer):
                a = ATT[layer]
                dh, U, K, g0, size = a["dh"], a["H"], a["keys"], unit0[layer], a["group"]
                NU = B * U
                if layer == "L0a":
                    spread_relative()
                if layer == "L2x":
                    find_nan()

                def maxima(u):
                    g = g0 + u
                    bank = psS[g % 2][:, 0:2 * K]
                    dve.wait_ge(s_qk, g + 1)
                    if layer == "L2x":
                        if g >= 2:
                            dve.wait_ge(s_exp, g - 1)
                        link(ts(clamped[:, g % 2, :], bank, CLAMP, -CLAMP, ALU.min, ALU.max))
                        bank = clamped[:, g % 2, :]
                    v.tensor_reduce(negmax[:, g % 2, :], bank.rearrange("p (h k) -> p h k", h=2), AX.X, ALU.max,
                                    negate=True).then_inc(s_max, 1)

                def copy_turned(u):
                    g = g0 + u
                    dve.wait_ge(s_tr, g + 1)
                    if g >= 2:
                        dve.wait_ge(s_pv, g - 1)
                    v.tensor_copy(probT[:, g % 2, :], psT[g % 2][:, :]).then_inc(s_ptc, 1)

                def normalize(gi):
                    gg = group0[layer] + gi
                    b, u0 = gi * size // U, gi * size % U
                    dve.wait_ge(s_pv, g0 + size * (gi + 1))
                    if gi >= 2 and layer != "L0a":
                        dve.wait_ge(s_side_full, order[(layer, ("ot", (gi - 2) * size // U, (gi - 2) % (U // size)))] + 1)
                    nh = 2 * size
                    link(v.reciprocal(rrec[:, 0:nh], rsum[:, b % 2, 2 * u0:2 * u0 + nh]))
                    if dh == 64:
                        tt(o_sb[:, gi % 2, :].rearrange("p (s d) -> p s d", d=64),
                           psO[gg % 2][:, :].rearrange("p (s d) -> p s d", d=64),
                           rrec[:, 0:nh].unsqueeze(2).broadcast_to([P, nh, 64]), ALU.mult).then_inc(s_norm, 1)
                    else:
                        for t in range(T):
                            num = psO[gg % 2][:, 0:256].rearrange("p (u t h d) -> p t u h d", t=T, h=2, d=8)[:, t]
                            rec = rrec[:, 0:nh].rearrange("p (u t h) -> p t u h", t=T, h=2)[:, t]
                            ins = tt(o_sb[:, gi % 2, P * t:P * t + P].rearrange("p (u h d) -> p u h d", h=2, d=8),
                                     num, rec.unsqueeze(3).broadcast_to([P, 8, 2, 8]), ALU.mult)
                        if layer == "L2x":
                            link(ins)
                            dve.wait_ge(s_side_done, order[(layer, ("vmean", b))] + 1)
                            for t in range(T):
                                ins = v.copy_predicated(o_sb[:, gi % 2, P * t:P * t + P], nanmask[:, :].broadcast_to([P, P]),
                                                        v_sb[:, 1024 + 128 * (b % 2):1152 + 128 * (b % 2)])
                        ins.then_inc(s_norm, 1)

                def add_relative(b):
                    dve.wait_ge(s_norm, group0[layer] + b + 1)
                    if b == 0:
                        dve.wait_ge(s_side_done, order[(layer, ("relout", 1, 1))] + 1)
                        dve.wait_ge(s_load["vec"], 48)
                    for t in range(T):
                        o = o_sb[:, b % 2, P * t:P * t + P].rearrange("p (h d) -> p h d", d=8)
                        ins = tt(o, o, rel_out[:, t, :, b, :], ALU.add)
                    link(ins)
                    moments(o_sb[:, b % 2, 0:256].rearrange("p (t d) -> p t d", t=T), 1e-3)

                def inner_norm(b):
                    link(center(o_res, o_sb[:, b % 2, 0:256].rearrange("p (t d) -> p t d", t=T)))
                    link(tt(o_res[:, :, :], o_res[:, :, :], wide_of("gamma").unsqueeze(1).broadcast_to([P, T, D]), ALU.mult))
                    link(tt(o_res[:, :, :], o_res[:, :, :], wide_of("beta").unsqueeze(1).broadcast_to([P, T, D]), ALU.add))

                for s in range(-1, NU + 13):
                    if s + 1 < NU:
                        maxima(s + 1)
                    if 0 <= s < NU:
                        copy_turned(s)
                    if dh == 64 and s >= 5 and (s - 5) % 4 == 0 and (s - 5) // 4 < NU // 4:
                        normalize((s - 5) // 4)
                    if dh == 8 and s > U and (s - 1) % U == 0 and (s - 1) // U - 1 < B:
                        normalize((s - 1) // U - 1)
                    for b in range(B):
                        if layer == "L0a" and s == (b + 1) * U + 2:
                            add_relative(b)
                        if s == (b + 1) * U + 7:
                            if layer == "L0a":
                                inner_norm(b)
                            tail_sum(layer, b)
                            tail_moments(layer, b)
                        if s == (b + 1) * U + 9 and layer != last_block:
                            tail_center(layer, b)

            def experts(layer):
                f = FFN[layer]
                E, glu = len(f["chunks"]), f["glu"]
                NE = B * E
                hop = hop0[layer]
                for n in range(-1, NE + 4):
                    if n + 1 < NE and glu:
                        g = exp0[layer] + n + 1
                        if g >= 2:
                            dve.wait_ge(s_down, g - 1)
                        for c in range(f["chunks"][(n + 1) % E]):
                            dve.wait_ge(s_sg, hop + 1 - glu_hop0)
                            tt(hT[:, g % 2, c, :], sg[:, hop % 2, :], psH[hop % 4][:, 256:512], ALU.mult).then_inc(s_hop, 1)
                            hop += 1
                    m = n - 1
                    if 0 <= m < NE:
                        b, e, g = m // E, m % E, exp0[layer] + m
                        dve.wait_ge(s_down, g + 1)
                        if g:
                            dve.wait_ge(s_acc, g)
                        for t in range(T):
                            o, xt = psO[g % 2][:, P * t:P * t + P], x[:, T * b + t, :]
                            if layer == "L2f" and e == E - 1:
                                ins = tt(xt, o, xt, ALU.add)
                            else:
                                ins = stt(xt, o, wexp[:, T * b + t, e:e + 1], xt, ALU.mult, ALU.add)
                        ins.then_inc(s_acc, 1)
                        if e == E - 1 and layer != "L3f":
                            dve.wait_ge(s_acc, g + 1)
                            tail_moments(layer, b)
                    m = n - 2
                    if 0 <= m < NE and m % E == E - 1 and layer != last_block:
                        tail_center(layer, m // E)

            dve.wait_ge(s_load["x"], 16)
            for b in range(B):
                tail_moments("init", b)
                tail_center("init", b)
            dve.wait_ge(s_const, 11)
            for layer in LAYERS:
                if layer in ATT:
                    attention(layer)
                elif layer in FFN:
                    routing(layer)
                    glu_hop0 = glu_first.get(layer, 0)
                    experts(layer)
                elif layer == "L1a":
                    for b in range(B):
                        dve.wait_ge(s_ga, b + 1)
                        if b == 0:
                            tt(c_state, gates[:, 0, :], gates[:, 3, :], ALU.mult).then_inc(s_c, 1)
                        else:
                            tt(c_in, gates[:, 0, :], gates[:, 3, :], ALU.mult)
                            link(tt(c_state, gates[:, 1, :], c_state, ALU.mult))
                            tt(c_state, c_state, c_in, ALU.add).then_inc(s_c, 1)
                        dve.wait_ge(s_tc, b + 1)
                        if b >= 2:
                            dve.wait_ge(s_side_full, order[(layer, ("hout", b - 2))] + 1)
                        tt(h_state(b), gates[:, 2, :], tanh_c, ALU.mult).then_inc(s_h, 1)
                        tail_sum(layer, b)
                        tail_moments(layer, b)
                        if layer != last_block:
                            tail_center(layer, b)
                elif layer == "L1f":
                    routing(layer)

                    def scale_x(n):
                        b = n // 8
                        dve.wait_ge(s_bc, n + 1)
                        if n >= 2:
                            dve.wait_ge(s_a1, n - 1)
                        tt(prob[:, n % 2, 0:256], xT(layer)[:, S * b:S * b + S], psS[n % 2][:, 0:256],
                           ALU.mult).then_inc(s_xs, 1)

                    def join(n):
                        b, e = n // 8, n % 8
                        dve.wait_ge(s_x23, n + 1)
                        if n >= 2:
                            dve.wait_ge(s_pacc, n - 1)
                        b3 = wide_of("L1f_b3")[:, P * e:P * e + P]
                        for t in range(T):
                            ins = stt(prob[:, n % 2, 256 + P * t:256 + P * t + P], psO[n % 2][:, P * t:P * t + P],
                                      wexp[:, T * b + t, e:e + 1], b3, ALU.mult, ALU.add)
                        link(ins)
                        for t in range(T):
                            ins = stt(o_sb[:, n % 2, P * t:P * t + P], psO[n % 2][:, 256 + P * t:256 + P * t + P],
                                      lg[:, T * b + t, e:e + 1], prob[:, n % 2, 256 + P * t:256 + P * t + P],
                                      ALU.mult, ALU.mult)
                        ins.then_inc(s_t23, 1)

                    scale_x(0)
                    scale_x(1)
                    for b in range(B):
                        for e in range(8):
                            n = 8 * b + e
                            if e < 6:
                                scale_x(n + 2)
                            join(n)
                            if e == 3 and b and layer != last_block:
                                pass
                        for c in range(2):
                            dve.wait_ge(s_shs, 2 * b + c + 1)
                            tt(hT[:, c, 3, :], sg[:, c, :], psS[c][:, 256:512], ALU.mult).then_inc(s_shh, 1)
                        if b + 1 < B:
                            scale_x(8 * b + 8)
                            scale_x(8 * b + 9)
                        dve.wait_ge(s_shd, b + 1)
                        dve.wait_ge(s_pacc, 8 * b + 8)
                        tt(tiles(b), psO[0][:, 0:256].rearrange("p (t d) -> p t d", t=T), tiles(b), ALU.add).then_inc(s_sho, 1)
                        dve.wait_ge(s_sho, b + 1)
                        tail_moments(layer, b)
                        if layer != last_block:
                            tail_center(layer, b)
                elif layer == "L3a":
                    link(v.memset(va3[:, :, 128:130], 1.0))
                    groups = lambda z: z.rearrange("p (g e) -> p g e", e=8)
                    for b in range(B):
                        for t in range(T):
                            n = T * b + t
                            dve.wait_ge(s_qkv, n + 1)
                            if b:
                                dve.wait_ge(s_ctx3, b)
                                dve.wait_ge(s_side_full, order[(layer, ("qT", b - 1))] + 1)
                            link(v.tensor_reduce(rrec[:, :], groups(psS[t][:, 0:256]), AX.X, ALU.max))
                            tt(groups(qk3[:, t, :]), groups(psS[t][:, 0:256]),
                               rrec[:, :].unsqueeze(2).broadcast_to([P, 32, 8]), ALU.subtract).then_inc(s_sub, 1)
                            dve.wait_ge(s_ex3, n + 1)
                            link(v.tensor_reduce(rrec[:, :], groups(qk3[:, t, :]), AX.X, ALU.add))
                            link(v.reciprocal(rsum[:, 0, :], rrec[:, :]))
                            tt(groups(qk3[:, t, :]), groups(qk3[:, t, :]),
                               rsum[:, 0, :].unsqueeze(2).broadcast_to([P, 32, 8]), ALU.mult).then_inc(s_sm3, 1)
                        dve.wait_ge(s_ctx3, b + 1)
                        ctx_ps = psT[0]
                        tt(groups(cm3[:, 0:128]), groups(ctx_ps[:, 0:128]), hmask[:, :].unsqueeze(2).broadcast_to([P, 16, 8]),
                           ALU.mult)
                        ts(cm3[:, 128:144], hmask[:, :], ctx_ps[:, 128:129], None, ALU.mult).then_inc(s_cm3, 1)
                        dve.wait_ge(s_num3, b + 1)
                        for t in range(T):
                            o = psT[1][:, 144 * t:144 * t + 144]
                            link(v.reciprocal(rrec[:, 0:16], o[:, 128:144]))
                            link(tt(groups(ol3[:, t, :]), groups(o[:, 0:128]),
                                    rrec[:, 0:16].unsqueeze(2).broadcast_to([P, 16, 8]), ALU.mult))
                            ins = tt(ol3[:, t, :], ol3[:, t, :], qk3[:, t, 0:128], ALU.add)
                        ins.then_inc(s_ol3, 1)
                        tail_sum(layer, b)
                        tail_moments(layer, b)
                        if layer != last_block:
                            tail_center(layer, b)


_IN = {}


def kernel(**a):
    import concourse.bacc as bacc
    from concourse.bass_utils import run_bass_kernel_spmd

    a = {k: np.asarray(z) for k, z in a.items()}
    f = {"x": a["x"].reshape(TOK, D), "ctxT": a["ctx_768"].reshape(TOK, CD).T, "rel": a["L0_attn_rel_table"]}

    def chunked(m):
        return m.reshape(-1, P, m.shape[-1]).transpose(1, 0, 2).reshape(P, -1)

    def by_expert(m):
        return m.transpose(1, 0, 2).reshape(m.shape[1], -1)

    for n in ("q", "k", "v"):
        f["L0a_w" + n] = a["L0_attn_W" + n]
        f["L2a_w" + n] = a["L2_attn_W" + n].T
        f["L0x_w" + n] = a["L0_xattn_W" + n]
        f["L1x_w" + n] = a["L1_xattn_W" + n]
        f["L2x_w" + n] = a["L2_xattn_W" + n]
        f["L3x_w" + n] = a["L3_xattn_w_" + n]
    f["L0x_wo"] = chunked(a["L0_xattn_Wo"])
    f["L1x_wo"] = chunked(a["L1_xattn_Wout"])
    f["L3x_wo"] = chunked(a["L3_xattn_w_o"])
    f["L2a_wo"] = a["L2_attn_Wo"].T
    f["L2x_wo"] = a["L2_xattn_Wo"]
    f["L1a_w"], f["L1a_u"] = a["L1_attn_w"], a["L1_attn_u"]
    f["L0f_up"] = by_expert(a["L0_ffn_w1"])
    f["L0f_down"] = chunked(a["L0_ffn_w2"].reshape(-1, D))
    for n in ("1", "2", "3"):
        f["L1f_w" + n] = by_expert(a["L1_ffn_w" + n].transpose(0, 2, 1))
    f["L1f_sg"], f["L1f_su"] = a["L1_ffn_sw1"].T, a["L1_ffn_sw2"].T
    f["L1f_sd"] = chunked(a["L1_ffn_sw3"].T)
    for n in ("gate", "up"):
        f["L2f_" + n] = np.concatenate([by_expert(a[f"L2_ffn_{n}_w"]), a[f"L2_ffn_sh_{n}_w"]], 1)
        f["L3f_" + n] = by_expert(a["L3_ffn_W_" + n].transpose(0, 2, 1))
    f["L2f_down"] = np.concatenate([by_expert(a["L2_ffn_down_w"]), chunked(a["L2_ffn_sh_down_w"])], 1)
    f["L3f_down"] = chunked(a["L3_ffn_W_down"].transpose(0, 2, 1).reshape(-1, D))
    f["L3a_wqkv"] = np.concatenate([a["L3_attn_W" + n].T for n in "qkv"], 1)
    f["L3a_wp"] = a["L3_attn_Wp"].T
    f["gw"] = np.concatenate([a["L0_ffn_gate_w"].T, a["L1_ffn_gate_w"].T, a["L2_ffn_router_w"].T, a["L3_ffn_gate_W"].T], 1)
    f["rows"] = np.concatenate([a["L0_xattn_bo"], a["L1_xattn_bout"], a["L2_attn_bo"], a["L2_xattn_bv"], a["L2_xattn_bo"],
                                a["L3_attn_bq"], a["L3_attn_bk"], a["L3_attn_bv"], a["L3_attn_bp"], a["L3_xattn_b_o"],
                                a["L0_ffn_b2"].reshape(-1), a["L1_ffn_b2"].reshape(-1)])[None]
    f["wide"] = np.concatenate([a["L0_attn_gamma"], a["L0_attn_beta"], a["L0_ffn_gate_b"], a["L2_ffn_bias"],
                                a["L1_ffn_b3"].reshape(-1)])[None]
    f["cols"] = np.concatenate([a["L0_ffn_b1"].reshape(-1, P).T, a["L1_attn_bias"].reshape(4, P).T, a["L1_ffn_b1"].T,
                                a["L2_xattn_bq"][:, None], a["L2_xattn_bk"][:, None]], 1)

    nc = bacc.Bacc("TRN2", target_bir_lowering=False, num_devices=1)
    arrays, d = {}, {}
    for name, z in f.items():
        z = np.ascontiguousarray(z)
        arrays["in_" + name] = z
        d[name] = nc.dram_tensor("in_" + name, z.shape, mybir.dt.from_np(z.dtype), kind="ExternalInput").ap()
    d["rel_ext"] = nc.dram_tensor("rel_ext", (528, 16), F32, kind="Internal").ap()
    out = nc.dram_tensor("out", (TOK, D), F32, kind="ExternalOutput").ap()
    build(nc, d, out)
    r = run_bass_kernel_spmd(nc, [arrays], core_ids=[0])
    return r.results[0]["out"].reshape(B, S, D)
```

```python
from contextlib import ExitStack

import numpy as np
import concourse.bass as bass
from concourse import mybir

F32 = mybir.dt.float32
BF16 = mybir.dt.bfloat16
F16 = mybir.dt.float16
ALU = mybir.AluOpType
ACT = mybir.ActivationFunctionType
AX = mybir.AxisListType

P = 128
B, S, D, CD = 8, 256, 128, 96
T = S // P
NT = B * T
TOK = B * S
LN_EPS = 1e-5
REL_ROWS = 255
MASKED = -1e30
SINK_ITERS, SINK_EPS = 20, 0.05
CLAMP = 10000.0
FLT_MIN = float(np.finfo(np.float32).tiny)

ATT = {
    "L0a": dict(H=16, dh=8, keys=256, group=8, scale=float(D) ** -0.5),
    "L0x": dict(H=16, dh=64, keys=256, group=4, scale=0.125),
    "L1x": dict(H=8, dh=64, keys=256, group=4, scale=0.125),
    "L2a": dict(H=16, dh=8, keys=192, group=8, scale=float(1.0 / np.float32(np.sqrt(8)))),
    "L2x": dict(H=16, dh=8, keys=256, group=8, scale=8.0 ** -0.5),
    "L3x": dict(H=16, dh=64, keys=256, group=4, scale=0.125),
}
FFN = {
    "L0f": dict(chunks=[4] * 8, glu=False, ahead=1),
    "L2f": dict(chunks=[1] * 16 + [2], glu=True, ahead=2),
    "L3f": dict(chunks=[4] * 8, glu=True, ahead=1),
}
LAYERS = ["L0a", "L0x", "L0f", "L1a", "L1x", "L1f", "L2a", "L2x", "L2f", "L3a", "L3x", "L3f"]
HALO = 32
PADS = S + 2 * HALO

ROWS = {}
_at = 0
for _n, _w in [("L0x_bo", 128), ("L1x_bo", 128), ("L2a_bo", 128), ("L2x_bv", 128), ("L2x_bo", 128),
               ("L3a_bqkv", 384), ("L3a_bp", 128), ("L3x_bo", 128), ("L0f_b2", 1024), ("L1f_b2", 1024)]:
    ROWS[_n] = _at
    _at += _w
ROWS_W = _at
WIDE = {}
_at = 0
for _n, _w in [("gamma", 128), ("beta", 128), ("L0f_gb", 8), ("L2f_bias", 16), ("L1f_b3", 1024)]:
    WIDE[_n] = (_at, _w)
    _at += _w
WIDE_W = _at
COLS = {}
_at = 0
for _n, _w in [("L0f_b1", 32), ("L1a_b", 4), ("L1f_b1", 8), ("L2x_bq", 1), ("L2x_bk", 1)]:
    COLS[_n] = _at
    _at += _w
COLS_W = _at

WEIGHTS = {}


def _place(layer, region, parts):
    at = 0
    for name, cols, rows in parts:
        WEIGHTS[f"{layer}_{name}"] = (region, at, cols, rows)
        at += cols


_place("L0a", "wL0a", [("wq", 128, 128), ("wk", 128, 128), ("wv", 128, 128)])
_place("L1a", "wL1a", [("w", 512, 128), ("u", 512, 128)])
_place("L2a", "wL2a", [("wq", 128, 128), ("wk", 128, 128), ("wv", 128, 128), ("wo", 128, 128)])
_place("L2x", "wL2x", [("wq", 128, 128), ("wk", 128, CD), ("wv", 128, CD), ("wo", 128, 128)])
_place("L3a", "wL3a", [("wqkv", 384, 128), ("wp", 128, 128)])
_place("L1x", "wL1x", [("wq", 512, 128), ("wk", 512, CD), ("wv", 512, CD), ("wo", 512, 128)])
for _l in ("L0x", "L3x"):
    _place(_l, "wB", [("wq", 1024, 128), ("wk", 1024, CD), ("wv", 1024, CD), ("wo", 1024, 128)])
_place("L1f", "wB", [("w1", 1024, 128), ("w2", 1024, 128), ("w3", 1024, 128),
                     ("sg", 256, 128), ("su", 256, 128), ("sd", 256, 128)])
_place("L0f", "wA", [("up", 4096, 128), ("down", 4096, 128)])
_place("L2f", "wA", [("gate", 2304, 128), ("up", 2304, 128), ("down", 2304, 128)])
_place("L3f", "wA", [("gate", 4096, 128), ("up", 4096, 128), ("down", 4096, 128)])
GATES = {"L0f": (0, 8), "L1f": (8, 8), "L2f": (16, 16), "L3f": (32, 8)}
REGION_W = {"wL0a": 384, "wL1a": 1024, "wL2a": 512, "wL2x": 512, "wL3a": 512, "wL1x": 2048,
            "wB": 4096, "wA": 12288}
FREED_BY = {"L1f": "L0x", "L3x": "L1f", "L2f": "L0f", "L3f": "L2f"}


def side_schedule():
    sched = {}

    def put(layer, step, item):
        if item[0] == "tail" and layer == LAYERS[-1]:
            return
        sched.setdefault((layer, step), []).append(item)

    for b in range(B):
        put("init", b, ("tail", b))
    for layer in LAYERS:
        if layer in ATT:
            a = ATT[layer]
            U = a["H"]
            if layer == "L2x":
                put(layer, -3, ("nan",))
            for b in range(B):
                if a["dh"] == 64:
                    for p in range(a["H"] // 2):
                        at = -3 if b == 0 else (b - 1) * U + 2 * p + 3
                        put(layer, at, ("qk", b, p))
                        put(layer, at, ("v", b, p))
                    for i in range(U // a["group"]):
                        put(layer, b * U + 4 * i + 8, ("ot", b, i))
                    put(layer, (b + 1) * U + 6, ("wo", b))
                else:
                    at = -3 if b == 0 else (b - 1) * U + 4
                    if layer == "L2a":
                        put(layer, at, ("q", b))
                        put(layer, at, ("k", b))
                    else:
                        put(layer, at, ("qk", b))
                    if layer == "L0a":
                        put(layer, -4, ("v", b))
                    else:
                        put(layer, at, ("v", b))
                        if layer == "L2x":
                            put(layer, at, ("vmean", b))
                        put(layer, (b + 1) * U + 4, ("ot", b, 0))
                        put(layer, (b + 1) * U + 6, ("wo", b))
                put(layer, (b + 1) * U + 12, ("tail", b))
            if layer == "L0a":
                for kt in range(2):
                    put(layer, -5, ("rel", kt))
                for t in range(T):
                    for half in range(2):
                        put(layer, -3, ("relout", t, half))
        elif layer in FFN:
            put(layer, -2, ("gate",))
            E = len(FFN[layer]["chunks"])
            for b in range(B):
                put(layer, (b + 1) * E + 3, ("tail", b))
        elif layer == "L1f":
            put(layer, -2, ("gate",))
            for b in range(B):
                put(layer, (b + 1) * 9 + 2, ("tail", b))
        elif layer == "L1a":
            for b in range(B):
                put(layer, b, ("hout", b))
                put(layer, b + 1, ("tail", b))
        elif layer == "L3a":
            for b in range(B):
                put(layer, b, ("qT", b))
                put(layer, b, ("ot", b, 0))
                put(layer, b, ("wo", b))
                put(layer, b + 2, ("tail", b))
    order = {}
    n = 0
    for layer in ["init"] + LAYERS:
        for step in sorted(s for (l, s) in sched if l == layer):
            for item in sched[(layer, step)]:
                order[(layer, item)] = n
                n += 1
    return sched, order


def build(nc, d, out):
    sched, order = side_schedule()
    last_block = LAYERS[-1]

    def before(layer):
        i = LAYERS.index(layer)
        return "init" if i == 0 else LAYERS[i - 1]

    unit0, group0, n_unit, n_group = {}, {}, 0, 0
    hop0, exp0, n_hop, n_exp = {}, {}, 0, 0
    for l in LAYERS:
        if l in ATT:
            unit0[l], group0[l] = n_unit, n_group
            n_unit += B * ATT[l]["H"]
            n_group += B * ATT[l]["H"] // ATT[l]["group"]
        if l in FFN:
            per = sum(c if FFN[l]["glu"] else c // 2 for c in FFN[l]["chunks"])
            hop0[l], exp0[l] = n_hop, n_exp
            n_hop += B * per
            n_exp += B * len(FFN[l]["chunks"])

    vno = {k: i for i, k in enumerate(sorted((k for k in order if k[1][0] == "v"), key=order.get))}
    glu_first, n_glu = {}, 0
    for l in LAYERS:
        if l in FFN and FFN[l]["glu"]:
            glu_first[l] = hop0[l] - n_glu
            n_glu += B * sum(FFN[l]["chunks"])
    N_VAR = B * (1 + len([l for l in LAYERS if l != "L3f"]) + ("L0a" in LAYERS))
    PER_VAR = 2 if last_block == "L0a" else 1
    tail_order = [order[k] for k in sorted((k for k in order if k[1][0] == "tail"), key=order.get)]
    zero_no, qz_no, scaled_no, rout_no, res_no = {}, {}, {}, {}, {}
    for l in LAYERS:
        if l in ATT:
            zero_no[l] = 1 + sum(1 for m in zero_no if ATT[m]["dh"] == 64)
            qz_no[l] = sum(1 for m in qz_no if ATT[m]["dh"] == 8)
            scaled_no[l] = len(scaled_no) + 1 + ("L2x" in scaled_no or l == "L2x")
        if l in GATES:
            rout_no[l] = len(rout_no) + 1
        if l in ATT or l in ("L1a", "L3a"):
            for b in range(B):
                res_no[(l, b)] = len(res_no)

    with ExitStack() as ctx:
        def sb(name, shape, dt=F32):
            return ctx.enter_context(nc.sbuf_tensor(name, shape, dt))

        def sem(name):
            return ctx.enter_context(nc.semaphore(name))

        psS = [ctx.enter_context(nc.psum_tensor(f"psS{i}", [P, 512], F32)) for i in range(2)]
        psT = [ctx.enter_context(nc.psum_tensor(f"psT{i}", [P, 512], F32)) for i in range(2)]
        psO = [ctx.enter_context(nc.psum_tensor(f"psO{i}", [P, 512], F32)) for i in range(2)]
        psM = [ctx.enter_context(nc.psum_tensor(f"psM{i}", [P, 512], F32)) for i in range(2)]
        psH = [psS[0], psS[1], psT[0], psT[1]]

        x = sb("x", [P, NT, D])
        xTs = sb("xTs", [P, 2, TOK])
        ctxT = sb("ctxT", [CD, TOK])
        qz = sb("qz", [P, 4096])
        kv = sb("kv", [P, 4096])
        prob = sb("prob", [P, 2, 512])
        probT = sb("probT", [P, 2, 512])
        o_sb = sb("o_sb", [P, 2, 512])
        oT = sb("oT", [P, 2048])
        o_res = sb("o_res", [P, T, D])
        hT = sb("hT", [P, 2, 4, 256])
        sg = sb("sg", [P, 2, 256])
        W = {r: sb(r, [P, w]) for r, w in REGION_W.items()}
        gw = sb("gw", [P, 40])
        bias_parts = sb("bias_parts", [P, ROWS_W], BF16)
        bias_raw = W["wA"][:, REGION_W["wA"] - 4096:REGION_W["wA"] - 4096 + ROWS_W]
        wide = sb("wide", [P, WIDE_W])
        cols = sb("cols", [P, COLS_W])
        ident = sb("ident", [P, P])
        ones = sb("ones", [P, P])
        onesb = sb("onesb", [P, P], BF16)
        identb = sb("identb", [P, P], BF16)
        band = sb("band", [P, 2, 192], BF16)
        relT = o_sb
        hmask = sb("hmask", [P, 16])
        inv_keys = sb("inv_keys", [P, P])
        nanmask = sb("nanmask", [P, 1], mybir.dt.int32)
        tri = sb("tri", [P, 16, 16])
        mhalf = sb("mhalf", [P, 2])
        negmax = sb("negmax", [P, 2, 2])
        rsum = sb("rsum", [P, 2, 32])
        rrec = sb("rrec", [P, 32])
        stats = sb("stats", [P, T, 6])
        mv = sb("mv", [P, T, 2])
        ve = sb("ve", [P, T])
        rstd = sb("rstd", [P, T])
        xn = sb("xn", [P, T, D])
        lg = sb("lg", [P, NT, 16])
        wexp = sb("wexp", [P, NT, 16])
        nanf = sb("nanf", [P, 8])
        rel_rows = hT[:, 0, :, :]
        v_all = hT[:, :, :, :].rearrange("p a c n -> p (a c n)").rearrange("p (b k n) -> p b k n", b=B, k=2)
        rel_out = oT[:, :].rearrange("p (t h b d) -> p t h b d", t=T, h=16, b=B)
        k_sb, v_sb = kv[:, 0:2048], kv[:, 2048:4096]
        xpad = hT[:, :, :, :].rearrange("p a c n -> p (a c n)")[:, 0:2 * PADS].rearrange("p (a n) -> p a n", a=2)
        clamped = hT[:, :, 0:2, :].rearrange("p a c n -> p a (c n)")
        gates = qz[:, 0:1024].rearrange("p (i n) -> p i n", i=4)
        c_state, tanh_c, c_in = qz[:, 1024:1280], qz[:, 1280:1536], qz[:, 2048:2304]
        qk3s = qz[:, 0:1024].rearrange("p (s t n) -> p s t n", s=2, t=T)
        va3s = qz[:, 1024:1544].rearrange("p (s t n) -> p s t n", s=2, t=T)
        cm3 = qz[:, 1600:1744]
        ol3 = qz[:, 2048:2304].rearrange("p (t n) -> p t n", t=T)
        la, sk_d, sk_e = (prob[:, 0, 128 * i:128 * i + 128].rearrange("p (n e) -> p n e", e=8) for i in range(3))
        sk_s, sk_l, sk_m = (prob[:, 1, 32 * i:32 * i + 32] for i in range(3))
        sk_col, sk_diag = prob[:, 1, 128:256], prob[:, 1, 256:264]
        rank, r_a, r_b = (probT[:, :, :].rearrange("p a n -> p (a n)")[:, 256 * i:256 * i + 256] for i in range(3))
        r_s = probT[:, 1, 256:512]

        v_parts = [v_sb[:, 0:1024].bitcast(BF16), v_sb[:, 1024:2048].bitcast(BF16),
                   hT[:, 0, :, :].rearrange("p c n -> p (c n)").bitcast(BF16)]

        def v_raw(layer, b, p=0):
            if layer == "L0a":
                return v_all[:, b, :, :].rearrange("p k n -> p (k n)")
            if layer == "L2a":
                return v_sb[:, 0:512]
            if layer == "L2x":
                return v_sb[:, 512 * (b % 2):512 * (b % 2) + 256]
            return hT[:, 1, vno[(layer, ("v", b, p))] % 2, :]

        def v_small(layer, b):
            n, at = (768, 512) if layer == "L2a" else (384, 1280)
            at += n * (b % 2)
            return v_sb[:, at:at + n].bitcast(BF16).rearrange("p (x c d) -> p x c d", c=3, d=8)

        def turned(g, lo):
            return probT[:, g % 2, 256 * lo:256 * lo + 256].bitcast(F16)

        def q_small(b):
            return k_sb[:, 640 + 256 * (b % 2):896 + 256 * (b % 2)]

        def k_of(layer, b):
            return k_sb[:, PADS * (b % 2):PADS * (b % 2) + (PADS if layer == "L2a" else S)]

        def rel_bias(r, kt):
            return qz[:, 2048 * (r % 2) + 1024 * kt:2048 * (r % 2) + 1024 * kt + 1024]

        def h_state(b):
            return qz[:, 1536 + 256 * (b % 2):1792 + 256 * (b % 2)]

        s_load = {n: sem(f"s_load_{n}") for n in ["x", "ctx", "vec", "bias", "rel", "gw"] + LAYERS}
        s_relbias = sem("s_relbias")
        s_rel_ext = sem("s_rel_ext")
        s_const = sem("s_const")
        s_bias_zero = sem("s_bias_zero")
        s_bias_split = sem("s_bias_split")
        s_scaled = sem("s_scaled")
        s_qzero = sem("s_qzero")
        s_side_full = sem("s_side_full")
        s_side_done = sem("s_side_done")
        s_qk = sem("s_qk")
        s_max = sem("s_max")
        s_exp = sem("s_exp")
        s_tr = sem("s_tr")
        s_pthi = sem("s_pthi")
        s_ptc = sem("s_ptc")
        s_vsplit = sem("s_vsplit")
        s_split_step = sem("s_split_step")
        s_pv = sem("s_pv")
        s_norm = sem("s_norm")
        s_qz = sem("s_qz")
        s_xpad = sem("s_xpad")
        s_var = sem("s_var")
        s_rstd = sem("s_rstd")
        s_xn = sem("s_xn")
        s_hfull = sem("s_hfull")
        s_sg = sem("s_sg")
        s_hop = sem("s_hop")
        s_down = sem("s_down")
        s_acc = sem("s_acc")
        s_dve = sem("s_dve")
        s_bc = sem("s_bc")
        s_xs = sem("s_xs")
        s_a1 = sem("s_a1")
        s_h1 = sem("s_h1")
        s_x23 = sem("s_x23")
        s_t23 = sem("s_t23")
        s_shg = sem("s_shg")
        s_shs = sem("s_shs")
        s_shh = sem("s_shh")
        s_shd = sem("s_shd")
        s_sho = sem("s_sho")
        s_xadd = sem("s_xadd")
        s_pacc = sem("s_pacc")
        s_g = sem("s_g")
        s_ga = sem("s_ga")
        s_c = sem("s_c")
        s_tc = sem("s_tc")
        s_h = sem("s_h")
        s_routing_exp = sem("s_routing_exp")
        s_routing_in = sem("s_routing_in")
        s_qkv = sem("s_qkv")
        s_sub = sem("s_sub")
        s_ex3 = sem("s_ex3")
        s_v3 = sem("s_v3")
        s_sm3 = sem("s_sm3")
        s_ctx3 = sem("s_ctx3")
        s_cm3 = sem("s_cm3")
        s_num3 = sem("s_num3")
        s_ol3 = sem("s_ol3")
        s_sk_in = sem("s_sk_in")
        s_sk_act = sem("s_sk_act")
        s_sk_v = sem("s_sk_v")
        s_sk_pe = sem("s_sk_pe")
        s_nansum = sem("s_nansum")
        s_out = sem("s_out")

        def w(layer, name):
            region, at, n, r = WEIGHTS[f"{layer}_{name}"]
            return W[region][0:r, at:at + n]

        def xT(layer):
            return xTs[:, LAYERS.index(layer) % 2, :]

        def wide_of(name):
            at, n = WIDE[name]
            return wide[:, at:at + n]

        def all_done(eng, layer):
            eng.wait_ge(s_side_done, order[(before(layer), ("tail", B - 1))] + 1)

        def n_loads(layer):
            return 16 * sum(1 for k in WEIGHTS if k.startswith(layer + "_"))

        block = ctx.enter_context(nc.Block())

        @block.sync
        def _(sp):
            x_view = d["x"].rearrange("(n p) d -> p n d", p=P)
            sp.dma_start(x[:, :, :], x_view).then_inc(s_load["x"], 16)
            if "L0a" in LAYERS:
                sp.dma_start(d["rel_ext"][0:REL_ROWS, :], d["rel"]).then_inc(s_rel_ext, 16)
                sp.dma_start(d["rel_ext"][REL_ROWS:528, :],
                             d["rel"][REL_ROWS - 1:REL_ROWS, :].broadcast_to([528 - REL_ROWS, 16])).then_inc(s_rel_ext, 16)
            for l in LAYERS:
                if l in FREED_BY:
                    continue
                for k in WEIGHTS:
                    if k.startswith(l + "_"):
                        region, at, n, r = WEIGHTS[k]
                        sp.dma_start(W[region][0:r, at:at + n], d[k]).then_inc(s_load[l], 16)
                if l == "L0a":
                    sp.dma_start(wide[:, :], d["wide"].broadcast_to([P, WIDE_W])).then_inc(s_load["vec"], 16)
                    sp.dma_start(cols[:, :], d["cols"]).then_inc(s_load["vec"], 16)
                    sp.dma_start(gw[:, :], d["gw"]).then_inc(s_load["gw"], 16)
                    sp.wait_ge(s_rel_ext, 32)
                    src = d["rel_ext"]
                    windows = bass.AP(tensor=src.tensor, offset=0, ap=[[16, P], [16 * P, 4], [1, 256]])
                    sp.dma_start(rel_rows, windows).then_inc(s_load["rel"], 16)
                    sp.dma_start(ctxT[:, :], d["ctxT"]).then_inc(s_load["ctx"], 16)
                    sp.wait_ge(s_bias_zero, 1)
                    for part in (0, 64, 96):
                        sp.dma_start(bias_raw[part:part + 1, :], d["rows"]).then_inc(s_load["bias"], 16)
            for l in LAYERS:
                if l not in FREED_BY:
                    continue
                prev = FREED_BY[l]
                sp.wait_ge(s_side_done, order[(prev, ("tail", B - 1))] + 1)
                for k in WEIGHTS:
                    if k.startswith(l + "_"):
                        region, at, n, r = WEIGHTS[k]
                        sp.dma_start(W[region][0:r, at:at + n], d[k]).then_inc(s_load[l], 16)
            o_view = out.rearrange("(n p) d -> p n d", p=P)
            for b in range(B):
                if last_block == "L3f":
                    sp.wait_ge(s_acc, exp0["L3f"] + 8 * (b + 1))
                else:
                    sp.wait_ge(s_var, N_VAR - (B - 1 - b) * PER_VAR)
                sp.dma_start(o_view[:, T * b:T * b + T, :], x[:, T * b:T * b + T, :]).then_inc(s_out, 16)
            sp.wait_ge(s_out, 16 * B)

        @block.gpsimd
        def _(pool):
            g = nc.gpsimd
            step = [0]

            def link(ins):
                step[0] += 1
                ins.then_inc(s_const, 1)
                pool.wait_ge(s_const, step[0])

            g.memset(bias_raw, 0.0).then_inc(s_bias_zero, 1)
            g.memset(mhalf[:, :], -0.5)
            g.memset(ones[:, :], 1.0)
            g.memset(onesb[:, :], 1.0)
            g.memset(inv_keys[:, :], 1.0 / S)
            link(g.memset(ident[:, :], 0.0))
            link(g.affine_select(out=ident[:, :], in_=ident[:, :], compare_op=ALU.not_equal, fill=1.0, base=0,
                                 pattern=[[-1, P]], channel_multiplier=1))
            link(g.tensor_copy(identb[:, :], ident[:, :]))
            link(g.memset(band[:, :, :], 0.0))
            link(g.affine_select(out=band[:, :, :], in_=band[:, :, :], compare_op=ALU.is_ge, fill=MASKED, base=0,
                                 pattern=[[0, 2], [1, 192]], channel_multiplier=-1))
            link(g.affine_select(out=band[:, :, :], in_=band[:, :, :], compare_op=ALU.is_ge, fill=MASKED,
                                 base=2 * HALO - 1, pattern=[[0, 2], [-1, 192]], channel_multiplier=1))
            link(g.memset(hmask[:, :], 1.0))
            link(g.affine_select(out=hmask[:, :], in_=hmask[:, :], compare_op=ALU.is_ge, fill=0.0, base=0,
                                 pattern=[[-8, 16]], channel_multiplier=1))
            link(g.affine_select(out=hmask[:, :], in_=hmask[:, :], compare_op=ALU.is_ge, fill=0.0, base=7,
                                 pattern=[[8, 16]], channel_multiplier=-1))
            link(g.memset(tri[:, :, :], 1.0))
            link(g.affine_select(out=tri[:, :, :], in_=tri[:, :, :], compare_op=ALU.is_gt, fill=0.0, base=0,
                                 pattern=[[1, 16], [-1, 16]], channel_multiplier=0))
            powers = [0]

            def inverse_root():
                n = powers[0]
                powers[0] += 1
                pool.wait_ge(s_var, n + 1)
                g.tensor_tensor(rstd[:, :], ve[:, :], mhalf[:, :], ALU.pow).then_inc(s_rstd, 1)

            def pad_x(layer, b):
                if b >= 2:
                    pool.wait_ge(s_side_done, order[(layer, ("v", b - 2))] + 1)
                g.tensor_copy(xpad[:, b % 2, HALO:HALO + S], xT(layer)[:, S * b:S * b + S]).then_inc(s_xpad, 1)

            def mask_queries(layer, b):
                pool.wait_ge(s_side_done, order[(layer, ("q" if layer == "L2a" else "qk", b))] + 1)
                for h in range(16):
                    if b:
                        pool.wait_ge(s_qk, unit0[layer] + (b - 1) * 16 + 2 * (h // 2) + 2)
                    g.tensor_scalar(qz[:, 256 * h:256 * h + 256], q_small(b), hmask[:, h:h + 1], 1.0,
                                    ALU.mult, ALU.mult).then_inc(s_qz, 1)

            split_steps = [0]

            def split_v(layer, b, p):
                n = vno[(layer, ("v", b, p))]
                raw = v_raw(layer, b, p)
                rest = raw.rearrange("p (k n) -> p k n", k=2)
                part = [z.rearrange("p (k n) -> p k n", k=2)[:, :, 128 * p:128 * p + 128] for z in v_parts]

                def then(ins):
                    split_steps[0] += 1
                    ins.then_inc(s_split_step, 1)
                    pool.wait_ge(s_split_step, split_steps[0])

                pool.wait_ge(s_side_done, order[(layer, ("v", b, p))] + 1)
                if b:
                    pool.wait_ge(s_pv, unit0[layer] + (b - 1) * ATT[layer]["H"] + 2 * p + 2)
                then(g.tensor_copy(part[0], rest))
                then(g.tensor_tensor(rest, rest, part[0], ALU.subtract))
                then(g.tensor_copy(part[1], rest))
                g.tensor_tensor(part[2], rest, part[1], ALU.subtract).then_inc(s_vsplit, 1)

            for b in range(B):
                inverse_root()
            for layer in LAYERS:
                if layer in ATT:
                    a = ATT[layer]
                    pool.wait_ge(s_load[layer], n_loads(layer))
                    g.tensor_scalar(w(layer, "wq"), w(layer, "wq"), a["scale"], 1.0, ALU.mult, ALU.mult).then_inc(s_scaled, 1)
                    if layer == "L2x":
                        pool.wait_ge(s_load["vec"], 32)
                        at = COLS["L2x_bq"]
                        g.tensor_scalar(cols[:, at:at + 1], cols[:, at:at + 1], a["scale"], None,
                                        ALU.mult).then_inc(s_scaled, 1)
                    all_done(pool, layer)
                    if a["dh"] == 64:
                        g.memset(qz[:, :], 0.0).then_inc(s_qzero, 1)
                    if layer == "L2a":
                        g.memset(xpad[:, :, 0:HALO], 0.0)
                        g.memset(xpad[:, :, HALO + S:PADS], 0.0)
                        g.memset(v_sb[0:64, 256:512], 0.0)
                        pad_x(layer, 0)
                    if layer == "L0a":
                        pool.wait_ge(s_side_full, order[(layer, ("relout", T - 1, 1))] + 1)
                    if a["dh"] == 64:
                        for s in range(-3, (B + 1) * a["H"] + 1):
                            for item in sched.get((layer, s), ()):
                                if item[0] == "v":
                                    split_v(layer, item[1], item[2])
                            if s > 8 and (s - 8) % a["H"] == 0:
                                inverse_root()
                        continue
                    for b in range(B):
                        if layer == "L2a" and b + 1 < B:
                            pad_x(layer, b + 1)
                        mask_queries(layer, b)
                        if b:
                            if layer == "L0a":
                                inverse_root()
                            inverse_root()
                    if layer == "L0a":
                        inverse_root()
                    inverse_root()
                elif layer == "L1f":
                    for b in range(B):
                        for e in range(8):
                            n = 8 * b + e
                            pool.wait_ge(s_t23, n + 1)
                            if n:
                                pool.wait_ge(s_pacc, n)
                            g.tensor_tensor(x[:, T * b:T * b + T, :], x[:, T * b:T * b + T, :],
                                            o_sb[:, n % 2, 0:256].rearrange("p (t d) -> p t d", t=T),
                                            ALU.add).then_inc(s_pacc, 1)
                        inverse_root()
                elif layer != "L3f":
                    for b in range(B):
                        inverse_root()

        @block.scalar
        def _(act):
            a_ = nc.scalar
            copy = lambda dst, src: a_.activation(dst, src, ACT.Copy)
            side = [0]

            def move(layer, item):
                k = side[0]
                side[0] += 1
                m = psM[k % 2]
                kind, b = item[0], (item[1] if len(item) > 1 else 0)
                act.wait_ge(s_side_full, k + 1)
                if kind == "tail":
                    nxt = LAYERS[0] if layer == "init" else LAYERS[LAYERS.index(layer) + 1]
                    ins = copy(xT(nxt)[:, S * b:S * b + S], m[:, 0:256])
                elif kind == "qk" and ATT[layer]["dh"] == 64:
                    p = item[2]
                    if b == 0 and p == 0:
                        act.wait_ge(s_qzero, zero_no[layer])
                    copy(qz[0:64, 512 * p:512 * p + 256], m[0:64, 0:256])
                    copy(qz[64:128, 512 * p + 256:512 * p + 512], m[64:128, 0:256])
                    ins = copy(k_sb[:, 256 * p:256 * p + 256], m[:, 256:512])
                elif kind == "qk":
                    if b >= 2:
                        act.wait_ge(s_qz, 16 * (8 * qz_no[layer] + b - 1))
                    if layer == "L2x":
                        cq, ck = COLS["L2x_bq"], COLS["L2x_bk"]
                        act.wait_ge(s_scaled, scaled_no[layer])
                        act.wait_ge(s_load["vec"], 32)
                        a_.activation(q_small(b), m[:, 0:256], ACT.Identity, bias=cols[:, cq:cq + 1])
                        ins = a_.activation(k_of(layer, b), m[:, 256:512], ACT.Identity, bias=cols[:, ck:ck + 1])
                    else:
                        copy(q_small(b), m[:, 0:256])
                        ins = copy(k_of(layer, b), m[:, 256:512])
                elif kind == "q":
                    if b >= 2:
                        act.wait_ge(s_qz, 16 * (8 * qz_no[layer] + b - 1))
                    ins = copy(q_small(b), m[:, 0:256])
                elif kind == "k":
                    ins = copy(k_of(layer, b), m[:, 0:PADS])
                elif kind == "v" and ATT[layer]["dh"] == 64:
                    n = vno[(layer, item)]
                    if b or item[2] >= 2:
                        act.wait_ge(s_vsplit, n - 1)
                    ins = copy(v_raw(layer, b, item[2]), m[:, 0:256])
                elif kind == "v":
                    if layer == "L0a":
                        ins = copy(v_raw(layer, b), m[:, 0:256])
                    elif layer == "L2a":
                        if b:
                            act.wait_ge(s_vsplit, vno[(layer, item)])
                        copy(v_sb[:, 0:256], m[:, 0:256])
                        ins = copy(v_sb[64:128, 256:512], m[64:128, 256:512])
                    else:
                        if b >= 2:
                            act.wait_ge(s_vsplit, vno[(layer, item)] - 1)
                        ins = copy(v_raw(layer, b), m[:, 0:256])
                elif kind == "vmean":
                    ins = copy(v_sb[:, 1024 + 128 * (b % 2):1152 + 128 * (b % 2)], m[:, 0:128])
                elif kind == "nan":
                    ins = copy(nanf[:, 5:6], m[:, 0:1])
                elif kind == "rel":
                    ins = copy(relT[:, b, :], m[:, :])
                elif kind == "relout":
                    t, half = item[1], item[2]
                    ins = copy(rel_out[:, t, 8 * half:8 * half + 8, :, :].rearrange("p h b d -> p (h b d)"), m[:, :])
                elif kind == "ot" and layer in ATT and ATT[layer]["dh"] == 64:
                    a = ATT[layer]
                    j0 = (2 * item[2]) % (a["H"] // 2)
                    dst = oT[:, 0:64 * a["H"] * T].rearrange("p (t j n) -> p j t n", t=T, j=a["H"] // 2)[:, j0:j0 + 2, :, :]
                    ins = copy(dst, m[:, :].rearrange("p (j t n) -> p j t n", j=2, t=T))
                elif kind in ("ot", "qT"):
                    ins = copy(oT[:, 0:256], m[:, 0:256]) if kind == "ot" else copy(oT[:, 256:512], m[:, 0:256])
                elif kind in ("wo", "hout"):
                    r = res_no[(layer, b)]
                    if r:
                        act.wait_ge(s_xadd, r)
                    ins = copy(o_res[:, :, :], m[:, 0:256].rearrange("p (t d) -> p t d", t=T))
                elif kind == "gate":
                    E = GATES[layer][1]
                    ins = copy(lg[:, :, 0:E], m[:, 0:NT * E].rearrange("p (n e) -> p n e", n=NT))
                ins.then_inc(s_side_done, 1)

            def moves(layer, step):
                for item in sched.get((layer, step), ()):
                    move(layer, item)

            def attention(layer):
                a = ATT[layer]
                U, K, g0 = a["H"], a["keys"], unit0[layer]
                NU = B * U
                for s in range(-5, NU + 14):
                    moves(layer, s)
                    if 0 <= s < NU:
                        g = g0 + s
                        act.wait_ge(s_tr, g + 1)
                        if g >= 2:
                            act.wait_ge(s_pv, g - 1)
                        copy(turned(g, 0), psT[g % 2][:, :]).then_inc(s_pthi, 1)
                    u = s + 2
                    if 0 <= u < NU:
                        g = g0 + u
                        act.wait_ge(s_max, g + 1)
                        if g >= 2:
                            act.wait_ge(s_tr, g - 1)
                        for i in range(2):
                            sc = clamped[:, g % 2, :] if layer == "L2x" else psS[g % 2][:, :]
                            ins = a_.activation(prob[:, g % 2, K * i:K * i + K], sc[:, K * i:K * i + K], ACT.Exp,
                                                bias=negmax[:, g % 2, i:i + 1],
                                                accum_out=rsum[:, (u // U) % 2, 2 * (u % U) + i:2 * (u % U) + i + 1])
                        ins.then_inc(s_exp, 1)

            def experts(layer):
                f = FFN[layer]
                E = len(f["chunks"])
                NE = B * E
                hop = hop0[layer]
                ahead = f["ahead"]
                for n in range(-ahead, NE + 4):
                    if n + ahead < NE:
                        e = (n + ahead) % E
                        g = exp0[layer] + n + ahead
                        C = f["chunks"][e]
                        if f["glu"]:
                            for c in range(C):
                                act.wait_ge(s_hfull, hop + 1)
                                if hop >= 2:
                                    act.wait_ge(s_hop, hop - 1)
                                a_.activation(sg[:, hop % 2, :], psH[hop % 4][:, 0:256], ACT.Silu).then_inc(s_sg, 1)
                                hop += 1
                        else:
                            if n + ahead == 0:
                                act.wait_ge(s_load["vec"], 32)
                            if g >= 2:
                                act.wait_ge(s_down, g - 1)
                            for c in range(0, C, 2):
                                act.wait_ge(s_hfull, hop + 1)
                                for i in range(2):
                                    at = COLS[layer + "_b1"] + 4 * e + c + i
                                    ins = a_.activation(hT[:, g % 2, c + i, :], psH[hop % 4][:, 256 * i:256 * i + 256],
                                                        ACT.Gelu, bias=cols[:, at:at + 1])
                                ins.then_inc(s_hop, 1)
                                hop += 1
                    if n >= -1:
                        moves(layer, n)

            for b in range(B):
                moves("init", b)
            for layer in LAYERS:
                if layer in ATT:
                    attention(layer)
                elif layer in FFN:
                    moves(layer, -2)
                    if layer != "L3f":
                        if layer == "L2f":
                            act.wait_ge(s_side_done, order[(layer, ("gate",))] + 1)
                        else:
                            act.wait_ge(s_routing_in, rout_no[layer])
                        a_.activation(wexp[:, :, 0:GATES[layer][1]], lg[:, :, 0:GATES[layer][1]],
                                      ACT.Exp if layer == "L0f" else ACT.Sigmoid).then_inc(s_routing_exp, 1)
                    if layer == "L3f":
                        a_.preload_act_table_set("natural_log_exp_and_others")
                        for k in range(4 * SINK_ITERS + 1):
                            act.wait_ge(s_sk_in, k + 1)
                            if k % 4 in (0, 2):
                                a_.activation(sk_e[:, :, :], sk_d[:, :, :] if k < 4 * SINK_ITERS else la[:, :, :],
                                              ACT.Exp).then_inc(s_sk_act, 1)
                            elif k % 4 == 1:
                                a_.activation(sk_l[:, 0:16], sk_s[:, 0:16], ACT.Ln).then_inc(s_sk_act, 1)
                            else:
                                a_.activation(sk_l[:, 0:8], psO[1][:, 0:8], ACT.Ln).then_inc(s_sk_act, 1)
                    experts(layer)
                elif layer == "L1f":
                    moves(layer, -2)
                    act.wait_ge(s_routing_in, rout_no[layer])
                    a_.activation(wexp[:, :, 0:8], lg[:, :, 0:8], ACT.Exp).then_inc(s_routing_exp, 1)
                    act.wait_ge(s_load["vec"], 32)
                    for b in range(B):
                        for e in range(9):
                            step = 9 * b + e
                            if e < 8:
                                n = 8 * b + e
                                act.wait_ge(s_a1, n + 1)
                                if n >= 2:
                                    act.wait_ge(s_x23, n - 1)
                                at = COLS["L1f_b1"] + e
                                a_.activation(hT[:, n % 2, 0, :], psT[n % 2][:, 0:256], ACT.Silu,
                                              bias=cols[:, at:at + 1]).then_inc(s_h1, 1)
                            else:
                                for c in range(2):
                                    act.wait_ge(s_shg, 2 * b + c + 1)
                                    if b:
                                        act.wait_ge(s_shh, 2 * (b - 1) + c + 1)
                                    a_.activation(sg[:, c, :], psS[c][:, 0:256], ACT.Silu).then_inc(s_shs, 1)
                            moves(layer, step)
                    moves(layer, 72)
                    moves(layer, 73)
                    moves(layer, 74)
                elif layer == "L1a":
                    act.wait_ge(s_load["vec"], 32)
                    for b in range(B + 1):
                        if b < B:
                            act.wait_ge(s_g, b + 1)
                            if b:
                                act.wait_ge(s_h, b)
                            for i in range(4):
                                at = COLS["L1a_b"] + i
                                ins = a_.activation(gates[:, i, :], psH[i][:, 0:256], ACT.Sigmoid if i < 3 else ACT.Tanh,
                                                    bias=cols[:, at:at + 1])
                            ins.then_inc(s_ga, 1)
                            act.wait_ge(s_c, b + 1)
                            a_.activation(tanh_c, c_state, ACT.Tanh).then_inc(s_tc, 1)
                        moves(layer, b)
                elif layer == "L3a":
                    for b in range(-1, B + 2):
                        if b + 1 < B:
                            for t in range(T):
                                n = T * (b + 1) + t
                                qk3, va3 = qk3s[:, (b + 1) % 2], va3s[:, (b + 1) % 2]
                                act.wait_ge(s_sub, n + 1)
                                a_.activation(qk3[:, t, :], qk3[:, t, :], ACT.Exp).then_inc(s_ex3, 1)
                                if b >= 1:
                                    act.wait_ge(s_ctx3, b)
                                copy(va3[:, t, 0:128], psS[t][:, 256:384]).then_inc(s_v3, 1)
                        moves(layer, b)

        @block.tensor
        def _(pe):
            mm = nc.tensor.matmul
            side = [0]
            tails = [0]

            def across(out_, in_):
                return nc.tensor.transpose(out_, in_, ident[:, :])

            def row_bias(out_, name, at=0, n=128, stop=True):
                return mm(out_, onesb[:, :], bias_parts[:, ROWS[name] + at:ROWS[name] + at + n], start=False, stop=stop)

            def fill(layer, item):
                k = side[0]
                side[0] += 1
                m = psM[k % 2]
                kind, b = item[0], (item[1] if len(item) > 1 else 0)
                if k >= 2:
                    pe.wait_ge(s_side_done, k - 1)
                tok = lambda t: slice(S * b + P * t, S * b + P * t + P)
                if kind == "tail":
                    n = tails[0]
                    tails[0] += 1
                    pe.wait_ge(s_xn, n + 1)
                    for t in range(T):
                        ins = across(m[:, P * t:P * t + P], xn[:, t, :])
                elif kind == "qk":
                    dh64 = ATT[layer]["dh"] == 64
                    at = 128 * item[2] if dh64 else 0
                    src = xT(layer) if layer == "L0a" else ctxT[:, :]
                    mm(m[:, 0:256], w(layer, "wq")[:, at:at + 128], xT(layer)[:, S * b:S * b + S], start=True, stop=True)
                    ins = mm(m[:, 256:512], w(layer, "wk")[:, at:at + 128], src[:, S * b:S * b + S], start=True, stop=True)
                elif kind == "q":
                    ins = mm(m[:, 0:256], w(layer, "wq"), xT(layer)[:, S * b:S * b + S], start=True, stop=True)
                elif kind == "k":
                    pe.wait_ge(s_xpad, b + 1)
                    ins = mm(m[:, 0:PADS], w(layer, "wk"), xpad[:, b % 2, :], start=True, stop=True)
                elif kind == "v":
                    if layer == "L2a":
                        for i, at in enumerate((0, P, P // 2, P + P // 2)):
                            ins = mm(m[:, P * i:P * i + P], xpad[:, b % 2, at:at + P], w(layer, "wv"), start=True, stop=True)
                    else:
                        at = 128 * item[2] if ATT[layer]["dh"] == 64 else 0
                        src = xT(layer) if layer == "L0a" else ctxT[:, :]
                        for kt in range(2):
                            ins = mm(m[:, P * kt:P * kt + P], src[:, tok(kt)], w(layer, "wv")[:, at:at + 128],
                                     start=True, stop=layer != "L2x")
                            if layer == "L2x":
                                ins = row_bias(m[:, P * kt:P * kt + P], "L2x_bv")
                elif kind == "vmean":
                    pe.wait_ge(s_side_done, order[(layer, ("v", b))] + 1)
                    for kt in range(2):
                        ins = mm(m[:, 0:128], inv_keys[:, :], v_sb[:, 512 * (b % 2) + P * kt:512 * (b % 2) + P * kt + P],
                                 start=kt == 0, stop=kt == 1)
                elif kind == "nan":
                    pe.wait_ge(s_nansum, 1)
                    ins = mm(m[:, 0:1], ones[:, :], nanf[:, 4:5], start=True, stop=True)
                elif kind == "rel":
                    if b == 0:
                        pe.wait_ge(s_load["rel"], 16)
                    for j in range(4):
                        ins = across(m[:, P * j:P * j + P], rel_rows[:, j, P * b:P * b + P])
                elif kind == "relout":
                    t, half = item[1], item[2]
                    r = 2 * t + half
                    pe.wait_ge(s_side_done, order[(layer, ("v", B - 1))] + 1)
                    pe.wait_ge(s_relbias, r + 1)
                    for h in range(8 * half, 8 * half + 8):
                        for kt in range(2):
                            at = 64 * (h % 8)
                            ins = mm(m[:, at:at + 64].rearrange("p (b d) -> p b d", b=B),
                                     rel_bias(r, kt)[:, P * (h % 8):P * (h % 8) + P],
                                     v_all[:, :, kt, 8 * h:8 * h + 8], start=kt == 0, stop=kt == 1)
                elif kind == "ot" and layer == "L3a":
                    pe.wait_ge(s_cm3, b + 1)
                    pe.wait_ge(s_side_done, order[(layer, ("qT", b))] + 1)
                    for t in range(T):
                        ins = mm(psT[1][:, 144 * t:144 * t + 144], oT[:, 256 + P * t:256 + P * t + P], cm3,
                                 start=True, stop=True)
                    ins.then_inc(s_num3, 1)
                    pe.wait_ge(s_ol3, b + 1)
                    for t in range(T):
                        ins = across(m[:, P * t:P * t + P], ol3[:, t, :])
                elif kind == "ot":
                    a = ATT[layer]
                    per = a["H"] // a["group"]
                    gi = per * b + item[2] if a["dh"] == 64 else b
                    pe.wait_ge(s_norm, group0[layer] + (gi + 1 if a["dh"] == 64 else per * (b + 1)))
                    for i in range(4 if a["dh"] == 64 else 2):
                        ins = across(m[:, P * i:P * i + P], o_sb[:, gi % 2, P * i:P * i + P])
                elif kind == "wo":
                    n_ot = 0 if layer == "L3a" or ATT[layer]["dh"] == 8 else ATT[layer]["H"] // ATT[layer]["group"] - 1
                    pe.wait_ge(s_side_done, order[(layer, ("ot", b, n_ot))] + 1)
                    J = ATT[layer]["H"] // 2 if layer in ATT and ATT[layer]["dh"] == 64 else 1
                    wo = w(layer, "wp" if layer == "L3a" else "wo")
                    if layer == "L0x":
                        pe.wait_ge(s_bias_split, 5)
                    for t in range(T):
                        for j in range(J):
                            mm(m[:, P * t:P * t + P], oT[:, P * (J * t + j):P * (J * t + j) + P],
                               wo[:, P * j:P * j + P], start=j == 0, stop=False)
                        ins = row_bias(m[:, P * t:P * t + P], layer + ("_bp" if layer == "L3a" else "_bo"))
                elif kind == "hout":
                    pe.wait_ge(s_h, b + 1)
                    for t in range(T):
                        ins = across(m[:, P * t:P * t + P], h_state(b)[:, P * t:P * t + P])
                elif kind == "qT":
                    pe.wait_ge(s_sm3, 2 * b + 2)
                    for t in range(T):
                        ins = across(m[:, P * t:P * t + P], qk3s[:, b % 2, t, 0:128])
                elif kind == "gate":
                    at, E = GATES[layer]
                    for n in range(NT):
                        ins = mm(m[:, E * n:E * n + E], xT(layer)[:, P * n:P * n + P], gw[:, at:at + E], start=True, stop=True)
                ins.then_inc(s_side_full, 1)

            def fills(layer, step):
                for item in sched.get((layer, step), ()):
                    fill(layer, item)

            def attention(layer):
                a = ATT[layer]
                dh, U, K, g0, size = a["dh"], a["H"], a["keys"], unit0[layer], a["group"]
                NU = B * U
                pe.wait_ge(s_scaled, scaled_no[layer])

                def scores(u):
                    b, r, g = u // U, u % U, g0 + u
                    p, t = r // 2, r % 2
                    bank = psS[g % 2]
                    if g >= 2 and (layer != "L2x" or u < 2):
                        pe.wait_ge(s_exp, g - 1)
                    elif g >= 2:
                        pe.wait_ge(s_max, g - 1)
                    if t == 0:
                        if dh == 64:
                            pe.wait_ge(s_side_done, order[(layer, ("qk", b, p))] + 1)
                        else:
                            pe.wait_ge(s_qz, 128 * qz_no[layer] + 16 * b + 2 * p + 2)
                            if p == 0:
                                pe.wait_ge(s_side_done, order[(layer, ("k" if layer == "L2a" else "qk", b))] + 1)
                    if layer == "L2a":
                        mm(bank[:, 0:2 * K], identb[:, :], band[:, :, :].rearrange("p h k -> p (h k)"), start=True, stop=False)
                    for i in range(2):
                        h = 2 * p + i
                        if dh == 64:
                            keys = k_sb[:, 256 * p:256 * p + 256]
                        elif layer == "L2a":
                            keys = k_of(layer, b)[:, P * t:P * t + K]
                        else:
                            keys = k_of(layer, b)
                        ins = mm(bank[:, K * i:K * i + K], qz[:, 256 * h + P * t:256 * h + P * t + P], keys,
                                 start=layer != "L2a", stop=layer != "L2a" or i == 1)
                    ins.then_inc(s_qk, 1)

                def turn(u):
                    g = g0 + u
                    pe.wait_ge(s_exp, g + 1)
                    if g >= 2:
                        pe.wait_ge(s_ptc, g - 1)
                    for i in range(2):
                        for kt in range(2):
                            at = K * i + (K - P) * kt
                            ins = across(psT[g % 2][:, P * (2 * i + kt):P * (2 * i + kt) + P], prob[:, g % 2, at:at + P])
                    ins.then_inc(s_tr, 1)

                def weigh(u):
                    b, r, g = u // U, u % U, g0 + u
                    p, t = r // 2, r % 2
                    gi = group0[layer] + u // size
                    pe.wait_ge(s_ptc, g + 1)
                    if t == 0 and (dh == 64 or p == 0):
                        pe.wait_ge(s_vsplit, vno[(layer, ("v", b, p) if dh == 64 else ("v", b))] + 1)
                    if u % size == 0 and gi >= 2:
                        pe.wait_ge(s_norm, gi - 1)
                    for i in range(2):
                        h = 2 * p + i
                        hi, lo = ([turned(g, z)[:, P * (2 * i + kt):P * (2 * i + kt) + P] for kt in range(2)] for z in range(2))
                        if dh == 64:
                            o = psO[gi % 2][:, (u % size) * 128 + 64 * i:(u % size) * 128 + 64 * i + 64]
                            for kt in range(2):
                                for pt, c in ((hi, 0), (hi, 1), (hi, 2), (lo, 0), (lo, 1)):
                                    at = 1024 * kt + 64 * h
                                    ins = mm(o, pt[kt], v_parts[c][:, at:at + 64], start=kt == 0 and pt is hi and c == 0,
                                             stop=kt == 1 and pt is lo and c == 1)
                        else:
                            at = 24 * (size * t + 2 * (p % (size // 2)) + i)
                            o = psO[gi % 2][:, at:at + 24]
                            vp = v_small(layer, b)
                            vs = [vp[:, 16 * (2 * kt + t if layer == "L2a" else kt) + h, :, :].rearrange("p c d -> p (c d)")
                                  for kt in range(2)]
                            mm(o, hi[0], vs[0], start=True, stop=False)
                            mm(o[:, 0:16], lo[0], vs[0][:, 0:16], start=False, stop=False)
                            mm(o[:, 0:16], lo[1], vs[1][:, 0:16], start=False, stop=False)
                            ins = mm(o, hi[1], vs[1], start=False, stop=True)
                    ins.then_inc(s_pv, 1)

                for s in range(-5, NU + 14):
                    if 0 <= s + 2 < NU:
                        scores(s + 2)
                    fills(layer, s)
                    if 0 <= s - 2 < NU:
                        weigh(s - 2)
                    if 0 <= s < NU:
                        turn(s)

            def experts(layer):
                f = FFN[layer]
                E, glu = len(f["chunks"]), f["glu"]
                NE = B * E
                hop = [hop0[layer]]
                hops_of = {}

                def up(n):
                    b, e = n // E, n % E
                    toks = xT(layer)[:, S * b:S * b + S]
                    at = 128 * sum(f["chunks"][:e])
                    for c in range(0, f["chunks"][e], 1 if glu else 2):
                        if hop[0] >= 4:
                            pe.wait_ge(s_hop, hop[0] - 3)
                        bank = psH[hop[0] % 4]
                        for i in range(2):
                            if glu:
                                lhsT = w(layer, ("gate", "up")[i])[:, at + 128 * c:at + 128 * c + 128]
                            else:
                                lhsT = w(layer, "up")[:, at + 128 * (c + i):at + 128 * (c + i) + 128]
                            ins = mm(bank[:, 256 * i:256 * i + 256], lhsT, toks, start=True, stop=True)
                        ins.then_inc(s_hfull, 1)
                        hop[0] += 1
                    hops_of[n] = hop[0]

                def down(n):
                    e, g = n % E, exp0[layer] + n
                    C = f["chunks"][e]
                    at = 128 * sum(f["chunks"][:e])
                    pe.wait_ge(s_hop, hops_of[n])
                    if g >= 2:
                        pe.wait_ge(s_acc, g - 1)
                    for t in range(T):
                        o = psO[g % 2][:, P * t:P * t + P]
                        for c in range(C):
                            ins = mm(o, hT[:, g % 2, c, P * t:P * t + P], w(layer, "down")[:, at + 128 * c:at + 128 * c + 128],
                                     start=c == 0, stop=c == C - 1 and layer != "L0f")
                        if layer == "L0f":
                            ins = row_bias(o, "L0f_b2", 128 * e)
                    ins.then_inc(s_down, 1)

                for n in range(-f["ahead"], NE + 4):
                    if n + f["ahead"] < NE:
                        up(n + f["ahead"])
                    if n >= -1:
                        fills(layer, n)
                    if 0 <= n < NE:
                        down(n)

            pe.wait_ge(s_const, 11)
            for b in range(B):
                fills("init", b)
            for layer in LAYERS:
                pe.wait_ge(s_load[layer], n_loads(layer))
                all_done(pe, layer)
                if layer == "L0a":
                    pe.wait_ge(s_load["vec"], 32)
                    pe.wait_ge(s_load["gw"], 16)
                    pe.wait_ge(s_load["ctx"], 16)
                if layer in ATT:
                    attention(layer)
                elif layer in FFN:
                    fills(layer, -2)
                    if layer == "L3f":
                        for it in range(SINK_ITERS):
                            pe.wait_ge(s_sk_v, 3 * it + 1)
                            across(psO[0][:, 0:128], sk_col).then_inc(s_sk_pe, 1)
                            pe.wait_ge(s_sk_v, 3 * it + 2)
                            mm(psO[0][:, 0:8], ones[:, :], sk_diag, start=True, stop=True).then_inc(s_sk_pe, 1)
                            pe.wait_ge(s_sk_v, 3 * it + 3)
                            mm(psO[1][:, 0:8], ones[:, :], sk_s[:, 16:24], start=True, stop=True).then_inc(s_sk_in, 1)
                    experts(layer)
                elif layer == "L1a":
                    def from_x(b):
                        if b:
                            pe.wait_ge(s_ga, b)
                        for i in range(4):
                            ins = mm(psH[i][:, 0:256], w(layer, "w")[:, P * i:P * i + P], xT(layer)[:, S * b:S * b + S],
                                     start=True, stop=b == 0)
                        if b == 0:
                            ins.then_inc(s_g, 1)

                    from_x(0)
                    for b in range(B + 1):
                        if 1 <= b < B:
                            pe.wait_ge(s_h, b)
                            for i in range(4):
                                ins = mm(psH[i][:, 0:256], w(layer, "u")[:, P * i:P * i + P], h_state(b - 1),
                                         start=False, stop=True)
                            ins.then_inc(s_g, 1)
                        if b + 1 < B:
                            from_x(b + 1)
                        fills(layer, b)
                elif layer == "L1f":
                    fills(layer, -2)

                    def spread(n):
                        b, e = n // 8, n % 8
                        if n == 0:
                            pe.wait_ge(s_routing_in, rout_no[layer] + 1)
                        if n >= 2:
                            pe.wait_ge(s_xs, n - 1)
                        if b and e < 2:
                            pe.wait_ge(s_shh, 2 * b)
                        for t in range(T):
                            ins = mm(psS[n % 2][:, P * t:P * t + P],
                                     wexp[:, T * b + t, e:e + 1].broadcast_to([P, P]), ident[:, :], start=True, stop=True)
                        ins.then_inc(s_bc, 1)

                    def first(n):
                        e = n % 8
                        pe.wait_ge(s_xs, n + 1)
                        if n >= 2:
                            pe.wait_ge(s_h1, n - 1)
                        mm(psT[n % 2][:, 0:256], w(layer, "w1")[:, P * e:P * e + P], prob[:, n % 2, 0:256],
                           start=True, stop=True).then_inc(s_a1, 1)

                    def second(n):
                        b, e = n // 8, n % 8
                        if n >= 2:
                            pe.wait_ge(s_t23, n - 1)
                        if b and e < 2:
                            pe.wait_ge(s_sho, b)
                        o = psO[n % 2]
                        for t in range(T):
                            mm(o[:, P * t:P * t + P], xT(layer)[:, S * b + P * t:S * b + P * t + P],
                               w(layer, "w3")[:, P * e:P * e + P], start=True, stop=True)
                        pe.wait_ge(s_h1, n + 1)
                        for t in range(T):
                            at = 256 + P * t
                            mm(o[:, at:at + P], hT[:, n % 2, 0, P * t:P * t + P], w(layer, "w2")[:, P * e:P * e + P],
                               start=True, stop=False)
                            ins = row_bias(o[:, at:at + P], "L1f_b2", 128 * e)
                        ins.then_inc(s_x23, 1)

                    spread(0)
                    spread(1)
                    first(0)
                    for b in range(B):
                        for e in range(8):
                            n = 8 * b + e
                            if n + 2 < 8 * B and e < 6:
                                spread(n + 2)
                            if n + 1 < 8 * B and e < 7:
                                first(n + 1)
                            second(n)
                            fills(layer, 9 * b + e)
                        pe.wait_ge(s_xs, 8 * b + 8)
                        toks = xT(layer)[:, S * b:S * b + S]
                        for c in range(2):
                            for i, name in enumerate(("sg", "su")):
                                ins = mm(psS[c][:, 256 * i:256 * i + 256], w(layer, name)[:, P * c:P * c + P], toks,
                                         start=True, stop=True)
                            ins.then_inc(s_shg, 1)
                        pe.wait_ge(s_t23, 8 * b + 8)
                        pe.wait_ge(s_shh, 2 * b + 2)
                        for t in range(T):
                            for c in range(2):
                                ins = mm(psO[0][:, P * t:P * t + P], hT[:, c, 3, P * t:P * t + P],
                                         w(layer, "sd")[:, P * c:P * c + P], start=c == 0, stop=c == 1)
                        ins.then_inc(s_shd, 1)
                        if b + 1 < B:
                            spread(8 * b + 8)
                            spread(8 * b + 9)
                            first(8 * b + 8)
                        fills(layer, 9 * b + 8)
                    for s in range(72, 76):
                        fills(layer, s)
                elif layer == "L3a":
                    def project(b):
                        for t in range(T):
                            if b:
                                pe.wait_ge(s_v3, T * (b - 1) + t + 1)
                            mm(psS[t][:, 0:384], xT(layer)[:, S * b + P * t:S * b + P * t + P], w(layer, "wqkv"),
                               start=True, stop=False)
                            row_bias(psS[t][:, 0:384], "L3a_bqkv", 0, 384).then_inc(s_qkv, 1)

                    project(0)
                    for b in range(B + 2):
                        if b + 1 < B:
                            project(b + 1)
                        if b < B:
                            pe.wait_ge(s_sm3, T * (b + 1))
                            pe.wait_ge(s_v3, T * (b + 1))
                            for t in range(T):
                                ins = mm(psT[0][:, 0:129], qk3s[:, b % 2, t, 128:256], va3s[:, b % 2, t, 0:129],
                                         start=t == 0, stop=t == 1)
                            ins.then_inc(s_ctx3, 1)
                        fills(layer, b)

        @block.vector
        def _(dve):
            v = nc.vector
            tt, ts, stt = v.tensor_tensor, v.tensor_scalar, v.scalar_tensor_tensor
            steps = [0]

            def link(ins):
                steps[0] += 1
                ins.then_inc(s_dve, 1)
                dve.wait_ge(s_dve, steps[0])

            powers, normed = [0], [0]

            def moments(src, eps):
                for t in range(T):
                    ins = v.bn_stats(stats[:, t, :], src[:, t, :])
                link(ins)
                for t in range(T):
                    ins = v.bn_aggr(mv[:, t, :], stats[:, t, :])
                link(ins)
                if powers[0]:
                    dve.wait_ge(s_rstd, powers[0])
                ts(ve[:, :], mv[:, :, 1], eps, None, ALU.add).then_inc(s_var, 1)
                powers[0] += 1

            def center(dst, src):
                dve.wait_ge(s_rstd, powers[0])
                for t in range(T):
                    ins = ts(dst[:, t, :], src[:, t, :], mv[:, t, 0:1], rstd[:, t:t + 1], ALU.subtract, ALU.mult)
                return ins

            def tiles(b):
                return x[:, T * b:T * b + T, :]

            def tail_sum(layer, b):
                if layer != "L0a":
                    dve.wait_ge(s_side_done, order[(layer, ("hout" if layer == "L1a" else "wo", b))] + 1)
                ins = tt(tiles(b), tiles(b), o_res[:, :, :], ALU.add)
                ins.then_inc(s_xadd, 1)
                dve.wait_ge(s_xadd, res_no[(layer, b)] + 1)

            def tail_moments(layer, b):
                moments(tiles(b), LN_EPS)

            def tail_center(layer, b):
                if normed[0]:
                    dve.wait_ge(s_side_full, tail_order[normed[0] - 1] + 1)
                normed[0] += 1
                center(xn, tiles(b)).then_inc(s_xn, 1)

            def largest_first(src, n, E, dst):
                gt = qz[:, 0:n * E * E].rearrange("p (n e j) -> p n e j", n=n, e=E)
                eq = kv[:, 0:n * E * E].rearrange("p (n e j) -> p n e j", n=n, e=E)
                vj = src.unsqueeze(2).broadcast_to([P, n, E, E])
                ve_ = src.unsqueeze(3).broadcast_to([P, n, E, E])
                tt(gt, vj, ve_, ALU.is_gt)
                link(tt(eq, vj, ve_, ALU.is_equal))
                link(tt(eq, eq, tri[:, 0:E, 0:E].unsqueeze(1).broadcast_to([P, n, E, E]), ALU.mult))
                link(tt(gt, gt, eq, ALU.add))
                link(v.tensor_reduce(dst, gt, AX.X, ALU.add))

            def pick_four(b, i):
                toks = slice(T * b, T * b + T)
                of = lambda z: z[:, 0:NT * 16].rearrange("p (n e) -> p n e", n=NT)[:, toks, :]
                beats = qz[:, 0:T * 256].rearrange("p (n e j) -> p n e j", n=T, e=16)
                ties = kv[:, 0:T * 256].rearrange("p (n e j) -> p n e j", n=T, e=16)
                vj = of(r_b).unsqueeze(2).broadcast_to([P, T, 16, 16])
                ve_ = of(r_b).unsqueeze(3).broadcast_to([P, T, 16, 16])
                wx, rk = wexp[:, toks, :], of(rank)
                c0, c1 = r_s[:, 0:T], r_s[:, T:2 * T]
                if i == 0:
                    tt(beats, vj, ve_, ALU.is_gt)
                    link(tt(ties, vj, ve_, ALU.is_equal))
                elif i == 1:
                    link(tt(ties, ties, tri[:, :, :].unsqueeze(1).broadcast_to([P, T, 16, 16]), ALU.mult))
                    link(tt(beats, beats, ties, ALU.add))
                elif i == 2:
                    link(v.tensor_reduce(rk, beats, AX.X, ALU.add))
                    link(ts(rk, rk, 3.5, None, ALU.is_lt))
                else:
                    link(tt(wx, wx, rk, ALU.mult))
                    link(v.tensor_reduce(c0, wx, AX.X, ALU.add))
                    link(ts(c0, c0, 1e-20, None, ALU.add))
                    link(v.reciprocal(c1, c0))
                    link(ts(c1, c1, 2.5, None, ALU.mult))
                    link(tt(wx, wx, c1.unsqueeze(2).broadcast_to([P, T, 16]), ALU.mult))

            def over_e(col, E):
                return col.unsqueeze(2).broadcast_to([P, NT, E])

            def routing(layer):
                at, E = GATES[layer]
                g = lg[:, :, 0:E]
                wx = wexp[:, :, 0:E]
                rk = rank[:, 0:NT * E].rearrange("p (n e) -> p n e", n=NT)
                ra = r_a[:, 0:NT * E].rearrange("p (n e) -> p n e", n=NT)
                rb = r_b[:, 0:NT * E].rearrange("p (n e) -> p n e", n=NT)
                c0, c1, c2 = r_s[:, 0:16], r_s[:, 16:32], r_s[:, 32:48]
                dve.wait_ge(s_side_done, order[(layer, ("gate",))] + 1)
                if layer == "L0f":
                    dve.wait_ge(s_load["vec"], 32)
                    link(tt(g, g, wide_of("L0f_gb").unsqueeze(1).broadcast_to([P, NT, E]), ALU.add))
                    link(v.tensor_reduce(c0, g, AX.X, ALU.max))
                    largest_first(g, NT, E, rk)
                    link(tt(g, g, over_e(c0, E), ALU.subtract))
                    ts(rk, rk, 1.5, None, ALU.is_lt).then_inc(s_routing_in, 1)
                    dve.wait_ge(s_routing_exp, rout_no[layer])
                    dve.wait_ge(s_routing_in, 1)
                    link(tt(wx, wx, rk, ALU.mult))
                    link(v.tensor_reduce(c1, wx, AX.X, ALU.add))
                    link(v.reciprocal(c2, c1))
                    link(tt(wx, wx, over_e(c2, E), ALU.mult))
                elif layer == "L1f":
                    link(v.tensor_reduce(c0, g, AX.X, ALU.max))
                    tt(g, g, over_e(c0, E), ALU.subtract).then_inc(s_routing_in, 1)
                    dve.wait_ge(s_routing_exp, rout_no[layer])
                    link(v.tensor_reduce(c1, wx, AX.X, ALU.add))
                    link(v.reciprocal(c2, c1))
                    link(tt(wx, wx, over_e(c2, E), ALU.mult))
                    link(stt(wx, wx, FLT_MIN, wx, ALU.is_ge, ALU.mult))
                    largest_first(wx, NT, E, rk)
                    link(ts(g, rk, 1.5, None, ALU.is_lt))
                    tt(wx, wx, g, ALU.mult).then_inc(s_routing_in, 1)
                    dve.wait_ge(s_routing_in, rout_no[layer] + 1)
                elif layer == "L2f":
                    dve.wait_ge(s_routing_exp, rout_no[layer])
                    s_ = rb
                    link(tt(s_, wx, wide_of("L2f_bias").unsqueeze(1).broadcast_to([P, NT, E]), ALU.add))
                    big, small = r_s[:, 0:128], r_s[:, 128:256]
                    pair = r_b[:, 0:256].rearrange("p (q i) -> p q i", i=2)
                    tt(big, pair[:, :, 0], pair[:, :, 1], ALU.max)
                    link(tt(small, pair[:, :, 0], pair[:, :, 1], ALU.add))
                    b2, s2 = (z.rearrange("p (g i) -> p g i", i=2) for z in (big, small))
                    gs = r_a[:, 0:64]
                    tt(r_a[:, 64:128], b2[:, :, 0], b2[:, :, 1], ALU.add)
                    link(tt(gs, s2[:, :, 0], s2[:, :, 1], ALU.max))
                    link(tt(gs, gs, r_a[:, 64:128], ALU.max))
                    gr = r_a[:, 128:192].rearrange("p (n e) -> p n e", n=NT)
                    largest_first(gs.rearrange("p (n e) -> p n e", n=NT), NT, 4, gr)
                    gm = r_a[:, 192:256]
                    link(ts(gm, r_a[:, 128:192], 1.5, None, ALU.is_lt))
                    msk = r_s[:, 0:256].bitcast(mybir.dt.int32)
                    link(v.tensor_copy(msk.rearrange("p (g e) -> p g e", e=4), gm.unsqueeze(2).broadcast_to([P, 64, 4])))
                    link(v.memset(rank, -1.0))
                    link(v.copy_predicated(rank, msk, r_b))
                    link(v.tensor_copy(r_b, rank))
                    for i in range(4):
                        pick_four(0, i)
                elif layer == "L3f":
                    link(v.memset(sk_col, 0.0))
                    link(ts(la, g, -1.0 / float(np.float32(SINK_EPS)), None, ALU.mult))
                    by_col = lambda z: z.rearrange("p n e -> p e n")
                    for it in range(SINK_ITERS):
                        link(v.tensor_reduce(sk_m[:, 0:16], la, AX.X, ALU.max))
                        tt(sk_d, la, over_e(sk_m[:, 0:16], E), ALU.subtract).then_inc(s_sk_in, 1)
                        dve.wait_ge(s_sk_act, 4 * it + 1)
                        v.tensor_reduce(sk_s[:, 0:16], sk_e, AX.X, ALU.add).then_inc(s_sk_in, 1)
                        dve.wait_ge(s_sk_act, 4 * it + 2)
                        link(tt(la, sk_d, over_e(sk_l[:, 0:16], E), ALU.subtract))
                        v.tensor_reduce(sk_col[:, 0:8], by_col(la), AX.X, ALU.max).then_inc(s_sk_v, 1)
                        dve.wait_ge(s_sk_pe, 2 * it + 1)
                        link(v.tensor_reduce(sk_m[:, 16:17], psO[0][:, 0:128], AX.X, ALU.max))
                        ts(sk_diag, ident[:, 0:8], sk_m[:, 16:17], None, ALU.mult).then_inc(s_sk_v, 1)
                        dve.wait_ge(s_sk_pe, 2 * it + 2)
                        tt(sk_d, la, psO[0][:, 0:8].unsqueeze(1).broadcast_to([P, NT, E]), ALU.subtract).then_inc(s_sk_in, 1)
                        dve.wait_ge(s_sk_act, 4 * it + 3)
                        v.tensor_reduce(sk_s[:, 16:24], by_col(sk_e), AX.X, ALU.add).then_inc(s_sk_v, 1)
                        dve.wait_ge(s_sk_act, 4 * it + 4)
                        ins = tt(la, sk_d, sk_l[:, 0:8].unsqueeze(1).broadcast_to([P, NT, E]), ALU.subtract)
                        if it < SINK_ITERS - 1:
                            link(ins)
                        else:
                            ins.then_inc(s_sk_in, 1)
                    dve.wait_ge(s_sk_act, 4 * SINK_ITERS + 1)
                    link(stt(sk_e, sk_e, FLT_MIN, sk_e, ALU.is_ge, ALU.mult))
                    largest_first(sk_e, NT, E, rk)
                    ts(ra, rk, 0.0, None, ALU.is_equal)
                    link(ts(rb, rk, 1.0, None, ALU.is_equal))
                    tt(ra, ra, sk_e[:, :, 0:1].broadcast_to([P, NT, E]), ALU.mult)
                    link(tt(rb, rb, sk_e[:, :, 1:2].broadcast_to([P, NT, E]), ALU.mult))
                    link(tt(wx, ra, rb, ALU.add))

            def find_nan():
                all_done(dve, "L2x")
                dve.wait_ge(s_scaled, scaled_no["L2x"])
                dve.wait_ge(s_load["ctx"], 16)
                link(v.memset(nanf[:, :], 0.0))
                v.tensor_reduce(nanf[:, 0:1], xT("L2x"), AX.X, ALU.add)
                v.tensor_reduce(nanf[0:CD, 1:2], ctxT[:, :], AX.X, ALU.add)
                v.tensor_reduce(nanf[:, 2:3], w("L2x", "wq"), AX.X, ALU.add)
                v.tensor_reduce(nanf[0:CD, 3:4], w("L2x", "wk"), AX.X, ALU.add)
                at = COLS["L2x_bq"]
                link(v.tensor_reduce(nanf[:, 6:7], cols[:, at:at + 2], AX.X, ALU.add))
                link(tt(nanf[:, 3:4], nanf[:, 3:4], nanf[:, 6:7], ALU.add))
                v.tensor_reduce(nanf[:, 4:5], nanf[:, 0:4], AX.X, ALU.add).then_inc(s_nansum, 1)
                dve.wait_ge(s_side_done, order[("L2x", ("nan",))] + 1)
                link(tt(nanmask[:, :], nanf[:, 5:6], nanf[:, 5:6], ALU.not_equal))

            def spread_relative():
                dve.wait_ge(s_side_done, order[("L0a", ("rel", 1))] + 1)
                for t in range(T):
                    for half in range(2):
                        r = 2 * t + half
                        if r >= 2:
                            dve.wait_ge(s_side_full, order[("L0a", ("relout", t - 1, half))] + 1)
                        for kt in range(2):
                            first = relT[:, kt, 0:1]
                            src = bass.AP(tensor=first.tensor, offset=first.offset + 255 - 8 * t - 128 * half,
                                          ap=[list(first.ap[0]), [-16, 8], [-1, 8], [16, 16]])
                            ins = v.tensor_copy(rel_bias(r, kt).rearrange("p (h m n) -> p h m n", h=8, m=8), src)
                        ins.then_inc(s_relbias, 1)

            def attention(layer):
                a = ATT[layer]
                dh, U, K, g0, size = a["dh"], a["H"], a["keys"], unit0[layer], a["group"]
                NU = B * U
                if layer == "L0a":
                    spread_relative()
                if layer == "L2x":
                    find_nan()

                def maxima(u):
                    g = g0 + u
                    bank = psS[g % 2][:, 0:2 * K]
                    dve.wait_ge(s_qk, g + 1)
                    if layer == "L2x" and g >= 2:
                        dve.wait_ge(s_exp, g - 1)
                    if layer == "L2x":
                        link(ts(clamped[:, g % 2, :], bank, CLAMP, -CLAMP, ALU.min, ALU.max))
                        bank = clamped[:, g % 2, :]
                    v.tensor_reduce(negmax[:, g % 2, :], bank.rearrange("p (h k) -> p h k", h=2), AX.X, ALU.max,
                                    negate=True).then_inc(s_max, 1)

                def turned_rest(u):
                    g = g0 + u
                    dve.wait_ge(s_pthi, g + 1)
                    tt(turned(g, 1), psT[g % 2][:, :], turned(g, 0), ALU.subtract).then_inc(s_ptc, 1)

                def split_small(b):
                    raw = v_raw(layer, b).rearrange("p (x d) -> p x d", d=8)
                    vp = v_small(layer, b)
                    dve.wait_ge(s_side_done, order[(layer, ("v", b))] + 1)
                    if layer != "L2a":
                        last = ("relout", T - 1, 1) if layer == "L0a" else ("vmean", b)
                        dve.wait_ge(s_side_full, order[(layer, last)] + 1)
                    if b >= 2:
                        dve.wait_ge(s_pv, g0 + U * (b - 1))
                    link(v.tensor_copy(vp[:, :, 0, :], raw))
                    link(tt(raw, raw, vp[:, :, 0, :], ALU.subtract))
                    link(v.tensor_copy(vp[:, :, 1, :], raw))
                    tt(vp[:, :, 2, :], raw, vp[:, :, 1, :], ALU.subtract).then_inc(s_vsplit, 1)

                def normalize(gi):
                    gg = group0[layer] + gi
                    b, u0 = gi * size // U, gi * size % U
                    dve.wait_ge(s_pv, g0 + size * (gi + 1))
                    nh = 2 * size
                    link(v.reciprocal(rrec[:, 0:nh], rsum[:, b % 2, 2 * u0:2 * u0 + nh]))
                    if dh == 64:
                        if gi >= 2:
                            dve.wait_ge(s_side_full, order[(layer, ("ot", (gi - 2) * size // U, (gi - 2) % (U // size)))] + 1)
                        tt(o_sb[:, gi % 2, :].rearrange("p (s d) -> p s d", d=64),
                           psO[gg % 2][:, :].rearrange("p (s d) -> p s d", d=64),
                           rrec[:, 0:nh].unsqueeze(2).broadcast_to([P, nh, 64]), ALU.mult).then_inc(s_norm, 1)
                    else:
                        if b >= 2 and layer != "L0a":
                            dve.wait_ge(s_side_full, order[(layer, ("ot", b - 2, 0))] + 1)
                        half = u0 // size
                        dst = [o_sb[:, b % 2, P * t + 8 * size * half:P * t + 8 * size * (half + 1)] for t in range(T)]
                        for t in range(T):
                            at = 24 * size * t
                            ins = v.tensor_reduce(dst[t].rearrange("p (x d) -> p x d", d=8),
                                                  psO[gg % 2][:, at:at + 24 * size].rearrange("p (x c d) -> p x d c", c=3, d=8),
                                                  AX.X, ALU.add)
                        link(ins)
                        for t in range(T):
                            rec = rrec[:, 0:nh].rearrange("p (u t h) -> p t u h", t=T, h=2)[:, t]
                            z = dst[t].rearrange("p (u h d) -> p u h d", h=2, d=8)
                            ins = tt(z, z, rec.unsqueeze(3).broadcast_to([P, size // 2, 2, 8]), ALU.mult)
                        if layer == "L2x" and half == U // size - 1:
                            link(ins)
                            dve.wait_ge(s_norm, gg)
                            dve.wait_ge(s_side_done, order[(layer, ("vmean", b))] + 1)
                            for t in range(T):
                                ins = v.copy_predicated(o_sb[:, b % 2, P * t:P * t + P], nanmask[:, :].broadcast_to([P, P]),
                                                        v_sb[:, 1024 + 128 * (b % 2):1152 + 128 * (b % 2)])
                        ins.then_inc(s_norm, 1)

                def add_relative(b):
                    dve.wait_ge(s_norm, group0[layer] + U // size * (b + 1))
                    if b == 0:
                        dve.wait_ge(s_side_done, order[(layer, ("relout", 1, 1))] + 1)
                        dve.wait_ge(s_load["vec"], 32)
                    for t in range(T):
                        o = o_sb[:, b % 2, P * t:P * t + P].rearrange("p (h d) -> p h d", d=8)
                        ins = tt(o, o, rel_out[:, t, :, b, :], ALU.add)
                    link(ins)
                    moments(o_sb[:, b % 2, 0:256].rearrange("p (t d) -> p t d", t=T), 1e-3)

                def inner_norm(b):
                    link(center(o_res, o_sb[:, b % 2, 0:256].rearrange("p (t d) -> p t d", t=T)))
                    link(tt(o_res[:, :, :], o_res[:, :, :], wide_of("gamma").unsqueeze(1).broadcast_to([P, T, D]), ALU.mult))
                    link(tt(o_res[:, :, :], o_res[:, :, :], wide_of("beta").unsqueeze(1).broadcast_to([P, T, D]), ALU.add))

                def split_biases(i):
                    dve.wait_ge(s_load["bias"], 48)
                    if i:
                        dve.wait_ge(s_bias_split, i)
                    z = (0, 64, 64, 96, 96)[i]
                    rest, part = bias_raw[z:P, :], bias_parts[z:P, :]
                    if i % 2 == 0:
                        v.tensor_copy(part, rest).then_inc(s_bias_split, 1)
                    else:
                        tt(rest, rest, part, ALU.subtract).then_inc(s_bias_split, 1)

                for s in range(-2, NU + 14):
                    if layer == "L0x" and 3 <= s < 18 and s % 3 == 0:
                        split_biases(s // 3 - 1)
                    if s + 2 < NU:
                        maxima(s + 2)
                    if 0 <= s - 1 < NU:
                        turned_rest(s - 1)
                    if s > size and (s - 2) % size == 0 and (s - 2) // size - 1 < NU // size:
                        normalize((s - 2) // size - 1)
                    if dh == 8 and (s == -1 or s % U == 6 and s // U + 1 < B):
                        split_small(0 if s == -1 else s // U + 1)
                    for b in range(B):
                        if layer == "L0a" and s == (b + 1) * U + 3:
                            add_relative(b)
                        if layer == "L0a" and s == (b + 1) * U + 7:
                            inner_norm(b)
                        if s == (b + 1) * U + 8:
                            tail_sum(layer, b)
                            tail_moments(layer, b)
                        if s == (b + 1) * U + 10 and layer != last_block:
                            tail_center(layer, b)

            def experts(layer):
                f = FFN[layer]
                E, glu = len(f["chunks"]), f["glu"]
                NE = B * E
                hop = hop0[layer]
                ahead = f["ahead"]

                def gated(n):
                    nonlocal hop
                    g = exp0[layer] + n
                    if g >= 2:
                        dve.wait_ge(s_down, g - 1)
                    for c in range(f["chunks"][n % E]):
                        dve.wait_ge(s_sg, hop + 1 - glu_hop0)
                        tt(hT[:, g % 2, c, :], sg[:, hop % 2, :], psH[hop % 4][:, 256:512], ALU.mult).then_inc(s_hop, 1)
                        hop += 1

                for n in range(-ahead, NE + 4):
                    if n + ahead < NE and glu and ahead == 1:
                        gated(n + ahead)
                    m = n - 1
                    if 0 <= m < NE:
                        b, e, g = m // E, m % E, exp0[layer] + m
                        dve.wait_ge(s_down, g + 1)
                        if g:
                            dve.wait_ge(s_acc, g)
                        for t in range(T):
                            o, xt = psO[g % 2][:, P * t:P * t + P], x[:, T * b + t, :]
                            if layer == "L2f" and e == E - 1:
                                ins = tt(xt, o, xt, ALU.add)
                            else:
                                ins = stt(xt, o, wexp[:, T * b + t, e:e + 1], xt, ALU.mult, ALU.add)
                        ins.then_inc(s_acc, 1)
                    if n + ahead < NE and glu and ahead == 2:
                        gated(n + ahead)
                    if layer == "L2f" and 0 <= m < NE and e in (2, 5, 8, 11) and b + 1 < B:
                        pick_four(b + 1, e // 3)
                    if 0 <= m < NE and m % E == E - 1 and layer != "L3f":
                        dve.wait_ge(s_acc, g + 1)
                        tail_moments(layer, b)
                    m = n - 2
                    if 0 <= m < NE and m % E == E - 1 and layer != last_block:
                        tail_center(layer, m // E)

            dve.wait_ge(s_load["x"], 16)
            for b in range(B):
                tail_moments("init", b)
                tail_center("init", b)
            dve.wait_ge(s_const, 11)
            for layer in LAYERS:
                if layer in ATT:
                    attention(layer)
                elif layer in FFN:
                    routing(layer)
                    glu_hop0 = glu_first.get(layer, 0)
                    experts(layer)
                elif layer == "L1a":
                    for b in range(B):
                        dve.wait_ge(s_ga, b + 1)
                        if b == 0:
                            tt(c_state, gates[:, 0, :], gates[:, 3, :], ALU.mult).then_inc(s_c, 1)
                        else:
                            tt(c_in, gates[:, 0, :], gates[:, 3, :], ALU.mult)
                            link(tt(c_state, gates[:, 1, :], c_state, ALU.mult))
                            tt(c_state, c_state, c_in, ALU.add).then_inc(s_c, 1)
                        dve.wait_ge(s_tc, b + 1)
                        if b >= 2:
                            dve.wait_ge(s_side_full, order[(layer, ("hout", b - 2))] + 1)
                        tt(h_state(b), gates[:, 2, :], tanh_c, ALU.mult).then_inc(s_h, 1)
                        tail_sum(layer, b)
                        tail_moments(layer, b)
                        if layer != last_block:
                            tail_center(layer, b)
                elif layer == "L1f":
                    routing(layer)

                    def scale_x(n):
                        b = n // 8
                        dve.wait_ge(s_bc, n + 1)
                        if n >= 2:
                            dve.wait_ge(s_a1, n - 1)
                        tt(prob[:, n % 2, 0:256], xT(layer)[:, S * b:S * b + S], psS[n % 2][:, 0:256],
                           ALU.mult).then_inc(s_xs, 1)

                    def join(n):
                        b, e = n // 8, n % 8
                        dve.wait_ge(s_x23, n + 1)
                        if n >= 2:
                            dve.wait_ge(s_pacc, n - 1)
                        b3 = wide_of("L1f_b3")[:, P * e:P * e + P]
                        for t in range(T):
                            ins = stt(prob[:, n % 2, 256 + P * t:256 + P * t + P], psO[n % 2][:, P * t:P * t + P],
                                      wexp[:, T * b + t, e:e + 1], b3, ALU.mult, ALU.add)
                        link(ins)
                        for t in range(T):
                            ins = stt(o_sb[:, n % 2, P * t:P * t + P], psO[n % 2][:, 256 + P * t:256 + P * t + P],
                                      lg[:, T * b + t, e:e + 1], prob[:, n % 2, 256 + P * t:256 + P * t + P],
                                      ALU.mult, ALU.mult)
                        ins.then_inc(s_t23, 1)

                    scale_x(0)
                    scale_x(1)
                    for b in range(B):
                        for e in range(8):
                            n = 8 * b + e
                            if e < 6:
                                scale_x(n + 2)
                            join(n)
                        for c in range(2):
                            dve.wait_ge(s_shs, 2 * b + c + 1)
                            tt(hT[:, c, 3, :], sg[:, c, :], psS[c][:, 256:512], ALU.mult).then_inc(s_shh, 1)
                        if b + 1 < B:
                            scale_x(8 * b + 8)
                            scale_x(8 * b + 9)
                        dve.wait_ge(s_shd, b + 1)
                        dve.wait_ge(s_pacc, 8 * b + 8)
                        tt(tiles(b), psO[0][:, 0:256].rearrange("p (t d) -> p t d", t=T), tiles(b), ALU.add).then_inc(s_sho, 1)
                        dve.wait_ge(s_sho, b + 1)
                        tail_moments(layer, b)
                        if layer != last_block:
                            tail_center(layer, b)
                elif layer == "L3a":
                    link(v.memset(va3s[:, :, :, 128:130], 1.0))
                    groups = lambda z: z.rearrange("p (g e) -> p g e", e=8)

                    def softmax_groups(b):
                        qk3 = qk3s[:, b % 2]
                        for t in range(T):
                            n = T * b + t
                            dve.wait_ge(s_qkv, n + 1)
                            if b >= 2:
                                dve.wait_ge(s_ctx3, b - 1)
                                dve.wait_ge(s_side_full, order[(layer, ("qT", b - 2))] + 1)
                            link(v.tensor_reduce(rrec[:, :], groups(psS[t][:, 0:256]), AX.X, ALU.max))
                            tt(groups(qk3[:, t, :]), groups(psS[t][:, 0:256]),
                               rrec[:, :].unsqueeze(2).broadcast_to([P, 32, 8]), ALU.subtract).then_inc(s_sub, 1)
                            dve.wait_ge(s_ex3, n + 1)
                            link(v.tensor_reduce(rrec[:, :], groups(qk3[:, t, :]), AX.X, ALU.add))
                            link(v.reciprocal(rsum[:, 0, :], rrec[:, :]))
                            tt(groups(qk3[:, t, :]), groups(qk3[:, t, :]),
                               rsum[:, 0, :].unsqueeze(2).broadcast_to([P, 32, 8]), ALU.mult).then_inc(s_sm3, 1)

                    def outputs(b):
                        dve.wait_ge(s_ctx3, b + 1)
                        ctx_ps = psT[0]
                        tt(groups(cm3[:, 0:128]), groups(ctx_ps[:, 0:128]), hmask[:, :].unsqueeze(2).broadcast_to([P, 16, 8]),
                           ALU.mult)
                        ts(cm3[:, 128:144], hmask[:, :], ctx_ps[:, 128:129], None, ALU.mult).then_inc(s_cm3, 1)
                        dve.wait_ge(s_num3, b + 1)
                        for t in range(T):
                            o = psT[1][:, 144 * t:144 * t + 144]
                            link(v.reciprocal(rrec[:, 0:16], o[:, 128:144]))
                            link(tt(groups(ol3[:, t, :]), groups(o[:, 0:128]),
                                    rrec[:, 0:16].unsqueeze(2).broadcast_to([P, 16, 8]), ALU.mult))
                            ins = tt(ol3[:, t, :], ol3[:, t, :], qk3s[:, b % 2, t, 0:128], ALU.add)
                        ins.then_inc(s_ol3, 1)

                    for b in range(-1, B + 1):
                        if b + 1 < B:
                            softmax_groups(b + 1)
                        if 0 <= b < B:
                            outputs(b)
                        if b >= 1:
                            tail_sum(layer, b - 1)
                            tail_moments(layer, b - 1)
                            if layer != last_block:
                                tail_center(layer, b - 1)


def kernel(**a):
    import concourse.bacc as bacc
    from concourse.bass_utils import run_bass_kernel_spmd

    a = {k: np.asarray(z) for k, z in a.items()}
    f = {"x": a["x"].reshape(TOK, D), "ctxT": a["ctx_768"].reshape(TOK, CD).T, "rel": a["L0_attn_rel_table"]}

    def chunked(m):
        return m.reshape(-1, P, m.shape[-1]).transpose(1, 0, 2).reshape(P, -1)

    def by_expert(m):
        return m.transpose(1, 0, 2).reshape(m.shape[1], -1)

    for n in ("q", "k", "v"):
        f["L0a_w" + n] = a["L0_attn_W" + n]
        f["L2a_w" + n] = a["L2_attn_W" + n].T
        f["L0x_w" + n] = a["L0_xattn_W" + n]
        f["L1x_w" + n] = a["L1_xattn_W" + n]
        f["L2x_w" + n] = a["L2_xattn_W" + n]
        f["L3x_w" + n] = a["L3_xattn_w_" + n]
    f["L0x_wo"] = chunked(a["L0_xattn_Wo"])
    f["L1x_wo"] = chunked(a["L1_xattn_Wout"])
    f["L3x_wo"] = chunked(a["L3_xattn_w_o"])
    f["L2a_wo"] = a["L2_attn_Wo"].T
    f["L2x_wo"] = a["L2_xattn_Wo"]
    f["L1a_w"], f["L1a_u"] = a["L1_attn_w"], a["L1_attn_u"]
    f["L0f_up"] = by_expert(a["L0_ffn_w1"])
    f["L0f_down"] = chunked(a["L0_ffn_w2"].reshape(-1, D))
    for n in ("1", "2", "3"):
        f["L1f_w" + n] = by_expert(a["L1_ffn_w" + n].transpose(0, 2, 1))
    f["L1f_sg"], f["L1f_su"] = a["L1_ffn_sw1"].T, a["L1_ffn_sw2"].T
    f["L1f_sd"] = chunked(a["L1_ffn_sw3"].T)
    for n in ("gate", "up"):
        f["L2f_" + n] = np.concatenate([by_expert(a[f"L2_ffn_{n}_w"]), a[f"L2_ffn_sh_{n}_w"]], 1)
        f["L3f_" + n] = by_expert(a["L3_ffn_W_" + n].transpose(0, 2, 1))
    f["L2f_down"] = np.concatenate([by_expert(a["L2_ffn_down_w"]), chunked(a["L2_ffn_sh_down_w"])], 1)
    f["L3f_down"] = chunked(a["L3_ffn_W_down"].transpose(0, 2, 1).reshape(-1, D))
    f["L3a_wqkv"] = np.concatenate([a["L3_attn_W" + n].T for n in "qkv"], 1)
    f["L3a_wp"] = a["L3_attn_Wp"].T
    f["gw"] = np.concatenate([a["L0_ffn_gate_w"].T, a["L1_ffn_gate_w"].T, a["L2_ffn_router_w"].T, a["L3_ffn_gate_W"].T], 1)
    f["rows"] = np.concatenate([a["L0_xattn_bo"], a["L1_xattn_bout"], a["L2_attn_bo"], a["L2_xattn_bv"], a["L2_xattn_bo"],
                                a["L3_attn_bq"], a["L3_attn_bk"], a["L3_attn_bv"], a["L3_attn_bp"], a["L3_xattn_b_o"],
                                a["L0_ffn_b2"].reshape(-1), a["L1_ffn_b2"].reshape(-1)])[None]
    f["wide"] = np.concatenate([a["L0_attn_gamma"], a["L0_attn_beta"], a["L0_ffn_gate_b"], a["L2_ffn_bias"],
                                a["L1_ffn_b3"].reshape(-1)])[None]
    f["cols"] = np.concatenate([a["L0_ffn_b1"].reshape(-1, P).T, a["L1_attn_bias"].reshape(4, P).T, a["L1_ffn_b1"].T,
                                a["L2_xattn_bq"][:, None], a["L2_xattn_bk"][:, None]], 1)

    nc = bacc.Bacc("TRN2", target_bir_lowering=False, num_devices=1)
    arrays, d = {}, {}
    for name, z in f.items():
        z = np.ascontiguousarray(z)
        arrays["in_" + name] = z
        d[name] = nc.dram_tensor("in_" + name, z.shape, mybir.dt.from_np(z.dtype), kind="ExternalInput").ap()
    d["rel_ext"] = nc.dram_tensor("rel_ext", (528, 16), F32, kind="Internal").ap()
    out = nc.dram_tensor("out", (TOK, D), F32, kind="ExternalOutput").ap()
    build(nc, d, out)
    r = run_bass_kernel_spmd(nc, [arrays], core_ids=[0])
    return r.results[0]["out"].reshape(B, S, D)
```
